# Optimizing a Trainium2 kernel written in Bass

```python
import numpy as np
import jax
import jax.numpy as jnp

def _softmax(x, axis=-1):
    return jax.nn.softmax(x, axis=axis)

def _gelu(x):
    return jax.nn.gelu(x, approximate=True)

def _silu(x):
    return jax.nn.silu(x)

def _sigmoid(x):
    return jax.nn.sigmoid(x)

def _layernorm(x, axis=-1, eps=1e-05):
    m = jnp.mean(x, axis=axis, keepdims=True)
    v = jnp.var(x, axis=axis, keepdims=True)
    return (x - m) / jnp.sqrt(v + eps)

def _scatter_add(tgt, idx, src, axis=0):
    return tgt.at[idx].add(src)

def _segment_sum(src, seg, n):
    return jax.ops.segment_sum(src, seg, n)
kernel_name = 'mk_metaformer_d1_conv_nchw256_r2_ce81ca'

def setup_inputs(seed: int=0):
    np.random.seed(seed)
    _w = jnp.asarray

    def _rec_inputs():
        import jax
        import jax.numpy as jnp
        _gk = jax.random.key(seed)
        x = -0.0002928 + 1 * jax.random.normal(jax.random.fold_in(_gk, 1), (4, 128, 32, 32), jnp.float32)
        return x
    x = _rec_inputs()

    def _L0_conv_setup():
        import jax, jax.numpy as jnp
        import numpy as np
        from jax import lax
        B, CIN, COUT, H, W = (4, 128, 128, 32, 32)
        K = 3
        PAD = 1
        STRIDE = 1

        def _dcnv2(x, offset_w, offset_b, dcn_w):
            b, c, h, w = x.shape
            kk = K * K
            o = lax.conv_general_dilated(x, offset_w, (STRIDE, STRIDE), ((PAD, PAD), (PAD, PAD)), dimension_numbers=('NCHW', 'OIHW', 'NCHW'))
            o = o + offset_b[None, :, None, None]
            ho, wo = (o.shape[2], o.shape[3])
            off = o[:, :2 * kk].reshape(b, kk, 2, ho, wo)
            dy, dx = (off[:, :, 0], off[:, :, 1])
            mask = jax.nn.sigmoid(o[:, 2 * kk:])
            ki, kj = jnp.meshgrid(jnp.arange(K), jnp.arange(K), indexing='ij')
            ki = ki.reshape(kk).astype(jnp.float32)
            kj = kj.reshape(kk).astype(jnp.float32)
            base_y = (jnp.arange(ho, dtype=jnp.float32) * STRIDE - PAD)[None, None, :, None] + ki[None, :, None, None]
            base_x = (jnp.arange(wo, dtype=jnp.float32) * STRIDE - PAD)[None, None, None, :] + kj[None, :, None, None]
            py = base_y + dy
            px = base_x + dx
            y0 = jnp.floor(py)
            x0 = jnp.floor(px)
            wy = py - y0
            wx = px - x0
            y0i = y0.astype(jnp.int32)
            x0i = x0.astype(jnp.int32)
            xT = x.transpose(0, 2, 3, 1)
            bidx = jnp.arange(b)[:, None, None, None]

            def gather(yi, xi):
                valid = (yi >= 0) & (yi < h) & (xi >= 0) & (xi < w)
                yc = jnp.clip(yi, 0, h - 1)
                xc = jnp.clip(xi, 0, w - 1)
                v = xT[bidx, yc, xc]
                return v * valid[..., None].astype(x.dtype)
            g00 = gather(y0i, x0i)
            g01 = gather(y0i, x0i + 1)
            g10 = gather(y0i + 1, x0i)
            g11 = gather(y0i + 1, x0i + 1)
            wy_ = wy[..., None]
            wx_ = wx[..., None]
            sampled = g00 * (1 - wy_) * (1 - wx_) + g01 * (1 - wy_) * wx_ + g10 * wy_ * (1 - wx_) + g11 * wy_ * wx_
            sampled = sampled * mask[..., None]
            wk = dcn_w.reshape(dcn_w.shape[0], c, kk)
            return jnp.einsum('bkhwc,ock->bohw', sampled, wk)
        key = jax.random.key(seed)
        k1, k2, k3, k4 = jax.random.split(key, 4)
        x = jax.random.normal(k1, (B, CIN, H, W), dtype=jnp.float32)
        offset_w = jax.random.normal(k2, (3 * K * K, CIN, K, K), dtype=jnp.float32) * 0.01
        offset_b = jax.random.normal(k3, (3 * K * K,), dtype=jnp.float32) * 0.01
        dcn_w = jax.random.normal(k4, (COUT, CIN, K, K), dtype=jnp.float32) * (1.0 / np.sqrt(CIN * K * K))
        return {'x': x, 'offset_w': offset_w, 'offset_b': offset_b, 'dcn_w': dcn_w}
    _L0_conv_all = _L0_conv_setup()
    _L0_conv_in = {k: v for k, v in _L0_conv_all.items() if k in ('offset_w', 'offset_b', 'dcn_w')}
    del _L0_conv_all

    def _L0_ffn_setup():
        import jax, jax.numpy as jnp
        import numpy as np
        B, N, D = (16, 2048, 128)
        NUM_EXPERTS, TOP_K, HEADS = (4, 2, 4)
        N_EDGES = 524288
        LN_EPS = 1e-05

        def _layernorm(x, g, b):
            mu = x.mean(-1, keepdims=True)
            var = ((x - mu) ** 2).mean(-1, keepdims=True)
            return (x - mu) * jax.lax.rsqrt(var + LN_EPS) * g + b

        def _forward(x, edge_index, W_gat, att_src, att_dst, b_gat, ln_gamma, ln_beta, W1, b1, W2, b2):
            Bc, Nc, Dc = x.shape
            M = Bc * Nc
            x_flat = x.reshape(M, Dc)
            h = (x_flat @ W_gat).reshape(M, HEADS, NUM_EXPERTS)
            loops = jnp.arange(M, dtype=edge_index.dtype)
            src = jnp.concatenate([edge_index[0], loops])
            dst = jnp.concatenate([edge_index[1], loops])
            a_src = (h * att_src).sum(-1)
            a_dst = (h * att_dst).sum(-1)
            e = jax.nn.leaky_relu(a_src[src] + a_dst[dst], negative_slope=0.2)
            e_max = jax.ops.segment_max(e, dst, num_segments=M)
            ee = jnp.exp(e - e_max[dst])
            denom = jax.ops.segment_sum(ee, dst, num_segments=M)
            alpha = ee / (denom[dst] + 1e-16)
            msg = h[src] * alpha[:, :, None]
            agg = jax.ops.segment_sum(msg, dst, num_segments=M).reshape(M, HEADS * NUM_EXPERTS) + b_gat
            scores = _layernorm(agg, ln_gamma, ln_beta).reshape(M, HEADS, NUM_EXPERTS).mean(1)
            scores = scores.reshape(Bc, Nc, NUM_EXPERTS)
            topk_s, topk_i = jax.lax.top_k(scores, TOP_K)
            w = jax.nn.softmax(topk_s, axis=-1)
            out = jnp.zeros_like(x)
            for ei in range(NUM_EXPERTS):
                g = jnp.where(topk_i == ei, w, 0.0).sum(-1)
                hh = jax.nn.gelu(x @ W1[ei] + b1[ei], approximate=False)
                out = out + g[..., None] * (hh @ W2[ei] + b2[ei])
            return out
        key = jax.random.key(seed)
        ks = jax.random.split(key, 8)
        s = 0.05
        return {'x': jax.random.normal(ks[0], (B, N, D), jnp.float32), 'W_gat': jax.random.normal(ks[1], (D, HEADS * NUM_EXPERTS), jnp.float32) * s, 'att_src': jax.random.normal(ks[2], (HEADS, NUM_EXPERTS), jnp.float32) * s, 'att_dst': jax.random.normal(ks[3], (HEADS, NUM_EXPERTS), jnp.float32) * s, 'b_gat': jnp.zeros((HEADS * NUM_EXPERTS,), jnp.float32), 'ln_gamma': jnp.ones((HEADS * NUM_EXPERTS,), jnp.float32), 'ln_beta': jnp.zeros((HEADS * NUM_EXPERTS,), jnp.float32), 'W1': jax.random.normal(ks[4], (NUM_EXPERTS, D, 2 * D), jnp.float32) * s, 'b1': jnp.zeros((NUM_EXPERTS, 2 * D), jnp.float32), 'W2': jax.random.normal(ks[5], (NUM_EXPERTS, 2 * D, D), jnp.float32) * s, 'b2': jnp.zeros((NUM_EXPERTS, D), jnp.float32), 'edge_index': jax.random.randint(ks[6], (2, N_EDGES), 0, B * N, jnp.int32)}
    _L0_ffn_all = _L0_ffn_setup()
    _L0_ffn_in = {k: v for k, v in _L0_ffn_all.items() if k in ('W_gat', 'att_src', 'att_dst', 'b_gat', 'ln_gamma', 'ln_beta', 'W1', 'b1', 'W2', 'b2', 'edge_index')}
    del _L0_ffn_all
    return {'x': x, 'L0_conv_offset_w': _L0_conv_in['offset_w'], 'L0_conv_offset_b': _L0_conv_in['offset_b'], 'L0_conv_dcn_w': _L0_conv_in['dcn_w'], 'L0_ffn_W_gat': _L0_ffn_in['W_gat'], 'L0_ffn_att_src': _L0_ffn_in['att_src'], 'L0_ffn_att_dst': _L0_ffn_in['att_dst'], 'L0_ffn_b_gat': _L0_ffn_in['b_gat'], 'L0_ffn_ln_gamma': _L0_ffn_in['ln_gamma'], 'L0_ffn_ln_beta': _L0_ffn_in['ln_beta'], 'L0_ffn_W1': _L0_ffn_in['W1'], 'L0_ffn_b1': _L0_ffn_in['b1'], 'L0_ffn_W2': _L0_ffn_in['W2'], 'L0_ffn_b2': _L0_ffn_in['b2'], 'L0_ffn_edge_index': _L0_ffn_in['edge_index']}

def reference(x, L0_conv_offset_w, L0_conv_offset_b, L0_conv_dcn_w, L0_ffn_W_gat, L0_ffn_att_src, L0_ffn_att_dst, L0_ffn_b_gat, L0_ffn_ln_gamma, L0_ffn_ln_beta, L0_ffn_W1, L0_ffn_b1, L0_ffn_W2, L0_ffn_b2, L0_ffn_edge_index):
    import jax
    import jax.numpy as jnp

    def _L0_conv_ref(x, offset_w, offset_b, dcn_w):
        import jax, jax.numpy as jnp
        import numpy as np
        from jax import lax
        B, CIN, COUT, H, W = (4, 128, 128, 32, 32)
        K = 3
        PAD = 1
        STRIDE = 1

        def _dcnv2(x, offset_w, offset_b, dcn_w):
            b, c, h, w = x.shape
            kk = K * K
            o = lax.conv_general_dilated(x, offset_w, (STRIDE, STRIDE), ((PAD, PAD), (PAD, PAD)), dimension_numbers=('NCHW', 'OIHW', 'NCHW'))
            o = o + offset_b[None, :, None, None]
            ho, wo = (o.shape[2], o.shape[3])
            off = o[:, :2 * kk].reshape(b, kk, 2, ho, wo)
            dy, dx = (off[:, :, 0], off[:, :, 1])
            mask = jax.nn.sigmoid(o[:, 2 * kk:])
            ki, kj = jnp.meshgrid(jnp.arange(K), jnp.arange(K), indexing='ij')
            ki = ki.reshape(kk).astype(jnp.float32)
            kj = kj.reshape(kk).astype(jnp.float32)
            base_y = (jnp.arange(ho, dtype=jnp.float32) * STRIDE - PAD)[None, None, :, None] + ki[None, :, None, None]
            base_x = (jnp.arange(wo, dtype=jnp.float32) * STRIDE - PAD)[None, None, None, :] + kj[None, :, None, None]
            py = base_y + dy
            px = base_x + dx
            y0 = jnp.floor(py)
            x0 = jnp.floor(px)
            wy = py - y0
            wx = px - x0
            y0i = y0.astype(jnp.int32)
            x0i = x0.astype(jnp.int32)
            xT = x.transpose(0, 2, 3, 1)
            bidx = jnp.arange(b)[:, None, None, None]

            def gather(yi, xi):
                valid = (yi >= 0) & (yi < h) & (xi >= 0) & (xi < w)
                yc = jnp.clip(yi, 0, h - 1)
                xc = jnp.clip(xi, 0, w - 1)
                v = xT[bidx, yc, xc]
                return v * valid[..., None].astype(x.dtype)
            g00 = gather(y0i, x0i)
            g01 = gather(y0i, x0i + 1)
            g10 = gather(y0i + 1, x0i)
            g11 = gather(y0i + 1, x0i + 1)
            wy_ = wy[..., None]
            wx_ = wx[..., None]
            sampled = g00 * (1 - wy_) * (1 - wx_) + g01 * (1 - wy_) * wx_ + g10 * wy_ * (1 - wx_) + g11 * wy_ * wx_
            sampled = sampled * mask[..., None]
            wk = dcn_w.reshape(dcn_w.shape[0], c, kk)
            return jnp.einsum('bkhwc,ock->bohw', sampled, wk)
        return _dcnv2(x, offset_w, offset_b, dcn_w)

    def _L0_ffn_ref(x, W_gat, att_src, att_dst, b_gat, ln_gamma, ln_beta, W1, b1, W2, b2, edge_index):
        import jax, jax.numpy as jnp
        import numpy as np
        B, N, D = (16, 2048, 128)
        NUM_EXPERTS, TOP_K, HEADS = (4, 2, 4)
        N_EDGES = 524288
        LN_EPS = 1e-05

        def _layernorm(x, g, b):
            mu = x.mean(-1, keepdims=True)
            var = ((x - mu) ** 2).mean(-1, keepdims=True)
            return (x - mu) * jax.lax.rsqrt(var + LN_EPS) * g + b

        def _forward(x, edge_index, W_gat, att_src, att_dst, b_gat, ln_gamma, ln_beta, W1, b1, W2, b2):
            Bc, Nc, Dc = x.shape
            M = Bc * Nc
            x_flat = x.reshape(M, Dc)
            h = (x_flat @ W_gat).reshape(M, HEADS, NUM_EXPERTS)
            loops = jnp.arange(M, dtype=edge_index.dtype)
            src = jnp.concatenate([edge_index[0], loops])
            dst = jnp.concatenate([edge_index[1], loops])
            a_src = (h * att_src).sum(-1)
            a_dst = (h * att_dst).sum(-1)
            e = jax.nn.leaky_relu(a_src[src] + a_dst[dst], negative_slope=0.2)
            e_max = jax.ops.segment_max(e, dst, num_segments=M)
            ee = jnp.exp(e - e_max[dst])
            denom = jax.ops.segment_sum(ee, dst, num_segments=M)
            alpha = ee / (denom[dst] + 1e-16)
            msg = h[src] * alpha[:, :, None]
            agg = jax.ops.segment_sum(msg, dst, num_segments=M).reshape(M, HEADS * NUM_EXPERTS) + b_gat
            scores = _layernorm(agg, ln_gamma, ln_beta).reshape(M, HEADS, NUM_EXPERTS).mean(1)
            scores = scores.reshape(Bc, Nc, NUM_EXPERTS)
            topk_s, topk_i = jax.lax.top_k(scores, TOP_K)
            w = jax.nn.softmax(topk_s, axis=-1)
            out = jnp.zeros_like(x)
            for ei in range(NUM_EXPERTS):
                g = jnp.where(topk_i == ei, w, 0.0).sum(-1)
                hh = jax.nn.gelu(x @ W1[ei] + b1[ei], approximate=False)
                out = out + g[..., None] * (hh @ W2[ei] + b2[ei])
            return out
        return _forward(x, edge_index, W_gat, att_src, att_dst, b_gat, ln_gamma, ln_beta, W1, b1, W2, b2)

    def _gn(v, G=32, eps=1e-05):
        B_, C_, H_, W_ = v.shape
        g = v.reshape(B_, G, C_ // G, H_, W_)
        m = jnp.mean(g, axis=(2, 3, 4), keepdims=True)
        s = jnp.var(g, axis=(2, 3, 4), keepdims=True)
        return ((g - m) / jnp.sqrt(s + eps)).reshape(v.shape)

    def _ln_c(v, eps=1e-06):
        m = jnp.mean(v, axis=1, keepdims=True)
        s = jnp.var(v, axis=1, keepdims=True)
        return (v - m) / jnp.sqrt(s + eps)

    def _ln_t(v, eps=1e-05):
        m = jnp.mean(v, axis=-1, keepdims=True)
        s = jnp.var(v, axis=-1, keepdims=True)
        return (v - m) / jnp.sqrt(s + eps)

    def _to_tokens(v):
        B_, C_, H_, W_ = v.shape
        return v.reshape(B_, C_, H_ * W_).transpose(0, 2, 1)

    def _from_tokens(t, like):
        B_, C_, H_, W_ = like.shape
        return t.transpose(0, 2, 1).reshape(B_, C_, H_, W_)
    x = x + _L0_conv_ref(_ln_c(x), L0_conv_offset_w, L0_conv_offset_b, L0_conv_dcn_w)
    t = _to_tokens(x)
    t = t + _L0_ffn_ref(_ln_t(t), L0_ffn_W_gat, L0_ffn_att_src, L0_ffn_att_dst, L0_ffn_b_gat, L0_ffn_ln_gamma, L0_ffn_ln_beta, L0_ffn_W1, L0_ffn_b1, L0_ffn_W2, L0_ffn_b2, L0_ffn_edge_index)
    x = _from_tokens(t, x)
    return x

_drawn_inputs = setup_inputs


def setup_inputs(seed=0):
    import zlib

    import numpy as np

    out = dict(_drawn_inputs(seed))
    spreads = {'L0_ffn_b_gat': (0.0, 0.8),
     'L0_ffn_ln_gamma': (1.0, 0.6),
     'L0_ffn_ln_beta': (0.0, 0.8),
     'L0_ffn_b1': (0.0, 0.1),
     'L0_ffn_b2': (0.0, 0.1)}
    factors = {'L0_conv_offset_b': 8.0, 'L0_ffn_att_src': 8.0, 'L0_ffn_att_dst': 8.0}
    for name, (base, spread) in spreads.items():
        noise = np.random.default_rng([zlib.crc32(name.encode()), seed]).standard_normal(out[name].shape)
        drawn = base * np.exp(spread * noise) if base else spread * noise
        out[name] = jnp.asarray(drawn.astype(out[name].dtype))
    for name, factor in factors.items():
        out[name] = (out[name] * factor).astype(out[name].dtype)
    return out
```

```python
from contextlib import ExitStack

import concourse.bass as bass
from concourse import mybir

P = 128
ALU = mybir.AluOpType
ACT = mybir.ActivationFunctionType
AX = mybir.AxisListType
F32 = mybir.dt.float32
BF16 = mybir.dt.bfloat16
I32 = mybir.dt.int32
RMAX = bass.bass_isa.ReduceOp.max


class Steps:

    def __init__(self, sem):
        self.sem, self.base, self.n = sem, 0, 0

    def now(self):
        return self.base + self.n

    def add(self, ins):
        ins.then_inc(self.sem, 1)
        self.n += 1


def metaformer(nc, x, offw, offb, dcnw, wgat, att_s, att_d, b_gat, ln_g, ln_b, w1, b1, w2, b2, edges, out,
               general_always=False):
    B, C, H, W = x.shape
    HW = H * W
    M = B * HW
    NT = M // P
    TB = HW // P
    K = 9
    NOFF = 3 * K
    HEADS, NE = att_s.shape
    HE = HEADS * NE
    HID = w1.shape[2]
    NF = HID // P
    EC = edges.shape[1] // P
    SHIFTS = [0, 1, W, W + 1]
    FRONT = W + 1
    EPS_C, EPS_T = 1e-6, 1e-5

    SEG = 256
    NSEG = EC // SEG
    CAP = 64
    PCAP = 16
    SUB = 13
    NSUB = NT // 4
    PC = SUB * NSUB
    ROW = HEADS + HEADS * (NE + 1)
    VAL = HEADS * (NE + 1)
    LO = 64
    assert PC % 8 == 0 and EC % SEG == 0 and NSEG * 2 == NT and M == LO * LO and NE == 4

    with ExitStack() as ctx:
        def sb(name, shape, dt=F32):
            return ctx.enter_context(nc.sbuf_tensor(name, shape, dt))

        def sem(name):
            return ctx.enter_context(nc.semaphore(name))

        cells = nc.dram_tensor("cells", [FRONT + M, 4 * C], F32)
        src_rows = nc.dram_tensor("src_rows", [M, ROW], F32)
        dst_rows = nc.dram_tensor("dst_rows", [M, HEADS], F32)

        chan = sb("chan", [P, M])
        x_tok = sb("x_tok", [P, NT, C])
        n_tok = sb("n_tok", [P, NT, C])
        padded = sb("padded", [P, 4624])
        onehots = padded[:, 0:4096].bitcast(BF16).rearrange("p (h j c) -> p h j c", h=2, j=LO)
        late_at = [0]

        def late(shape):
            n = 1
            for d in shape[1:]:
                n *= d
            late_at[0] += n
            assert late_at[0] <= 4624
            flat = padded[:, late_at[0] - n:late_at[0]]
            if len(shape) == 3:
                return flat.rearrange("p (a b) -> p a b", b=shape[2])
            return flat.rearrange("p (a b c) -> p a b c", b=shape[2], c=shape[3])

        arena = sb("arena", [P, 2 * EC + 2 * K * 4 * C])
        edge_i = arena[:, 0:2 * EC].bitcast(I32).rearrange("p (s e) -> p s e", s=2)
        edge_f = arena[:, 0:2 * EC].bitcast(I32)
        cell = arena[:, 2 * EC:].rearrange("p (u k f) -> p u k f", u=2, k=K)
        shifted = arena[:, 2 * EC:2 * EC + 6 * (H + 2) * W].rearrange("p (u s y x) -> p u s y x", u=2, s=3, y=H + 2)
        shifted_flat = arena[:, 2 * EC:2 * EC + 6 * (H + 2) * W].rearrange("p (u s f) -> p u s f", u=2, s=3)
        y_exp = arena[:, 0:NT * NE * C].rearrange("p (i e c) -> p i e c", i=NT, e=NE)
        NAB, NST = 2 * 2 * K * C, 2 * K * C
        scratch = sb("scratch", [P, NAB + NST])
        mixed = scratch[:, 0:NAB].rearrange("p (u h k c) -> p u h k c", u=2, h=2, k=K)
        samp = scratch[:, NAB:].rearrange("p (u k c) -> p u k c", u=2, k=K)

        ident = sb("ident", [P, P])
        last_row = sb("last_row", [P, P])
        fold = sb("fold", [LO, 2, P])
        offw_sb = sb("offw_sb", [P, K, NOFF])
        dcnw_sb = sb("dcnw_sb", [P, K, C])
        wgat_sb = sb("wgat_sb", [P, HE])
        w1_sb = sb("w1_sb", [P, NE, HID])
        w2_sb = sb("w2_sb", [P, NE, NF, C])
        b1_sb = sb("b1_sb", [P, NE, NF])
        b2_sb = sb("b2_sb", [P, NE, C])
        offb_sb = sb("offb_sb", [P, NOFF])
        small = sb("small", [P, 5, HE])

        iota_i = sb("iota_i", [P, P], I32)
        iota_f = sb("iota_f", [P, P])
        lanes = sb("lanes", [P, LO, 64], BF16)
        part_i = sb("part_i", [P, 4], I32)
        part_f = sb("part_f", [P, 4])
        zero_bf = sb("zero_bf", [P, LO], BF16)
        zero_f = sb("zero_f", [P, 320])
        pool_gate = sb("pool_gate", [P, 4])
        dve_gate = sb("dve_gate", [P, 64])

        stats = sb("stats", [P, NT, 6])
        st_a = sb("st_a", [P, 3, NT])
        mean = sb("mean", [P, NT])
        rstd = sb("rstd", [P, NT])

        idx_f = sb("idx_f", [P, NT + 2, K])
        corner_w = sb("corner_w", [P, NT + 2, 4, K])
        idx_slot = sb("idx_slot", [P, 2, K], I32)
        w_slot = sb("w_slot", [P, 2, 4, K])

        key_a = sb("key_a", [P, 2, SEG])
        kept = sb("kept", [P, CAP + 8])
        kept_i = sb("kept_i", [P, 3, CAP], I32)
        kept_lohi = sb("kept_lohi", [P, 2, CAP], BF16)
        pairs1 = sb("pairs1", [P, NSEG * PCAP])
        pairs2 = sb("pairs2", [P, PC + 8])
        lost = sb("lost", [P, 2])
        pk_i = sb("pk_i", [P, 4, PC], I32)
        pk_src = sb("pk_src", [P, PC + 2 * SUB])
        pk_dst = sb("pk_dst", [P, PC + 2 * SUB])
        pk_lo = sb("pk_lo", [P, PC])
        pk_hi = sb("pk_hi", [P, PC])
        pk_void = sb("pk_void", [P, PC])
        hist_sb = sb("hist_sb", [LO, LO])
        count = sb("count", [P, NT])

        trow = late([P, NT, ROW])
        a_dst = late([P, NT, HEADS])
        tmp16 = late([P, NT, HE])
        amax_p = sb("amax_p", [P, HEADS + 1])
        amax = sb("amax", [P, HEADS + 1])
        last_tok = sb("last_tok", [P, ROW])
        src_idx = sb("src_idx", [P, 2, SUB], I32)
        dst_idx = sb("dst_idx", [P, 2, SUB], I32)
        src_got = late([P, 2, SUB, ROW])
        dst_got = late([P, 2, SUB, HEADS])
        lg = late([P, 4, SUB, HEADS])
        ex = late([P, SUB, HEADS])
        val = arena[:, NT * NE * C + NT * VAL:NT * NE * C + (NT + SUB) * VAL].rearrange("p (c v) -> p c v", v=VAL)
        hi_hot = late([P, SUB, NT])
        lo_hot = scratch[:, 0:SUB * P].rearrange("p (c l) -> p c l", c=SUB)
        NR = 4
        spread = scratch[:, SUB * P:SUB * P + NR * NT * VAL].rearrange("p (r i v) -> p r i v", r=NR, i=NT)
        hid = scratch[:, 4608:4608 + 2048].rearrange("p (f t) -> p f t", f=4)
        sums = late([P, NT, VAL])
        dn = late([P, 6, NT, HEADS])
        score = late([P, NT, NE])
        gate = late([P, NT, NE])
        cmp = scratch[:, 6656:6912].rearrange("p (n i) -> p n i", n=8)
        general_i = sb("general_i", [P, 1], I32)
        GC = 8
        g_edge = sb("g_edge", [P, 2, GC], I32)
        g_int = sb("g_int", [P, 2, GC], I32)
        g_lohi = sb("g_lohi", [P, 2, GC])

        act_gate = sb("act_gate", [P, 4])
        off_sb = scratch[:, 0:NT * NOFF].rearrange("p (t c) -> p t c", c=NOFF)
        TK = NT * K
        (py, px, cy, cx, hy0, hy1, hx0, hx1, mask) = (
            scratch[:, NT * NOFF + n * TK:NT * NOFF + (n + 1) * TK].rearrange("p (t k) -> p t k", k=K) for n in range(9))
        (cy_i, cx_i, by_i, bx_i, bt_i) = (
            scratch[:, NT * NOFF + (9 + n) * TK:NT * NOFF + (10 + n) * TK].bitcast(I32).rearrange("p (t k) -> p t k", k=K)
            for n in range(5))
        bigf = arena[:, NT * NE * C:NT * NE * C + NT * VAL]
        big = bigf[:, :].rearrange("p (i h f) -> p i h f", h=HEADS, f=NE + 1)
        N_ENDS = sum((FRONT > shift) + (shift > 0) for shift in SHIFTS)
        POOL_CONST = 14
        HID_CREDIT = 2
        LOOP_STEPS = 25
        PAIR_STEPS = 6

        banks = [ctx.enter_context(nc.psum_tensor(f"bank{n}", [P, 512], F32)) for n in range(8)]

        x_in = [sem(f"x_in{b}") for b in range(B)]
        w_in = sem("w_in")
        e_in = sem("e_in")
        pool_step = sem("pool_step")
        x_turned, x_copied = sem("x_turned"), sem("x_copied")
        var_ready, root_done = sem("var_ready"), sem("root_done")
        zeros_ready, ends_out = sem("zeros_ready"), sem("ends_out")
        gate_done = sem("gate_done")
        general_known = sem("general_known")
        g_rows_in = [[sem(f"general_{n}_in{u}") for n in ("src", "dst")] for u in range(2)]
        (g_step, g_free, g_edges_in, g_idx, g_lg, g_ex, g_spread, g_used, g_sums, g_gate) = (
            sem("general_" + n) for n in ("step", "free", "edges_in", "idx", "lg", "ex", "spread", "used", "sums",
                                          "gate"))
        normed, n_turned, n_copied = sem("normed"), sem("n_turned"), sem("n_copied")
        cells_out = [sem(f"cells_out{b}") for b in range(B)]
        off_done, off_read, mask_done = sem("off_done"), sem("off_read"), sem("mask_done")
        dve = sem("dve")
        act = sem("act")
        idx_ready = sem("idx_ready")
        cells_in = [sem(f"cells_in{u}") for u in range(2)]
        scaled, mixed_done, turned, samp_ready, conv_done = (
            sem(n) for n in ("scaled", "mixed_done", "turned", "samp_ready", "conv_done"))
        hot_ready, hist_done = sem("hot_ready"), sem("hist_done")
        hist_copied, folded = sem("hist_copied"), sem("folded")
        t_normed, t_turned, t_copied = sem("t_normed"), sem("t_turned"), sem("t_copied")
        proj_done, rows_ready, rows_out = sem("proj_done"), sem("rows_ready"), sem("rows_out")
        amax_ready, amax_done, last_done = sem("amax_ready"), sem("amax_done"), sem("last_done")
        pair_idx_ready = sem("pair_idx_ready")
        pair_in = [sem(f"pair_in{u}") for u in range(2)]
        pair_lg, pair_ex = sem("pair_lg"), sem("pair_ex")
        spread_ready, spread_used = sem("spread_ready"), sem("spread_used")
        up_done, hid_ready, down_done, y_ready = sem("up_done"), sem("hid_ready"), sem("down_done"), sem("y_ready")
        sums_done = sem("sums_done")
        dn_ready, dn_exp = sem("dn_ready"), sem("dn_exp")
        sc_ready, sc_exp = sem("sc_ready"), sem("sc_exp")
        res_ready, res_turned, res_copied, res_out = (sem(n) for n in ("res_ready", "res_turned", "res_copied", "res_out"))

        block = ctx.enter_context(nc.Block())

        PARAMS = [(offw_sb[:, :, :], offw), (dcnw_sb[:, :, :], dcnw), (wgat_sb[:, :], wgat),
                  (w1_sb[:, :, :], w1.rearrange("e d f -> d e f")),
                  (w2_sb[:, :, :, :], w2.rearrange("e (f p) d -> p e f d", p=P)),
                  (b1_sb[:, :, :], b1),
                  (b2_sb[:, :, :], b2.partition_broadcast(P)),
                  (offb_sb[:, :], offb.partition_broadcast(P))]
        PARAMS += [(small[:, n, :], v.partition_broadcast(P)) for n, v in enumerate(
            (att_s.rearrange("h e -> (h e)"), att_d.rearrange("h e -> (h e)"), b_gat, ln_g, ln_b))]

        @block.sync
        def _(sp):
            for b in range(B):
                sp.dma_start(chan[:, b * HW:(b + 1) * HW], x[b].rearrange("c h w -> c (h w)")).then_inc(x_in[b], 16)
            for dst, src in PARAMS:
                sp.dma_start(dst, src).then_inc(w_in, 16)
            for s in range(2):
                sp.dma_start(edge_i[:, s, :], edges[s].rearrange("(p e) -> p e", p=P)).then_inc(e_in, 16)
            sp.wait_ge(zeros_ready, 1)
            for c, shift in enumerate(SHIFTS):
                for r0, r1 in ((0, FRONT - shift), (FRONT + M - shift, FRONT + M)):
                    if r1 > r0:
                        sp.dma_start(cells[r0:r1, c * C:(c + 1) * C], zero_f[0:r1 - r0, 0:C]).then_inc(ends_out, 16)
            for b in range(B):
                sp.wait_ge(normed, b + 1)
                for c, shift in enumerate(SHIFTS):
                    r0 = FRONT + b * HW - shift
                    sp.dma_start(cells[r0:r0 + HW, c * C:(c + 1) * C].rearrange("(i p) c -> p i c", p=P),
                                 n_tok[:, b * TB:(b + 1) * TB, :]).then_inc(cells_out[b], 16)
            sp.wait_ge(rows_ready, 1)
            sp.dma_start(src_rows[:, :].rearrange("(i p) c -> p i c", p=P), trow[:, :, :]).then_inc(rows_out, 16)
            sp.dma_start(dst_rows[:, :].rearrange("(i p) c -> p i c", p=P), a_dst[:, :, :]).then_inc(rows_out, 16)
            sp.wait_ge(general_known, 1)
            general = sp.value_load(general_i[0:1, 0:1], min_val=0, max_val=1)
            with sp.If(general == 1):
                with sp.Fori(0, EC // GC) as it:
                    sp.wait_ge(g_free, it + 1)
                    for s in range(2):
                        sp.dma_start(g_edge[:, s, :], edges[s].rearrange("(p e) -> p e", p=P)[:, bass.ds(it * GC, GC)])\
                            .then_inc(g_edges_in, 16)
            for g in range(NT // 4):
                sp.wait_ge(res_copied, g + 1)
                b, h = divmod(g, TB // 4)
                sp.dma_start(out[b].rearrange("c h w -> c (h w)")[:, h * 512:(h + 1) * 512],
                             chan[:, g * 512:(g + 1) * 512]).then_inc(res_out, 16)
            sp.wait_ge(res_out, 16 * (NT // 4))

        @block.gpsimd
        def _(pool):
            st = Steps(pool_step)
            st.add(nc.gpsimd.memset(ident[:, :], 0.0))
            st.add(nc.gpsimd.memset(last_row[:, :], 1.0))
            st.add(nc.gpsimd.memset(fold[:, :, :], 0.0))
            nc.gpsimd.memset(pool_gate[:, :], 0.0).then_inc(gate_done, 1)
            st.add(nc.gpsimd.memset(arena[:, 2 * EC:2 * EC + 6 * (H + 2) * W], 0.0))
            pool.wait_ge(pool_step, st.now())
            st.add(nc.gpsimd.affine_select(out=ident[:, :], in_=ident[:, :], compare_op=ALU.not_equal, fill=1.0,
                                           base=0, pattern=[[-1, P]], channel_multiplier=1))
            st.add(nc.gpsimd.affine_select(out=last_row[:, :], in_=last_row[:, :], compare_op=ALU.is_ge, fill=0.0,
                                           base=-(P - 1), pattern=[[0, P]], channel_multiplier=1))
            for h in range(2):
                st.add(nc.gpsimd.affine_select(out=fold[:, h, :], in_=fold[:, h, :], compare_op=ALU.not_equal,
                                               fill=1.0, base=h * LO, pattern=[[-1, P]], channel_multiplier=1))
            st.add(nc.gpsimd.iota(iota_i[:, :], [[1, P]], base=0, channel_multiplier=0))
            st.add(nc.gpsimd.iota(lanes[:, :, :], [[1, LO], [0, 64]], base=0, channel_multiplier=0,
                                  allow_small_or_imprecise_dtypes=True))
            st.add(nc.gpsimd.iota(part_i[:, 0:1], [[0, 1]], base=0, channel_multiplier=1))
            st.add(nc.gpsimd.iota(by_i, [[0, B], [P // W, TB], [1, 3], [0, 3]], base=-1, channel_multiplier=0))
            st.add(nc.gpsimd.iota(bx_i, [[0, NT], [0, 3], [1, 3]], base=-1, channel_multiplier=0))
            st.add(nc.gpsimd.iota(bt_i, [[HW, B], [0, TB], [0, K]], base=FRONT, channel_multiplier=0))
            assert st.n == POOL_CONST

            for b in range(B):
                pool.wait_ge(cells_out[b], 64)
            pool.wait_ge(ends_out, 16 * N_ENDS)
            with pool.Fori(0, NT // 2) as it:
                for u in range(2):
                    pool.wait_ge(idx_ready, 2 * it + u + 1)
                    pool.wait_ge(gate_done, 2 * it + u + 1)
                    nc.gpsimd.tensor_tensor(pool_gate[:, u:u + 1], ident[:, 0:1], ident[:, 1:2], ALU.add).then_inc(gate_done, 1)
                    for k in range(K):
                        nc.gpsimd.indirect_dma_start(
                            cell[:, u, k, :], None, cells[:, :],
                            bass.IndirectOffsetOnAxis(ap=idx_slot[:, u, k:k + 1], axis=0)).then_inc(cells_in[u], 16)

            pool.wait_ge(amax_ready, 1)
            nc.gpsimd.partition_all_reduce(amax[:, :], amax_p[:, :], P, RMAX).then_inc(amax_done, 1)
            pool.wait_ge(rows_out, 32)
            with pool.Fori(0, NSUB // 2) as it:
                for u in range(2):
                    pool.wait_ge(pair_idx_ready, 2 * it + u + 1)
                    pool.wait_ge(gate_done, 2 * it + u + 1 + NT)
                    nc.gpsimd.tensor_tensor(pool_gate[:, 2 + u:3 + u], ident[:, 0:1], ident[:, 1:2], ALU.add).then_inc(gate_done, 1)
                    for c in range(SUB):
                        nc.gpsimd.indirect_dma_start(
                            src_got[:, u, c, :], None, src_rows[:, :],
                            bass.IndirectOffsetOnAxis(ap=src_idx[:, u, c:c + 1], axis=0)).then_inc(pair_in[u], 16)
                        nc.gpsimd.indirect_dma_start(
                            dst_got[:, u, c, :], None, dst_rows[:, :],
                            bass.IndirectOffsetOnAxis(ap=dst_idx[:, u, c:c + 1], axis=0)).then_inc(pair_in[u], 16)

            pool.wait_ge(general_known, 1)
            general = pool.value_load(general_i[0:1, 0:1], min_val=0, max_val=1)
            with pool.If(general == 1):
                nc.gpsimd.memset(pool_gate[:, 0:2], 0.0).then_inc(g_gate, 1)
                with pool.Fori(0, EC // GC // 2) as it:
                  for u in range(2):
                    pool.wait_ge(g_idx, 2 * it + u + 1)
                    pool.wait_ge(g_gate, 2 * it + u + 1)
                    nc.gpsimd.tensor_tensor(pool_gate[:, 0:1], ident[:, 0:1], ident[:, 1:2], ALU.add).then_inc(g_gate, 1)
                    for c in range(GC):
                        nc.gpsimd.indirect_dma_start(
                            src_got[:, 0, c, :], None, src_rows[:, :],
                            bass.IndirectOffsetOnAxis(ap=src_idx[:, 0, c:c + 1], axis=0)).then_inc(g_rows_in[u][0], 16)
                        nc.gpsimd.indirect_dma_start(
                            dst_got[:, 0, c, :], None, dst_rows[:, :],
                            bass.IndirectOffsetOnAxis(ap=dst_idx[:, 0, c:c + 1], axis=0)).then_inc(g_rows_in[u][1], 16)

        @block.tensor
        def _(pe):
            pe.wait_ge(pool_step, POOL_CONST)
            for b in range(B):
                pe.wait_ge(x_in[b], 16)
                for h in range(2):
                    g = 2 * b + h
                    if g >= 2:
                        pe.wait_ge(x_copied, g - 1)
                    for q in range(4):
                        t = 4 * g + q
                        mm = nc.tensor.transpose(banks[g % 2][:, q * P:(q + 1) * P], chan[:, t * P:(t + 1) * P], ident[:, :])
                    mm.then_inc(x_turned, 1)
            pe.wait_ge(w_in, 16 * len(PARAMS))
            for b in range(B):
                pe.wait_ge(normed, b + 1)
                for h in range(2):
                    g = 2 * b + h
                    if g >= 2:
                        pe.wait_ge(n_copied, g - 1)
                    for q in range(4):
                        mm = nc.tensor.transpose(banks[2 + g % 2][:, q * P:(q + 1) * P], n_tok[:, 4 * g + q, :], ident[:, :])
                    mm.then_inc(n_turned, 1)
                pe.wait_ge(n_copied, 2 * b + 2)
                for q in range(TB):
                    t = b * TB + q
                    o = banks[4 + t // 16][:, (t % 16) * 32:(t % 16) * 32 + NOFF]
                    y0 = q * (P // W)
                    for k in range(K):
                        ki, kj = divmod(k, 3)
                        mm = nc.tensor.matmul(o, shifted_flat[:, b % 2, kj, (y0 + ki) * W:(y0 + ki) * W + P], offw_sb[:, k, :],
                                              start=(k == 0), stop=(k == K - 1))
                mm.then_inc(off_done, 1)

            hist = banks[7][0:LO, 0:LO]
            nc.tensor.matmul(hist, zero_bf[:, :], zero_bf[:, :], start=True, stop=False).then_inc(hist_done, 1)
            with pe.Fori(0, NT // 2) as it:
                for u in range(2):
                    acc = banks[3 + u][:, 0:C]

                    def turn(g):
                        pe.wait_ge(mixed_done, 6 * it + 3 * u + g + 1)
                        for j in range(3):
                            for h in range(2):
                                mm = nc.tensor.matmul(banks[g][:, j * P:(j + 1) * P], mixed[:, u, h, 3 * g + j, :],
                                                      ident[:, :], start=(h == 0), stop=(h == 1))
                        mm.then_inc(turned, 1)

                    def weigh(g):
                        pe.wait_ge(samp_ready, 6 * it + 3 * u + g + 1)
                        for k in range(3 * g, 3 * g + 3):
                            mm = nc.tensor.matmul(acc, samp[:, u, k, :], dcnw_sb[:, k, :], start=(k == 0), stop=(k == K - 1))
                        if g == 2:
                            mm.then_inc(conv_done, 1)
                    turn(0)
                    turn(1)
                    weigh(0)
                    turn(2)
                    weigh(1)
                    weigh(2)
                pe.wait_ge(hot_ready, it + 1)
                for c in range(CAP):
                    mm = nc.tensor.matmul(hist, onehots[:, 0, :, c], onehots[:, 1, :, c], start=False, stop=False)
                mm.then_inc(hist_done, 1)
            nc.tensor.matmul(hist, zero_bf[:, :], zero_bf[:, :], start=False, stop=True).then_inc(hist_done, 1)

            proj = banks[2]
            for g in range(NT // 4 + 1):
                if g < NT // 4:
                    pe.wait_ge(t_normed, g + 1)
                    if g >= 2:
                        pe.wait_ge(t_copied, g - 1)
                    for q in range(4):
                        mm = nc.tensor.transpose(banks[g % 2][:, q * P:(q + 1) * P], n_tok[:, 4 * g + q, :], ident[:, :])
                    mm.then_inc(t_turned, 1)
                if g >= 1:
                    pe.wait_ge(t_copied, g)
                    for t in range(4 * g - 4, 4 * g):
                        mm = nc.tensor.matmul(proj[:, t * HE:(t + 1) * HE], chan[:, t * P:(t + 1) * P], wgat_sb[:, :],
                                              start=True, stop=True)
            mm.then_inc(proj_done, 1)
            pe.wait_ge(hist_copied, 1)
            hv = hist_sb[:, :].rearrange("l (i h) -> l h i", h=2)
            for h in range(2):
                mm = nc.tensor.matmul(banks[3][:, 0:NT], fold[:, h, :], hv[:, h, :], start=(h == 0), stop=(h == 1))
            mm.then_inc(folded, 1)
            pe.wait_ge(rows_ready, 1)
            nc.tensor.matmul(banks[6][:, 0:ROW], last_row[:, :], trow[:, NT - 1, :], start=True, stop=True)\
                .then_inc(last_done, 1)

            half = NT // 2 * VAL
            sum_bank = [banks[0][:, 0:half], banks[1][:, 0:half]]
            for h in range(2):
                pe.wait_ge(t_copied, NT // 4)
                mm = nc.tensor.matmul(sum_bank[h], zero_f[:, 0:P], zero_f[:, 0:half], start=True, stop=False)
            mm.then_inc(spread_used, NR)
            with pe.Fori(0, NSUB // 2) as it:
                for u in range(2):
                    sub = 2 * it + u
                    col = 0
                    for e in range(NE):
                        chunk = chan[:, bass.ds(sub * 512, 512)]
                        for f in range(NF):
                            n = e * NF + f
                            pe.wait_ge(hid_ready, NE * NF * sub + n + 1)
                            nc.tensor.matmul(banks[4 + n % 2][:, :], w1_sb[:, e, f * P:(f + 1) * P], chunk,
                                             start=True, stop=True).then_inc(up_done, 1)
                        for _ in range(4 if e == 0 else 3):
                            pe.wait_ge(spread_ready, SUB * sub + col + 1)
                            for h in range(2):
                                mm = nc.tensor.matmul(sum_bank[h], lo_hot[:, col, :],
                                                      spread[:, col % NR, h * NT // 2:(h + 1) * NT // 2, :],
                                                      start=False, stop=False)
                            mm.then_inc(spread_used, 1)
                            col += 1
                        pe.wait_ge(hid_ready, NE * NF * sub + (e + 1) * NF + HID_CREDIT)
                        pe.wait_ge(y_ready, NE * sub + e + 1)
                        for q in range(4):
                            for f in range(NF):
                                mm = nc.tensor.matmul(banks[6 + e % 2][:, q * C:(q + 1) * C],
                                                      hid[:, (e % 2) * NF + f, q * P:(q + 1) * P], w2_sb[:, e, f, :],
                                                      start=(f == 0), stop=(f == NF - 1))
                        mm.then_inc(down_done, 1)
            for h in range(2):
                mm = nc.tensor.matmul(sum_bank[h], zero_f[:, 0:P], zero_f[:, 0:half], start=False, stop=True)
            mm.then_inc(sums_done, 1)

            pe.wait_ge(general_known, 1)
            general = pe.value_load(general_i[0:1, 0:1], min_val=0, max_val=1)
            with pe.If(general == 1):
                for h in range(2):
                    mm = nc.tensor.matmul(sum_bank[h], zero_f[:, 0:P], zero_f[:, 0:half], start=True, stop=False)
                mm.then_inc(g_used, NR)
                with pe.Fori(0, EC // GC) as it:
                    for col in range(GC):
                        pe.wait_ge(g_spread, GC * it + col + 1)
                        for h in range(2):
                            mm = nc.tensor.matmul(sum_bank[h], lo_hot[:, col, :],
                                                  spread[:, col % NR, h * NT // 2:(h + 1) * NT // 2, :],
                                                  start=False, stop=False)
                        mm.then_inc(g_used, 1)
                for h in range(2):
                    mm = nc.tensor.matmul(sum_bank[h], zero_f[:, 0:P], zero_f[:, 0:half], start=False, stop=True)
                mm.then_inc(g_sums, 1)

            for g in range(NT // 4):
                pe.wait_ge(res_ready, g + 1)
                if g >= 2:
                    pe.wait_ge(res_copied, g - 1)
                if g < 2:
                    pe.wait_ge(down_done, NE * NSUB)
                for q in range(4):
                    mm = nc.tensor.transpose(banks[4 + g % 2][:, q * P:(q + 1) * P], x_tok[:, 4 * g + q, :], ident[:, :])
                mm.then_inc(res_turned, 1)

        @block.scalar
        def _(ac):
            def root(v, n):
                ac.wait_ge(var_ready, n)
                nc.scalar.sqrt(v, v).then_inc(root_done, 1)

            for g in range(NT // 4):
                ac.wait_ge(x_turned, g + 1)
                nc.scalar.copy(x_tok[:, 4 * g:4 * g + 4, :], banks[g % 2][:, :]).then_inc(x_copied, 1)
                if g % 2 == 1:
                    b = g // 2
                    root(rstd[:, b * TB:(b + 1) * TB], b + 1)
            ac.wait_ge(pool_step, POOL_CONST)
            for g in range(NT // 4):
                ac.wait_ge(n_turned, g + 1)
                b, h = divmod(g, 2)
                if b >= 2:
                    ac.wait_ge(off_done, b - 1)
                img = banks[2 + g % 2][:, :].rearrange("p (y x) -> p y x", x=W)
                rows = slice(1 + 16 * h, 17 + 16 * h)
                nc.scalar.copy(shifted[:, b % 2, 0, rows, 1:W], img[:, :, 0:W - 1])
                nc.scalar.copy(shifted[:, b % 2, 1, rows, :], img)
                nc.scalar.copy(shifted[:, b % 2, 2, rows, 0:W - 1], img[:, :, 1:W]).then_inc(n_copied, 1)
            ac.wait_ge(off_read, 1)
            nc.scalar.activation(mask, off_sb[:, :, 2 * K:3 * K], ACT.Sigmoid).then_inc(mask_done, 1)

            with ac.Fori(0, NT // 2) as it:
                for u in range(2):
                    ac.wait_ge(cells_in[u], 16 * K * (it + 1))

                    def scale(g):
                        for k in range(3 * g, 3 * g + 3):
                            for h in range(2):
                                ins = nc.scalar.activation(mixed[:, u, h, k, :], cell[:, u, k, h * C:(h + 1) * C], ACT.Copy,
                                                           scale=w_slot[:, u, h, k:k + 1])
                        ins.then_inc(scaled, 1)

                    def evict(g):
                        ac.wait_ge(turned, 6 * it + 3 * u + g + 1)
                        nc.scalar.copy(samp[:, u, 3 * g:3 * g + 3, :], banks[g][:, 0:3 * P]).then_inc(samp_ready, 1)
                    scale(0)
                    scale(1)
                    evict(0)
                    scale(2)
                    evict(1)
                    evict(2)

            root(rstd[:, :], B + 1)
            for g in range(NT // 4):
                ac.wait_ge(t_turned, g + 1)
                nc.scalar.copy(chan[:, g * 512:(g + 1) * 512], banks[g % 2][:, :]).then_inc(t_copied, 1)

            ac.wait_ge(off_read, 1)
            nc.scalar.copy(act_gate[:, 0:1], ident[:, 0:1]).then_inc(hid_ready, HID_CREDIT)
            with ac.Fori(0, NSUB // 2) as it:
                for u in range(2):
                    sub = 2 * it + u
                    ac.wait_ge(pair_lg, sub + 1)
                    nc.scalar.activation(ex[:, :, :], lg[:, 3, :, :], ACT.Exp).then_inc(pair_ex, 1)
                    for e in range(NE):
                        for f in range(NF):
                            n = e * NF + f
                            ac.wait_ge(up_done, NE * NF * sub + n + 1)
                            nc.scalar.activation(hid[:, (e % 2) * NF + f, :], banks[4 + n % 2][:, :], ACT.Gelu,
                                                 bias=b1_sb[:, e, f:f + 1]).then_inc(hid_ready, 1)
            ac.wait_ge(general_known, 1)
            general = ac.value_load(general_i[0:1, 0:1], min_val=0, max_val=1)
            with ac.If(general == 1):
                with ac.Fori(0, EC // GC) as it:
                    ac.wait_ge(g_lg, it + 1)
                    nc.scalar.activation(ex[:, 0:GC, :], lg[:, 3, 0:GC, :], ACT.Exp).then_inc(g_ex, 1)
            ac.wait_ge(dn_ready, 1)
            nc.scalar.activation(dn[:, 0:2, :, :], dn[:, 0:2, :, :], ACT.Exp).then_inc(dn_exp, 1)
            root(cmp[:, 1, :], B + 2)
            ac.wait_ge(sc_ready, 1)
            nc.scalar.activation(gate[:, :, :], gate[:, :, :], ACT.Exp).then_inc(sc_exp, 1)
            for g in range(NT // 4):
                ac.wait_ge(res_turned, g + 1)
                nc.scalar.copy(chan[:, g * 512:(g + 1) * 512], banks[4 + g % 2][:, :]).then_inc(res_copied, 1)

        @block.vector
        def _(ve):
            st = Steps(dve)
            V = nc.vector

            def done(ins):
                st.add(ins)
                ve.wait_ge(dve, st.now())

            roots = [0]

            def moments(i0, n, eps):
                s = stats[:, i0:i0 + n, :]
                a, d, v = (st_a[:, j, i0:i0 + n] for j in range(3))
                V.tensor_tensor(a, s[:, :, 1], s[:, :, 4], ALU.add)
                V.tensor_tensor(d, s[:, :, 1], s[:, :, 4], ALU.subtract)
                done(V.tensor_tensor(v, s[:, :, 2], s[:, :, 5], ALU.add))
                V.tensor_scalar(mean[:, i0:i0 + n], a, 0.5, None, ALU.mult)
                done(V.tensor_tensor(d, d, d, ALU.mult))
                done(V.scalar_tensor_tensor(out=v, in0=d, scalar=C / 4.0, in1=v, op0=ALU.mult, op1=ALU.add))
                V.tensor_scalar(rstd[:, i0:i0 + n], v, 1.0 / C, eps, ALU.mult, ALU.add).then_inc(var_ready, 1)
                roots[0] += 1
                ve.wait_ge(root_done, roots[0])
                done(V.reciprocal(rstd[:, i0:i0 + n], rstd[:, i0:i0 + n]))

            V.memset(zero_bf[:, :], 0.0)
            V.memset(zero_f[:, :], 0.0).then_inc(zeros_ready, 1)
            V.memset(lost[:, :], 0.0)
            V.memset(pk_src[:, :], 0.0)
            V.memset(pk_dst[:, :], 0.0)
            V.memset(idx_f[:, NT:NT + 2, :], 0.0)
            V.memset(corner_w[:, NT:NT + 2, :, :], 0.0)
            done(V.memset(dve_gate[:, :], 0.0))

            for b in range(B):
                for h in range(2):
                    ve.wait_ge(x_copied, 2 * b + h + 1)
                    for q in range(4):
                        t = b * TB + 4 * h + q
                        ins = V.bn_stats(stats[:, t, :], x_tok[:, t, :])
                done(ins)
                moments(b * TB, TB, EPS_C)
                for t in range(b * TB, (b + 1) * TB):
                    ins = V.tensor_scalar(n_tok[:, t, :], x_tok[:, t, :], mean[:, t:t + 1], rstd[:, t:t + 1],
                                          ALU.subtract, ALU.mult)
                ins.then_inc(normed, 1)

            ve.wait_ge(pool_step, POOL_CONST)
            V.tensor_copy(iota_f[:, :], iota_i[:, :])
            V.tensor_scalar(part_i[:, 1:2], part_i[:, 0:1], 5, None, ALU.arith_shift_right)
            done(V.tensor_scalar(part_i[:, 2:3], part_i[:, 0:1], W - 1, None, ALU.bitwise_and))
            done(V.tensor_copy(part_f[:, 1:3], part_i[:, 1:3]))

            ve.wait_ge(w_in, 16 * len(PARAMS))
            ve.wait_ge(off_done, B)
            for h in range(2):
                o = banks[4 + h][:, :].rearrange("p (t c) -> p t c", c=32)[:, :, 0:NOFF]
                ins = V.tensor_tensor(off_sb[:, 16 * h:16 * h + 16, :], o,
                                      offb_sb[:, :].unsqueeze(1).to_broadcast([P, 16, NOFF]), ALU.add)
            st.add(ins)
            V.tensor_scalar(py, by_i, part_f[:, 1:2], None, ALU.add)
            done(V.tensor_scalar(px, bx_i, part_f[:, 2:3], None, ALU.add))
            dyx = off_sb[:, :, 0:2 * K].rearrange("p t (k s) -> p t k s", s=2)
            V.tensor_tensor(py, py, dyx[:, :, :, 0], ALU.add).then_inc(off_read, 1)
            done(V.tensor_tensor(px, px, dyx[:, :, :, 1], ALU.add))
            for q, c in ((py, cy), (px, cx)):
                ins = V.tensor_scalar(c, q, -0.5, 0.0, ALU.add, ALU.max)
            done(ins)
            V.tensor_scalar(cy_i, cy, float(H - 2), None, ALU.min)
            done(V.tensor_scalar(cx_i, cx, float(W - 2), None, ALU.min))
            V.tensor_copy(cy, cy_i)
            done(V.tensor_copy(cx, cx_i))
            V.tensor_tensor(py, py, cy, ALU.subtract)
            V.tensor_tensor(px, px, cx, ALU.subtract)
            done(V.scalar_tensor_tensor(out=cy, in0=cy, scalar=float(W), in1=cx, op0=ALU.mult, op1=ALU.add))
            V.tensor_tensor(idx_f[:, 0:NT, :], cy, bt_i, ALU.add)
            for r, h0, h1 in ((py, hy0, hy1), (px, hx0, hx1)):
                V.tensor_scalar(h0, r, -1.0, 1.0, ALU.mult, ALU.add)
                ins = V.tensor_scalar(h1, r, -1.0, 2.0, ALU.mult, ALU.add)
            done(ins)
            for r, h0, h1 in ((py, hy0, hy1), (px, hx0, hx1)):
                V.scalar_tensor_tensor(out=h0, in0=r, scalar=1.0, in1=h0, op0=ALU.add, op1=ALU.min)
                ins = V.scalar_tensor_tensor(out=h1, in0=r, scalar=1.0, in1=h1, op0=ALU.mult, op1=ALU.min)
            done(ins)
            ve.wait_ge(mask_done, 1)
            V.tensor_scalar(hx0, hx0, 0.0, None, ALU.max)
            V.tensor_scalar(hx1, hx1, 0.0, None, ALU.max)
            V.scalar_tensor_tensor(out=hy0, in0=hy0, scalar=0.0, in1=mask, op0=ALU.max, op1=ALU.mult)
            done(V.scalar_tensor_tensor(out=hy1, in0=hy1, scalar=0.0, in1=mask, op0=ALU.max, op1=ALU.mult))
            for c, (hy, hx) in enumerate(((hy0, hx0), (hy0, hx1), (hy1, hx0), (hy1, hx1))):
                ins = V.tensor_tensor(corner_w[:, 0:NT, c, :], hy, hx, ALU.mult)
            done(ins)
            for u in range(2):
                V.tensor_copy(w_slot[:, u, :, :], corner_w[:, u, :, :])
                V.tensor_copy(idx_slot[:, u, :], idx_f[:, u, :]).then_inc(idx_ready, 1)

            idx_flat = idx_f[:, :, :].rearrange("p t k -> p (t k)")
            w_flat = corner_w[:, :, :, :].rearrange("p t c k -> p (t c k)")
            x_flat = x_tok[:, :, :].rearrange("p t c -> p (t c)")
            ve.wait_ge(e_in, 32)
            loop_at = st.now()
            st.base, st.n = None, 0
            STEPS = LOOP_STEPS
            with ve.Fori(0, NT // 2) as it:
                st.base = it * STEPS + loop_at
                gates = [0]

                def step(ins):
                    st.add(ins)
                    ve.wait_ge(dve, st.now())

                def gated(ins_of):
                    V.tensor_scalar(dve_gate[0:1, gates[0]:gates[0] + 1], iota_f[0:1, 0:1], 0.0, None, ALU.add)
                    gates[0] += 1
                    step(ins_of())

                def tile_work(u):
                    for g in range(3):
                        ve.wait_ge(scaled, 6 * it + 3 * u + g + 1)
                        for k in range(3 * g, 3 * g + 3):
                            for h in range(2):
                                ins = V.scalar_tensor_tensor(
                                    out=mixed[:, u, h, k, :], in0=cell[:, u, k, (2 + h) * C:(3 + h) * C],
                                    scalar=w_slot[:, u, 2 + h, k:k + 1], in1=mixed[:, u, h, k, :],
                                    op0=ALU.mult, op1=ALU.add)
                        ins.then_inc(mixed_done, 1)
                    ve.wait_ge(mixed_done, 6 * it + 3 * u + 3)
                    V.tensor_scalar(w_slot[:, u, :, :].rearrange("p c k -> p (c k)"),
                                    w_flat[:, bass.ds((2 * it + u + 2) * 4 * K, 4 * K)], 0.0, None, ALU.add)
                    V.tensor_scalar(idx_slot[:, u, :], idx_flat[:, bass.ds((2 * it + u + 2) * K, K)],
                                    0.0, None, ALU.add).then_inc(idx_ready, 1)

                def residual(u):
                    ve.wait_ge(conv_done, 2 * it + u + 1)
                    xs = x_flat[:, bass.ds((2 * it + u) * C, C)]
                    st.add(V.tensor_tensor(xs, banks[3 + u][:, 0:C], xs, ALU.add))

                tile_work(0)
                e_src = edge_f[:, bass.ds(it * SEG, SEG)]
                e_dst = edge_f[:, bass.ds(it * SEG + EC, SEG)]
                ka, kb = key_a[:, 0, :], key_a[:, 1, :]
                V.tensor_scalar(kb, e_dst, float(M), None, ALU.is_lt)
                step(V.tensor_scalar(ka, e_src, float(M - 1), -float(M), ALU.min, ALU.mult))
                step(V.scalar_tensor_tensor(out=ka, in0=ka, scalar=float(M * (M - 1) + 1), in1=e_dst, op0=ALU.add, op1=ALU.add))
                step(V.tensor_tensor(ka, ka, kb, ALU.mult))
                for r in range(CAP // 8 + 1):
                    top = kept[:, 8 * r:8 * r + 8]
                    gated(lambda: V.max(top, ka))
                    if r < CAP // 8:
                        gated(lambda: V.match_replace(ka, top, ka, 0.0))
                residual(0)
                V.tensor_tensor(lost[:, 0:1], lost[:, 0:1], kept[:, CAP:CAP + 1], ALU.max)
                V.scalar_tensor_tensor(out=lost[:, 1:2], in0=kept[:, PCAP:PCAP + 1], scalar=float(M) + 0.5,
                                       in1=lost[:, 1:2], op0=ALU.is_gt, op1=ALU.max)
                V.tensor_scalar(pairs1[:, bass.ds(it * PCAP, PCAP)], kept[:, 0:PCAP], 0.0, None, ALU.add)
                step(V.tensor_scalar(kept_i[:, 0, :], kept[:, 0:CAP], -1.0, None, ALU.add))
                tile_work(1)
                V.tensor_scalar(kept_i[:, 1, :], kept_i[:, 0, :], LO - 1, None, ALU.bitwise_and)
                step(V.tensor_scalar(kept_i[:, 2, :], kept_i[:, 0, :], 6, None, ALU.arith_shift_right))
                step(V.tensor_copy(kept_lohi[:, :, :], kept_i[:, 1:3, :]))
                ve.wait_ge(hist_done, it + 1)
                for h in range(2):
                    ins = V.tensor_tensor(onehots[:, h, :, :], lanes[:, :, :],
                                          kept_lohi[:, h, :].unsqueeze(1).to_broadcast([P, LO, CAP]), ALU.is_equal)
                ins.then_inc(hot_ready, 1)
                residual(1)
                assert st.n == STEPS, st.n
            st.base, st.n = loop_at + STEPS * (NT // 2), 0

            ve.wait_ge(dve, st.now())
            ve.wait_ge(hist_done, NT // 2 + 2)
            V.tensor_copy(hist_sb[:, :], banks[7][0:LO, 0:LO]).then_inc(hist_copied, 1)
            for r in range(PC // 8 + 1):
                top = pairs2[:, 8 * r:8 * r + 8]
                if r == 0:
                    V.tensor_scalar(lost[:, 0:1], lost[:, 0:1], lost[:, 1:2], None, ALU.max)
                    hits = key_a[:, 0, 0:NSEG * PCAP]
                    done(V.tensor_scalar(hits, pairs1[:, :], float(M) + 0.5, None, ALU.is_gt))
                    done(V.tensor_tensor(pairs1[:, :], pairs1[:, :], hits, ALU.mult))
                done(V.max(top, pairs1[:, :]))
                if r < PC // 8:
                    done(V.match_replace(pairs1[:, :], top, pairs1[:, :], 0.0))
            V.tensor_tensor(lost[:, 0:1], lost[:, 0:1], pairs2[:, PC:PC + 1], ALU.max)

            for t in range(NT):
                ins = V.bn_stats(stats[:, t, :], x_tok[:, t, :])
            done(ins)
            moments(0, NT, EPS_T)
            ve.wait_ge(cells_out[B - 1], 64)
            for t in range(NT):
                ins = V.tensor_scalar(n_tok[:, t, :], x_tok[:, t, :], mean[:, t:t + 1], rstd[:, t:t + 1],
                                      ALU.subtract, ALU.mult)
                if t % 4 == 3:
                    ins.then_inc(t_normed, 1)

            keys = pairs2[:, 0:PC]
            V.tensor_scalar(pk_void[:, :], keys, 0.5, 64.0, ALU.is_lt, ALU.mult)
            done(V.tensor_scalar(pk_i[:, 0, :], keys, -1.0, None, ALU.add))
            V.tensor_scalar(pk_i[:, 1, :], pk_i[:, 0, :], 12, None, ALU.arith_shift_right)
            V.tensor_scalar(pk_i[:, 2, :], pk_i[:, 0, :], M - 1, None, ALU.bitwise_and)
            done(V.tensor_scalar(pk_i[:, 3, :], pk_i[:, 0, :], P - 1, None, ALU.bitwise_and))
            V.tensor_scalar(pk_src[:, 0:PC], pk_i[:, 1, :], -1.0, float(M - 1), ALU.mult, ALU.add)
            V.tensor_copy(pk_dst[:, 0:PC], pk_i[:, 2, :])
            V.tensor_copy(pk_lo[:, :], pk_i[:, 3, :])
            done(V.tensor_scalar(pk_i[:, 0, :], pk_i[:, 2, :], 7, None, ALU.arith_shift_right))
            V.tensor_scalar(pk_src[:, 0:PC], pk_src[:, 0:PC], float(M - 1), None, ALU.min)
            done(V.tensor_tensor(pk_hi[:, :], pk_i[:, 0, :], pk_void[:, :], ALU.add))
            for u in range(2):
                V.tensor_copy(src_idx[:, u, :], pk_src[:, u * SUB:(u + 1) * SUB])
                V.tensor_copy(dst_idx[:, u, :], pk_dst[:, u * SUB:(u + 1) * SUB]).then_inc(pair_idx_ready, 1)

            done(V.memset(trow[:, :, :], 1.0))
            h_of = trow[:, :, HEADS:ROW].rearrange("p i (h f) -> p i h f", h=HEADS)[:, :, :, 1:]
            ve.wait_ge(proj_done, 1)
            pv = banks[2][:, :].rearrange("p (i f) -> p i f", f=HE)
            pv4 = banks[2][:, :].rearrange("p (i h e) -> p i h e", h=HEADS, e=NE)
            V.tensor_copy(h_of, pv4)
            for n, dst in ((0, trow[:, :, 0:HEADS]), (1, a_dst[:, :, :])):
                done(V.tensor_tensor(tmp16[:, :, :], pv, small[:, n, :].unsqueeze(1).to_broadcast([P, NT, HE]), ALU.mult))
                ins = V.tensor_reduce(dst, tmp16[:, :, :].rearrange("p i (h e) -> p i h e", e=NE), AX.X, ALU.add)
                done(ins)
            V.tensor_scalar(amax_p[:, HEADS:HEADS + 1], lost[:, 0:1], 1.0 if general_always else 0.0, None, ALU.add)
            V.tensor_reduce(amax_p[:, 0:HEADS], trow[:, :, 0:HEADS].rearrange("p i h -> p h i"), AX.X, ALU.max)\
                .then_inc(amax_ready, 1)
            V.tensor_copy(act_gate[:, 1:2], ident[:, 0:1]).then_inc(rows_ready, 1)

            ve.wait_ge(folded, 1)
            V.tensor_copy(count[:, :], banks[3][:, 0:NT])
            ve.wait_ge(last_done, 1)
            done(V.tensor_copy(last_tok[:, :], banks[6][:, 0:ROW]))

            a_src = trow[:, :, 0:HEADS]
            ve.wait_ge(amax_done, 1)
            V.tensor_scalar(general_i[:, :], amax[:, HEADS:HEADS + 1], 0.5, None, ALU.is_gt).then_inc(general_known, 1)
            V.tensor_tensor(dn[:, 0, :, :], a_src, a_dst[:, :, :], ALU.add)
            V.tensor_tensor(dn[:, 1, :, :], a_dst[:, :, :], last_tok[:, 0:HEADS].unsqueeze(1).to_broadcast([P, NT, HEADS]), ALU.add)
            done(V.tensor_tensor(dn[:, 2, :, :], a_dst[:, :, :], amax[:, 0:HEADS].unsqueeze(1).to_broadcast([P, NT, HEADS]), ALU.add))
            done(V.scalar_tensor_tensor(out=dn[:, 0:3, :, :], in0=dn[:, 0:3, :, :], scalar=0.2, in1=dn[:, 0:3, :, :],
                                        op0=ALU.mult, op1=ALU.max))
            V.tensor_tensor(dn[:, 0, :, :], dn[:, 0, :, :], dn[:, 2, :, :], ALU.subtract)
            V.tensor_tensor(dn[:, 1, :, :], dn[:, 1, :, :], dn[:, 2, :, :], ALU.subtract).then_inc(dn_ready, 1)

            def one_hots(lo, hi, n):
                V.tensor_tensor(lo_hot[:, 0:n, :], iota_f[:, :].unsqueeze(1).to_broadcast([P, n, P]),
                                lo.unsqueeze(2).to_broadcast([P, n, P]), ALU.is_equal)
                V.tensor_tensor(hi_hot[:, 0:n, :], iota_f[:, 0:NT].unsqueeze(1).to_broadcast([P, n, NT]),
                                hi.unsqueeze(2).to_broadcast([P, n, NT]), ALU.is_equal)

            def exponents(step, sg, dg, n):
                V.tensor_tensor(lg[:, 0, 0:n, :], sg[:, :, 0:HEADS], dg, ALU.add)
                step(V.tensor_tensor(lg[:, 1, 0:n, :], dg, amax[:, 0:HEADS].unsqueeze(1).to_broadcast([P, n, HEADS]), ALU.add))
                step(V.scalar_tensor_tensor(out=lg[:, 0:2, 0:n, :], in0=lg[:, 0:2, 0:n, :], scalar=0.2,
                                            in1=lg[:, 0:2, 0:n, :], op0=ALU.mult, op1=ALU.max))
                return V.tensor_tensor(lg[:, 3, 0:n, :], lg[:, 0, 0:n, :], lg[:, 1, 0:n, :], ALU.subtract)

            def messages(sg, n):
                return V.tensor_tensor(val[:, 0:n, :].rearrange("p c (h f) -> p c h f", h=HEADS),
                                       sg[:, :, HEADS:ROW].rearrange("p c (h f) -> p c h f", h=HEADS),
                                       ex[:, 0:n, :].unsqueeze(3).to_broadcast([P, n, HEADS, NE + 1]), ALU.mult)

            def spread_column(col):
                return V.tensor_tensor(spread[:, col % NR, :, :],
                                       hi_hot[:, col, :].unsqueeze(2).to_broadcast([P, NT, VAL]),
                                       val[:, col, :].unsqueeze(1).to_broadcast([P, NT, VAL]), ALU.mult)

            V.tensor_copy(act_gate[:, 2:3], ident[:, 0:1]).then_inc(y_ready, 1)
            V.tensor_copy(act_gate[:, 3:4], ident[:, 0:1]).then_inc(y_ready, 1)
            loop_at = st.now()
            PSTEPS = PAIR_STEPS
            with ve.Fori(0, NSUB // 2) as it:
                st.base, st.n = it * PSTEPS + loop_at, 0

                def step(ins):
                    st.add(ins)
                    ve.wait_ge(dve, st.now())

                for u in range(2):
                    sub = 2 * it + u
                    sg, dg = src_got[:, u, :, :], dst_got[:, u, :, :]
                    ve.wait_ge(spread_used, SUB * sub + NR)
                    one_hots(pk_lo[:, bass.ds(sub * SUB, SUB)], pk_hi[:, bass.ds(sub * SUB, SUB)], SUB)
                    ve.wait_ge(pair_in[u], 32 * SUB * (it + 1))
                    exponents(step, sg, dg, SUB).then_inc(pair_lg, 1)
                    ve.wait_ge(pair_ex, sub + 1)
                    step(messages(sg, SUB))
                    V.tensor_scalar(src_idx[:, u, :], pk_src[:, bass.ds((sub + 2) * SUB, SUB)], 0.0, None, ALU.add)
                    V.tensor_scalar(dst_idx[:, u, :], pk_dst[:, bass.ds((sub + 2) * SUB, SUB)], 0.0, None, ALU.add)\
                        .then_inc(pair_idx_ready, 1)
                    col = 0
                    for e in range(NE):
                        for _ in range(4 if e == 0 else 3):
                            if col >= NR:
                                ve.wait_ge(spread_used, SUB * sub + col + 1)
                            spread_column(col).then_inc(spread_ready, 1)
                            col += 1
                        ve.wait_ge(down_done, NE * sub + e + 1)
                        V.tensor_tensor(y_exp[:, bass.ds(sub * 4, 4), e, :],
                                        banks[6 + e % 2][:, :].rearrange("p (q c) -> p q c", q=4),
                                        b2_sb[:, e, :].unsqueeze(1).to_broadcast([P, 4, C]), ALU.add).then_inc(y_ready, 1)
                assert st.n == PSTEPS, st.n
            st.base, st.n = loop_at + PSTEPS * (NSUB // 2), 0

            ve.wait_ge(sums_done, 1)
            ve.wait_ge(general_known, 1)
            general = ve.value_load(general_i[0:1, 0:1], min_val=0, max_val=1)
            with ve.If(general == 1):
                V.tensor_scalar(count[:, :], count[:, :], 0.0, None, ALU.mult)
                V.tensor_copy(act_gate[:, 1:2], ident[:, 0:1]).then_inc(g_free, 1)
                V.tensor_copy(act_gate[:, 2:3], ident[:, 0:1]).then_inc(g_step, 1)
                G_STEPS = 5
                with ve.Fori(0, EC // GC // 2) as it:
                  for u in range(2):
                    gs = Steps(g_step)
                    gs.base = (2 * it + u) * G_STEPS + 1

                    def step(ins):
                        gs.add(ins)
                        ve.wait_ge(g_step, gs.now())

                    ve.wait_ge(g_step, gs.now())
                    ve.wait_ge(g_edges_in, 64 * it + 32 * u + 32)
                    V.tensor_scalar(src_idx[:, 0, 0:GC], g_edge[:, 0, :], float(M - 1), None, ALU.min)
                    V.tensor_scalar(dst_idx[:, 0, 0:GC], g_edge[:, 1, :], float(M - 1), None, ALU.min).then_inc(g_idx, 1)
                    V.tensor_scalar(g_int[:, 0, :], g_edge[:, 1, :], P - 1, None, ALU.bitwise_and)
                    step(V.tensor_scalar(g_int[:, 1, :], g_edge[:, 1, :], 7, None, ALU.arith_shift_right))
                    step(V.tensor_copy(g_lohi[:, :, :], g_int[:, :, :]))
                    V.tensor_scalar(dve_gate[0:1, 0:1], iota_f[0:1, 0:1], 0.0, None, ALU.add).then_inc(g_free, 1)
                    ve.wait_ge(g_used, GC * (2 * it + u) + NR)
                    one_hots(g_lohi[:, 0, :], g_lohi[:, 1, :], GC)
                    for n in range(2):
                        ve.wait_ge(g_rows_in[u][n], 16 * GC * (it + 1))
                    exponents(step, src_got[:, 0, 0:GC, :], dst_got[:, 0, 0:GC, :], GC).then_inc(g_lg, 1)
                    ve.wait_ge(g_ex, 2 * it + u + 1)
                    step(messages(src_got[:, 0, 0:GC, :], GC))
                    for col in range(GC):
                        if col >= NR:
                            ve.wait_ge(g_used, GC * (2 * it + u) + col + 1)
                        spread_column(col).then_inc(g_spread, 1)
                    assert gs.n == G_STEPS, gs.n
                ve.wait_ge(g_sums, 1)

            for h in range(2):
                ins = V.tensor_copy(sums[:, h * NT // 2:(h + 1) * NT // 2, :], banks[h][:, 0:NT // 2 * VAL])
            done(ins)
            ve.wait_ge(dn_exp, 1)
            own, lastw = dn[:, 0, :, :], dn[:, 1, :, :]
            done(V.tensor_tensor(lastw, lastw, count[:, :].unsqueeze(2).to_broadcast([P, NT, HEADS]), ALU.mult))
            sums4 = sums[:, :, :].rearrange("p i (h f) -> p i h f", h=HEADS)
            rows4 = trow[:, :, HEADS:ROW].rearrange("p i (h f) -> p i h f", h=HEADS)
            last4 = last_tok[:, HEADS:ROW].rearrange("p (h f) -> p h f", h=HEADS)
            F = NE + 1
            for h in range(HEADS):
                V.tensor_tensor(rows4[:, :, h, :], rows4[:, :, h, :], own[:, :, h].unsqueeze(2).to_broadcast([P, NT, F]), ALU.mult)
                ins = V.tensor_tensor(big[:, :, h, :], last4[:, h, :].unsqueeze(1).to_broadcast([P, NT, F]),
                                      lastw[:, :, h].unsqueeze(2).to_broadcast([P, NT, F]), ALU.mult)
            done(ins)
            done(V.tensor_tensor(sums[:, :, :], sums[:, :, :], trow[:, :, HEADS:ROW], ALU.add))
            done(V.tensor_tensor(sums4, sums4, big, ALU.add))
            den = dn[:, 2, :, :]
            done(V.tensor_scalar(den, sums4[:, :, :, 0], 1e-16, None, ALU.add))
            done(V.reciprocal(den, den))
            t4 = tmp16[:, :, :].rearrange("p i (h e) -> p i h e", e=NE)
            done(V.tensor_tensor(t4, sums4[:, :, :, 1:], den.unsqueeze(3).to_broadcast([P, NT, HEADS, NE]), ALU.mult))

            def vec(n):
                return small[:, n, :].unsqueeze(1).to_broadcast([P, NT, HE])
            done(V.tensor_tensor(tmp16[:, :, :], tmp16[:, :, :], vec(2), ALU.add))
            mu, var = cmp[:, 0, :], cmp[:, 1, :]
            done(V.tensor_reduce(mu, tmp16[:, :, :], AX.X, ALU.add))
            done(V.tensor_scalar(mu, mu, 1.0 / HE, None, ALU.mult))
            done(V.tensor_tensor(tmp16[:, :, :], tmp16[:, :, :], mu.unsqueeze(2).to_broadcast([P, NT, HE]), ALU.subtract))
            sq = bigf[:, 0:NT * HE].rearrange("p (i f) -> p i f", f=HE)
            done(V.tensor_tensor(sq, tmp16[:, :, :], tmp16[:, :, :], ALU.mult))
            done(V.tensor_reduce(var, sq, AX.X, ALU.add))
            V.tensor_scalar(var, var, 1.0 / HE, EPS_T, ALU.mult, ALU.add).then_inc(var_ready, 1)
            ve.wait_ge(root_done, B + 2)
            done(V.reciprocal(var, var))
            done(V.tensor_tensor(tmp16[:, :, :], tmp16[:, :, :], var.unsqueeze(2).to_broadcast([P, NT, HE]), ALU.mult))
            done(V.tensor_tensor(tmp16[:, :, :], tmp16[:, :, :], vec(3), ALU.mult))
            done(V.tensor_tensor(tmp16[:, :, :], tmp16[:, :, :], vec(4), ALU.add))
            done(V.tensor_reduce(score[:, :, :], tmp16[:, :, :].rearrange("p i (h e) -> p i e h", e=NE), AX.X, ALU.add))
            done(V.tensor_scalar(score[:, :, :], score[:, :, :], 1.0 / HEADS, None, ALU.mult))
            top = cmp[:, 2, :]
            done(V.tensor_reduce(top, score[:, :, :], AX.X, ALU.max))
            V.tensor_tensor(gate[:, :, :], score[:, :, :], top.unsqueeze(2).to_broadcast([P, NT, NE]), ALU.subtract)\
                .then_inc(sc_ready, 1)
            beat = bigf[:, 0:NE * NT].rearrange("p (e i) -> p e i", e=NE)
            done(V.memset(beat, 0.0))
            for a in range(NE):
                for b in range(a + 1, NE):
                    done(V.tensor_tensor(cmp[:, 3, :], score[:, :, a], score[:, :, b], ALU.is_ge))
                    V.tensor_tensor(beat[:, b, :], beat[:, b, :], cmp[:, 3, :], ALU.add)
                    done(V.tensor_tensor(cmp[:, 4, :], score[:, :, a], score[:, :, b], ALU.is_lt))
                    done(V.tensor_tensor(beat[:, a, :], beat[:, a, :], cmp[:, 4, :], ALU.add))
            ve.wait_ge(sc_exp, 1)
            done(V.scalar_tensor_tensor(out=gate[:, :, :], in0=beat.rearrange("p e i -> p i e"), scalar=1.5,
                                        in1=gate[:, :, :], op0=ALU.is_lt, op1=ALU.mult))
            done(V.tensor_reduce(cmp[:, 5, :], gate[:, :, :], AX.X, ALU.add))
            done(V.reciprocal(cmp[:, 5, :], cmp[:, 5, :]))
            done(V.tensor_tensor(gate[:, :, :], gate[:, :, :], cmp[:, 5, :].unsqueeze(2).to_broadcast([P, NT, NE]), ALU.mult))

            for g in range(NT // 4):
                for e in range(NE):
                    for t in range(4 * g, 4 * g + 4):
                        ins = V.scalar_tensor_tensor(out=x_tok[:, t, :], in0=y_exp[:, t, e, :], scalar=gate[:, t, e:e + 1],
                                                     in1=x_tok[:, t, :], op0=ALU.mult, op1=ALU.add)
                    if e < NE - 1:
                        done(ins)
                ins.then_inc(res_ready, 1)


_INS = ["x", "L0_conv_offset_w", "L0_conv_offset_b", "L0_conv_dcn_w", "L0_ffn_W_gat", "L0_ffn_att_src", "L0_ffn_att_dst",
        "L0_ffn_b_gat", "L0_ffn_ln_gamma", "L0_ffn_ln_beta", "L0_ffn_W1", "L0_ffn_b1", "L0_ffn_W2", "L0_ffn_b2",
        "L0_ffn_edge_index"]


def kernel(**inputs):
    import numpy as np
    import concourse.bacc as bacc
    from concourse import mybir as mb
    from concourse.bass_utils import run_bass_kernel_spmd as run

    nc = bacc.Bacc("TRN2", target_bir_lowering=False, num_devices=1)
    arrays, args = {}, []
    for name in _INS:
        a = np.asarray(inputs[name])
        if name == "L0_conv_offset_w" or name == "L0_conv_dcn_w":
            a = a.reshape(a.shape[0], a.shape[1], 9).transpose(1, 2, 0)
        if name == "L0_ffn_b1":
            a = a.reshape(a.shape[0], -1, 128).transpose(2, 0, 1)
        a = np.ascontiguousarray(a)
        arrays[f"in_{name}_dram"] = a
        args.append(nc.dram_tensor(f"in_{name}_dram", a.shape, mb.dt.from_np(a.dtype), kind="ExternalInput").ap())
    args.append(nc.dram_tensor("out_0_dram", inputs["x"].shape, mb.dt.float32, kind="ExternalOutput").ap())
    metaformer(nc, *args)
    r = run(nc, [arrays], core_ids=[0])
    return r.results[0]["out_0_dram"]
```

```python
from contextlib import ExitStack

import concourse.bass as bass
from concourse import mybir

P = 128
ALU = mybir.AluOpType
ACT = mybir.ActivationFunctionType
AX = mybir.AxisListType
F32 = mybir.dt.float32
BF16 = mybir.dt.bfloat16
I32 = mybir.dt.int32
RMAX = bass.bass_isa.ReduceOp.max


class Steps:

    def __init__(self, sem):
        self.sem, self.base, self.n = sem, 0, 0

    def now(self):
        return self.base + self.n

    def add(self, ins):
        ins.then_inc(self.sem, 1)
        self.n += 1


def metaformer(nc, x, offw, offb, dcnw, wgat, att_s, att_d, b_gat, ln_g, ln_b, w1, b1, w2, b2, edges, out,
               general_always=False):
    B, C, H, W = x.shape
    HW = H * W
    M = B * HW
    NT = M // P
    TB = HW // P
    K = 9
    NOFF = 3 * K
    HEADS, NE = att_s.shape
    HE = HEADS * NE
    HID = w1.shape[2]
    NF = HID // P
    EC = edges.shape[1] // P
    SHIFTS = [0, 1, W, W + 1]
    FRONT = W + 1
    EPS_C, EPS_T = 1e-6, 1e-5

    SEG = 256
    NSEG = EC // SEG
    CAP = 64
    PCAP = 16
    SUB = 13
    NSUB = NT // 4
    PC = SUB * NSUB
    ROW = HEADS + HEADS * (NE + 1)
    VAL = HEADS * (NE + 1)
    LO = 64
    assert PC % 8 == 0 and EC % SEG == 0 and NSEG * 2 == NT and M == LO * LO and NE == 4

    with ExitStack() as ctx:
        def sb(name, shape, dt=F32):
            return ctx.enter_context(nc.sbuf_tensor(name, shape, dt))

        def sem(name):
            return ctx.enter_context(nc.semaphore(name))

        cells = nc.dram_tensor("cells", [FRONT + M, 4 * C], F32)
        src_rows = nc.dram_tensor("src_rows", [M, ROW], F32)
        dst_rows = nc.dram_tensor("dst_rows", [M, HEADS], F32)

        chan = sb("chan", [P, M])
        x_all = sb("x_all", [P, 1 + NT, C])
        x_tok = x_all[:, 1:, :]
        n_tok = sb("n_tok", [P, NT, C])
        PH, PW = H + 2, W + 2
        padded = sb("padded", [P, B * PH * PW])
        ringed = padded[:, :].rearrange("p (b y x) -> p b y x", b=B, y=PH)
        onehots = padded[:, 0:4096].bitcast(BF16).rearrange("p (h j c) -> p h j c", h=2, j=LO)
        late_at = [0]

        def late(shape):
            n = 1
            for d in shape[1:]:
                n *= d
            late_at[0] += n
            assert late_at[0] <= B * PH * PW
            flat = padded[:, late_at[0] - n:late_at[0]]
            if len(shape) == 3:
                return flat.rearrange("p (a b) -> p a b", b=shape[2])
            return flat.rearrange("p (a b c) -> p a b c", b=shape[2], c=shape[3])

        arena = sb("arena", [P, 2 * EC + 2 * K * 4 * C])
        edge_i = arena[:, 0:2 * EC].bitcast(I32).rearrange("p (s e) -> p s e", s=2)
        edge_f = arena[:, 0:2 * EC].bitcast(I32)
        cell = arena[:, 2 * EC:].rearrange("p (u k c f) -> p u k c f", u=2, k=K, c=4)
        y_exp = arena[:, 0:NT * NE * C].rearrange("p (i e c) -> p i e c", i=NT, e=NE)
        NSC, NST = 6912, 2 * K * C
        scratch = sb("scratch", [P, NSC])
        samp = scratch[:, NSC - NST:].rearrange("p (u k c) -> p u k c", u=2, k=K)

        ident = sb("ident", [P, P])
        last_row = sb("last_row", [P, P])
        fold = sb("fold", [LO, 2, P])
        offw_sb = sb("offw_sb", [P, K, 32])
        dcnw_sb = sb("dcnw_sb", [P, K, C])
        wgat_sb = sb("wgat_sb", [P, HE])
        w1_sb = sb("w1_sb", [P, NE, HID])
        w2_sb = sb("w2_sb", [P, NE, NF, C])
        b1_sb = sb("b1_sb", [P, NE, NF])
        b2_sb = sb("b2_sb", [P, NE, C])
        offb_sb = sb("offb_sb", [P, NOFF])
        small = sb("small", [P, 5, HE])

        iota_i = arena[:, 2 * EC:2 * EC + P].bitcast(I32)
        iota_f = sb("iota_f", [P, P])
        lanes = sb("lanes", [P, LO, 64], BF16)
        part_i = sb("part_i", [P, 4], I32)
        part_f = sb("part_f", [P, 4])
        zero_bf = sb("zero_bf", [P, LO], BF16)
        zero_f = sb("zero_f", [P, 320])
        pool_gate = sb("pool_gate", [P, 5])
        dve_gate = sb("dve_gate", [P, 64])

        stats = sb("stats", [P, NT, 6])
        st_a = sb("st_a", [P, 3, NT])
        mean = sb("mean", [P, NT])
        rstd = sb("rstd", [P, NT])

        idx_f = sb("idx_f", [P, NT + 2, K])
        corner_w = sb("corner_w", [P, NT + 2, 4, K])
        idx_slot = sb("idx_slot", [P, 2, K], I32)
        w_slot = sb("w_slot", [P, 2, 4, K])

        key_a = sb("key_a", [P, 2, SEG])
        kept = sb("kept", [P, CAP + 8])
        kept_i = sb("kept_i", [P, 3, CAP], I32)
        kept_lohi = sb("kept_lohi", [P, 2, CAP], BF16)
        pairs1 = sb("pairs1", [P, NSEG * PCAP])
        pairs2 = sb("pairs2", [P, PC + 8])
        lost = sb("lost", [P, 2])
        pk_i = sb("pk_i", [P, 4, PC], I32)
        pk_src = sb("pk_src", [P, PC + 2 * SUB])
        pk_dst = sb("pk_dst", [P, PC + 2 * SUB])
        pk_lo = sb("pk_lo", [P, PC])
        pk_hi = sb("pk_hi", [P, PC])
        pk_void = sb("pk_void", [P, PC])
        hist_sb = sb("hist_sb", [LO, LO])
        count = sb("count", [P, NT])

        trow = late([P, NT, ROW])
        a_dst = late([P, NT, HEADS])
        tmp16 = late([P, NT, HE])
        amax_p = sb("amax_p", [P, HEADS + 1])
        amax = sb("amax", [P, HEADS + 1])
        last_tok = sb("last_tok", [P, ROW])
        src_idx = sb("src_idx", [P, 2, SUB], I32)
        dst_idx = sb("dst_idx", [P, 2, SUB], I32)
        src_got = late([P, 2, SUB, ROW])
        dst_got = late([P, 2, SUB, HEADS])
        lg = late([P, 4, SUB, HEADS])
        ex = late([P, SUB, HEADS])
        val = arena[:, NT * NE * C + NT * VAL:NT * NE * C + (NT + SUB) * VAL].rearrange("p (c v) -> p c v", v=VAL)
        hi_hot = late([P, SUB, NT])
        lo_hot = scratch[:, 0:SUB * P].rearrange("p (c l) -> p c l", c=SUB)
        NR = 4
        spread = scratch[:, SUB * P:SUB * P + NR * NT * VAL].rearrange("p (r i v) -> p r i v", r=NR, i=NT)
        hid = scratch[:, 4608:4608 + 2048].rearrange("p (f t) -> p f t", f=4)
        sums = late([P, NT, VAL])
        dn = late([P, 6, NT, HEADS])
        score = late([P, NT, NE])
        gate = late([P, NT, NE])
        cmp = scratch[:, 6656:6912].rearrange("p (n i) -> p n i", n=8)
        general_i = sb("general_i", [P, 1], I32)
        GC = 8
        g_edge = sb("g_edge", [P, 2, GC], I32)
        g_int = sb("g_int", [P, 2, GC], I32)
        g_lohi = sb("g_lohi", [P, 2, GC])

        act_gate = sb("act_gate", [P, 4])
        off_sb = scratch[:, 0:NT * NOFF].rearrange("p (t c) -> p t c", c=NOFF)
        TK = NT * K
        OROWS = 8
        NCH = H // OROWS
        col_sums = scratch[:, NSC - 2 * OROWS * W - NOFF:NSC - NOFF].rearrange("p (u f) -> p u f", u=2)
        add_taps = scratch[:, NSC - NOFF:NSC]
        (py, px, cy, cx, hy0, hy1, hx0, hx1, mask) = (
            scratch[:, NT * NOFF + n * TK:NT * NOFF + (n + 1) * TK].rearrange("p (t k) -> p t k", k=K) for n in range(9))
        (cy_i, cx_i, by_i, bx_i, bt_i) = (
            scratch[:, NT * NOFF + (9 + n) * TK:NT * NOFF + (10 + n) * TK].bitcast(I32).rearrange("p (t k) -> p t k", k=K)
            for n in range(5))
        bigf = arena[:, NT * NE * C:NT * NE * C + NT * VAL]
        big = bigf[:, :].rearrange("p (i h f) -> p i h f", h=HEADS, f=NE + 1)
        N_ENDS = sum((FRONT > shift) + (shift > 0) for shift in SHIFTS)
        POOL_CONST = 12
        HID_CREDIT = 2
        SLOTS = 6
        LOOP_STEPS = 25
        PAIR_STEPS = 6

        banks = [ctx.enter_context(nc.psum_tensor(f"bank{n}", [P, 512], F32)) for n in range(8)]

        x_in = [sem(f"x_in{b}") for b in range(B)]
        w_in, offw_in = sem("w_in"), sem("offw_in")
        ident_ready, ring_ready, pad_ready, add_ready = (sem(n) for n in ("ident_ready", "ring_ready", "pad_ready",
                                                                          "add_ready"))
        cols_done, cols_copied = sem("cols_done"), sem("cols_copied")
        e_in = sem("e_in")
        pool_step = sem("pool_step")
        x_turned, x_copied = sem("x_turned"), sem("x_copied")
        var_ready, root_done = sem("var_ready"), sem("root_done")
        zeros_ready, ends_out = sem("zeros_ready"), sem("ends_out")
        gate_done = sem("gate_done")
        general_known = sem("general_known")
        g_rows_in = [[sem(f"general_{n}_in{u}") for n in ("src", "dst")] for u in range(2)]
        (g_step, g_free, g_edges_in, g_idx, g_lg, g_ex, g_spread, g_used, g_sums, g_gate) = (
            sem("general_" + n) for n in ("step", "free", "edges_in", "idx", "lg", "ex", "spread", "used", "sums",
                                          "gate"))
        normed, n_turned, n_copied = sem("normed"), sem("n_turned"), sem("n_copied")
        cells_out = [sem(f"cells_out{b}") for b in range(B)]
        off_done, off_read, mask_done = sem("off_done"), sem("off_read"), sem("mask_done")
        dve = sem("dve")
        act = sem("act")
        idx_ready = sem("idx_ready")
        cells_in = [sem(f"cells_in{s}") for s in range(6)]
        scaled_a, scaled_v, w_ready, turned, samp_ready, conv_done = (
            sem(n) for n in ("scaled_a", "scaled_v", "w_ready", "turned", "samp_ready", "conv_done"))
        hot_ready, hist_done = sem("hot_ready"), sem("hist_done")
        hist_copied, folded = sem("hist_copied"), sem("folded")
        t_normed, t_turned, t_copied = sem("t_normed"), sem("t_turned"), sem("t_copied")
        proj_done, rows_ready, rows_out = sem("proj_done"), sem("rows_ready"), sem("rows_out")
        amax_ready, amax_done, last_done = sem("amax_ready"), sem("amax_done"), sem("last_done")
        pair_idx_ready = sem("pair_idx_ready")
        pair_in = [sem(f"pair_in{u}") for u in range(2)]
        pair_lg, pair_ex = sem("pair_lg"), sem("pair_ex")
        spread_ready, spread_used = sem("spread_ready"), sem("spread_used")
        up_done, hid_ready, down_done, y_ready = sem("up_done"), sem("hid_ready"), sem("down_done"), sem("y_ready")
        sums_done = sem("sums_done")
        dn_ready, dn_exp = sem("dn_ready"), sem("dn_exp")
        sc_ready, sc_exp = sem("sc_ready"), sem("sc_exp")
        res_ready, res_turned, res_copied, res_out = (sem(n) for n in ("res_ready", "res_turned", "res_copied", "res_out"))

        block = ctx.enter_context(nc.Block())

        PARAMS = [(offb_sb[:, :], offb.partition_broadcast(P)), (dcnw_sb[:, :, :], dcnw), (wgat_sb[:, :], wgat),
                  (w1_sb[:, :, :], w1.rearrange("e d f -> d e f")),
                  (w2_sb[:, :, :, :], w2.rearrange("e (f p) d -> p e f d", p=P)),
                  (b1_sb[:, :, :], b1),
                  (b2_sb[:, :, :], b2.partition_broadcast(P))]
        PARAMS += [(small[:, n, :], v.partition_broadcast(P)) for n, v in enumerate(
            (att_s.rearrange("h e -> (h e)"), att_d.rearrange("h e -> (h e)"), b_gat, ln_g, ln_b))]

        @block.sync
        def _(sp):
            for b in range(B):
                sp.dma_start(chan[:, b * HW:(b + 1) * HW], x[b].rearrange("c h w -> c (h w)")).then_inc(x_in[b], 16)
            sp.wait_ge(pad_ready, 1)
            sp.dma_start(offw_sb[:, :, 0:NOFF], offw).then_inc(offw_in, 16)
            for dst, src in PARAMS:
                sp.dma_start(dst, src).then_inc(w_in, 16)
            sp.wait_ge(zeros_ready, 1)
            for c, shift in enumerate(SHIFTS):
                for r0, r1 in ((0, FRONT - shift), (FRONT + M - shift, FRONT + M)):
                    if r1 > r0:
                        sp.dma_start(cells[r0:r1, c * C:(c + 1) * C], zero_f[0:r1 - r0, 0:C]).then_inc(ends_out, 16)
            for b in range(B):
                sp.wait_ge(normed, b + 1)
                for c, shift in enumerate(SHIFTS):
                    r0 = FRONT + b * HW - shift
                    sp.dma_start(cells[r0:r0 + HW, c * C:(c + 1) * C].rearrange("(i p) c -> p i c", p=P),
                                 n_tok[:, b * TB:(b + 1) * TB, :]).then_inc(cells_out[b], 16)
            for s in range(2):
                sp.dma_start(edge_i[:, s, :], edges[s].rearrange("(p e) -> p e", p=P)).then_inc(e_in, 16)
            sp.wait_ge(rows_ready, 1)
            sp.dma_start(src_rows[:, :].rearrange("(i p) c -> p i c", p=P), trow[:, :, :]).then_inc(rows_out, 16)
            sp.dma_start(dst_rows[:, :].rearrange("(i p) c -> p i c", p=P), a_dst[:, :, :]).then_inc(rows_out, 16)
            sp.wait_ge(general_known, 1)
            general = sp.value_load(general_i[0:1, 0:1], min_val=0, max_val=1)
            with sp.If(general == 1):
                with sp.Fori(0, EC // GC) as it:
                    sp.wait_ge(g_free, it + 1)
                    for s in range(2):
                        sp.dma_start(g_edge[:, s, :], edges[s].rearrange("(p e) -> p e", p=P)[:, bass.ds(it * GC, GC)])\
                            .then_inc(g_edges_in, 16)
            for g in range(NT // 4):
                sp.wait_ge(res_copied, g + 1)
                b, h = divmod(g, TB // 4)
                sp.dma_start(out[b].rearrange("c h w -> c (h w)")[:, h * 512:(h + 1) * 512],
                             chan[:, g * 512:(g + 1) * 512]).then_inc(res_out, 16)
            sp.wait_ge(res_out, 16 * (NT // 4))

        @block.gpsimd
        def _(pool):
            st = Steps(pool_step)
            st.add(nc.gpsimd.memset(ident[:, :], 0.0))
            pool.wait_ge(pool_step, st.now())
            nc.gpsimd.affine_select(out=ident[:, :], in_=ident[:, :], compare_op=ALU.not_equal, fill=1.0,
                                    base=0, pattern=[[-1, P]], channel_multiplier=1).then_inc(ident_ready, 1)
            nc.gpsimd.memset(ringed[:, :, ::PH - 1, :], 0.0)
            nc.gpsimd.memset(ringed[:, :, 1:PH - 1, ::PW - 1], 0.0).then_inc(ring_ready, 1)
            st.add(nc.gpsimd.memset(last_row[:, :], 1.0))
            st.add(nc.gpsimd.memset(fold[:, :, :], 0.0))
            nc.gpsimd.memset(pool_gate[:, 0:4], 0.0).then_inc(gate_done, 1)
            nc.gpsimd.memset(pool_gate[:, 4:5], 0.0).then_inc(turned, SLOTS)
            pool.wait_ge(pool_step, st.now())
            st.add(nc.gpsimd.affine_select(out=last_row[:, :], in_=last_row[:, :], compare_op=ALU.is_ge, fill=0.0,
                                           base=-(P - 1), pattern=[[0, P]], channel_multiplier=1))
            for h in range(2):
                st.add(nc.gpsimd.affine_select(out=fold[:, h, :], in_=fold[:, h, :], compare_op=ALU.not_equal,
                                               fill=1.0, base=h * LO, pattern=[[-1, P]], channel_multiplier=1))
            st.add(nc.gpsimd.iota(iota_i[:, :], [[1, P]], base=0, channel_multiplier=0))
            st.add(nc.gpsimd.iota(part_i[:, 0:1], [[0, 1]], base=0, channel_multiplier=1))
            st.add(nc.gpsimd.iota(by_i, [[0, B], [P // W, TB], [1, 3], [0, 3]], base=-1, channel_multiplier=0))
            st.add(nc.gpsimd.iota(bx_i, [[0, NT], [0, 3], [1, 3]], base=-1, channel_multiplier=0))
            st.add(nc.gpsimd.iota(bt_i, [[HW, B], [0, TB], [0, K]], base=FRONT, channel_multiplier=0))
            st.add(nc.gpsimd.iota(lanes[:, :, :], [[1, LO], [0, 64]], base=0, channel_multiplier=0,
                                  allow_small_or_imprecise_dtypes=True))
            assert st.n == POOL_CONST, st.n

            for b in range(B):
                pool.wait_ge(cells_out[b], 64)
            pool.wait_ge(ends_out, 16 * N_ENDS)
            with pool.Fori(0, NT // 2) as it:
                for u in range(2):
                    for g in range(3):
                        n = 6 * it + 3 * u + g
                        pool.wait_ge(idx_ready, n + 1)
                        pool.wait_ge(turned, n + 1)
                        pool.wait_ge(gate_done, n + 1)
                        nc.gpsimd.tensor_tensor(pool_gate[:, 0:1], ident[:, 0:1], ident[:, 1:2], ALU.add)\
                            .then_inc(gate_done, 1)
                        for k in range(3 * g, 3 * g + 3):
                            nc.gpsimd.indirect_dma_start(
                                cell[:, u, k, :, :].rearrange("p c f -> p (c f)"), None, cells[:, :],
                                bass.IndirectOffsetOnAxis(ap=idx_slot[:, u, k:k + 1], axis=0))\
                                .then_inc(cells_in[3 * u + g], 16)

            pool.wait_ge(amax_ready, 1)
            nc.gpsimd.partition_all_reduce(amax[:, :], amax_p[:, :], P, RMAX).then_inc(amax_done, 1)
            pool.wait_ge(rows_out, 32)
            with pool.Fori(0, NSUB // 2) as it:
                for u in range(2):
                    pool.wait_ge(pair_idx_ready, 2 * it + u + 1)
                    pool.wait_ge(gate_done, 2 * it + u + 1 + 3 * NT)
                    nc.gpsimd.tensor_tensor(pool_gate[:, 2 + u:3 + u], ident[:, 0:1], ident[:, 1:2], ALU.add).then_inc(gate_done, 1)
                    for c in range(SUB):
                        nc.gpsimd.indirect_dma_start(
                            src_got[:, u, c, :], None, src_rows[:, :],
                            bass.IndirectOffsetOnAxis(ap=src_idx[:, u, c:c + 1], axis=0)).then_inc(pair_in[u], 16)
                        nc.gpsimd.indirect_dma_start(
                            dst_got[:, u, c, :], None, dst_rows[:, :],
                            bass.IndirectOffsetOnAxis(ap=dst_idx[:, u, c:c + 1], axis=0)).then_inc(pair_in[u], 16)

            pool.wait_ge(general_known, 1)
            general = pool.value_load(general_i[0:1, 0:1], min_val=0, max_val=1)
            with pool.If(general == 1):
                nc.gpsimd.memset(pool_gate[:, 0:2], 0.0).then_inc(g_gate, 1)
                with pool.Fori(0, EC // GC // 2) as it:
                  for u in range(2):
                    pool.wait_ge(g_idx, 2 * it + u + 1)
                    pool.wait_ge(g_gate, 2 * it + u + 1)
                    nc.gpsimd.tensor_tensor(pool_gate[:, 0:1], ident[:, 0:1], ident[:, 1:2], ALU.add).then_inc(g_gate, 1)
                    for c in range(GC):
                        nc.gpsimd.indirect_dma_start(
                            src_got[:, 0, c, :], None, src_rows[:, :],
                            bass.IndirectOffsetOnAxis(ap=src_idx[:, 0, c:c + 1], axis=0)).then_inc(g_rows_in[u][0], 16)
                        nc.gpsimd.indirect_dma_start(
                            dst_got[:, 0, c, :], None, dst_rows[:, :],
                            bass.IndirectOffsetOnAxis(ap=dst_idx[:, 0, c:c + 1], axis=0)).then_inc(g_rows_in[u][1], 16)

        @block.tensor
        def _(pe):
            pe.wait_ge(ident_ready, 1)
            for b in range(B):
                pe.wait_ge(x_in[b], 16)
                for h in range(2):
                    g = 2 * b + h
                    if g >= 2:
                        pe.wait_ge(x_copied, g - 1)
                    for q in range(4):
                        t = 4 * g + q
                        mm = nc.tensor.transpose(banks[g % 2][:, q * P:(q + 1) * P], chan[:, t * P:(t + 1) * P], ident[:, :])
                    mm.then_inc(x_turned, 1)

            def add_columns(m):
                pe.wait_ge(cols_copied, m + 1)
                b, j = divmod(m, NCH)
                for q in range(2):
                    o = (2 * j + q) * 32
                    mm = nc.tensor.matmul(banks[4 + b][:, o:o + NOFF], col_sums[0:96, m % 2, q * P:(q + 1) * P],
                                          add_taps[0:96, :], start=True, stop=True)
                mm.then_inc(off_done, 1)

            pe.wait_ge(offw_in, 16)
            pe.wait_ge(ring_ready, 1)
            pe.wait_ge(add_ready, 1)
            for b in range(B):
                pe.wait_ge(normed, b + 1)
                for h in range(2):
                    g = 2 * b + h
                    if g >= 2:
                        pe.wait_ge(n_copied, g - 1)
                    for q in range(4):
                        mm = nc.tensor.transpose(banks[2 + g % 2][:, q * P:(q + 1) * P], n_tok[:, 4 * g + q, :], ident[:, :])
                    mm.then_inc(n_turned, 1)
                pe.wait_ge(n_copied, 2 * b + 2)
                for j in range(NCH):
                    m = b * NCH + j
                    if m == 0:
                        pe.wait_ge(x_copied, NT // 4)
                    if m >= 2:
                        pe.wait_ge(cols_copied, m - 1)
                    for ki in range(3):
                        at = (b * PH + j * OROWS + ki) * PW
                        mm = nc.tensor.matmul(banks[m % 2][0:96, 0:OROWS * PW],
                                              offw_sb[:, 3 * ki:3 * ki + 3, :].rearrange("p k c -> p (k c)"),
                                              padded[:, at:at + OROWS * PW], start=(ki == 0), stop=(ki == 2))
                    mm.then_inc(cols_done, 1)
                    if m >= 1:
                        add_columns(m - 1)
            add_columns(B * NCH - 1)

            pe.wait_ge(w_in, 16 * len(PARAMS))
            pe.wait_ge(off_read, B)
            hist = banks[7][0:LO, 0:LO]
            nc.tensor.matmul(hist, zero_bf[:, :], zero_bf[:, :], start=True, stop=False).then_inc(hist_done, 1)
            nc.tensor.matmul(banks[4][:, 0:C], zero_f[:, 0:P], zero_f[:, 0:C], start=True, stop=False)

            def turn(n, u, g):
                pe.wait_ge(scaled_a, n + 1)
                pe.wait_ge(scaled_v, n + 1)
                for j in range(3):
                    for c in range(4):
                        mm = nc.tensor.matmul(banks[g][:, j * P:(j + 1) * P], cell[:, u, 3 * g + j, c, :], ident[:, :],
                                              is_transpose=True, start=(c == 0), stop=(c == 3))
                mm.then_inc(turned, 1)

            def weigh(n, u, g):
                pe.wait_ge(samp_ready, n + 1)
                for k in range(3 * g, 3 * g + 3):
                    mm = nc.tensor.matmul(banks[3 + u][:, 0:C], samp[:, u, k, :], dcnw_sb[:, k, :],
                                          start=(k == 0), stop=(k == K - 1))
                if g == 2:
                    mm.then_inc(conv_done, 1)

            with pe.Fori(0, NT // 2) as it:
                for u in range(2):
                    n = 6 * it + 3 * u
                    turn(n, u, 0)
                    weigh(n, 1 - u, 2)
                    turn(n + 1, u, 1)
                    weigh(n + 1, u, 0)
                    turn(n + 2, u, 2)
                    weigh(n + 2, u, 1)
                pe.wait_ge(hot_ready, it + 1)
                for c in range(CAP):
                    mm = nc.tensor.matmul(hist, onehots[:, 0, :, c], onehots[:, 1, :, c], start=False, stop=False)
                mm.then_inc(hist_done, 1)
            weigh(3 * NT, 1, 2)
            nc.tensor.matmul(hist, zero_bf[:, :], zero_bf[:, :], start=False, stop=True).then_inc(hist_done, 1)

            proj = banks[2]
            for g in range(NT // 4 + 1):
                if g < NT // 4:
                    pe.wait_ge(t_normed, g + 1)
                    if g >= 2:
                        pe.wait_ge(t_copied, g - 1)
                    for q in range(4):
                        mm = nc.tensor.transpose(banks[g % 2][:, q * P:(q + 1) * P], n_tok[:, 4 * g + q, :], ident[:, :])
                    mm.then_inc(t_turned, 1)
                if g >= 1:
                    pe.wait_ge(t_copied, g)
                    for t in range(4 * g - 4, 4 * g):
                        mm = nc.tensor.matmul(proj[:, t * HE:(t + 1) * HE], chan[:, t * P:(t + 1) * P], wgat_sb[:, :],
                                              start=True, stop=True)
            mm.then_inc(proj_done, 1)
            pe.wait_ge(hist_copied, 1)
            hv = hist_sb[:, :].rearrange("l (i h) -> l h i", h=2)
            for h in range(2):
                mm = nc.tensor.matmul(banks[3][:, 0:NT], fold[:, h, :], hv[:, h, :], start=(h == 0), stop=(h == 1))
            mm.then_inc(folded, 1)
            pe.wait_ge(rows_ready, 1)
            nc.tensor.matmul(banks[6][:, 0:ROW], last_row[:, :], trow[:, NT - 1, :], start=True, stop=True)\
                .then_inc(last_done, 1)

            half = NT // 2 * VAL
            sum_bank = [banks[0][:, 0:half], banks[1][:, 0:half]]
            for h in range(2):
                pe.wait_ge(t_copied, NT // 4)
                mm = nc.tensor.matmul(sum_bank[h], zero_f[:, 0:P], zero_f[:, 0:half], start=True, stop=False)
            mm.then_inc(spread_used, NR)
            with pe.Fori(0, NSUB // 2) as it:
                for u in range(2):
                    sub = 2 * it + u
                    col = 0
                    for e in range(NE):
                        chunk = chan[:, bass.ds(sub * 512, 512)]
                        for f in range(NF):
                            n = e * NF + f
                            pe.wait_ge(hid_ready, NE * NF * sub + n + 1)
                            nc.tensor.matmul(banks[4 + n % 2][:, :], w1_sb[:, e, f * P:(f + 1) * P], chunk,
                                             start=True, stop=True).then_inc(up_done, 1)
                        for _ in range(4 if e == 0 else 3):
                            pe.wait_ge(spread_ready, SUB * sub + col + 1)
                            for h in range(2):
                                mm = nc.tensor.matmul(sum_bank[h], lo_hot[:, col, :],
                                                      spread[:, col % NR, h * NT // 2:(h + 1) * NT // 2, :],
                                                      start=False, stop=False)
                            mm.then_inc(spread_used, 1)
                            col += 1
                        pe.wait_ge(hid_ready, NE * NF * sub + (e + 1) * NF + HID_CREDIT)
                        pe.wait_ge(y_ready, NE * sub + e + 1)
                        for q in range(4):
                            for f in range(NF):
                                mm = nc.tensor.matmul(banks[6 + e % 2][:, q * C:(q + 1) * C],
                                                      hid[:, (e % 2) * NF + f, q * P:(q + 1) * P], w2_sb[:, e, f, :],
                                                      start=(f == 0), stop=(f == NF - 1))
                        mm.then_inc(down_done, 1)
            for h in range(2):
                mm = nc.tensor.matmul(sum_bank[h], zero_f[:, 0:P], zero_f[:, 0:half], start=False, stop=True)
            mm.then_inc(sums_done, 1)

            pe.wait_ge(general_known, 1)
            general = pe.value_load(general_i[0:1, 0:1], min_val=0, max_val=1)
            with pe.If(general == 1):
                for h in range(2):
                    mm = nc.tensor.matmul(sum_bank[h], zero_f[:, 0:P], zero_f[:, 0:half], start=True, stop=False)
                mm.then_inc(g_used, NR)
                with pe.Fori(0, EC // GC) as it:
                    for col in range(GC):
                        pe.wait_ge(g_spread, GC * it + col + 1)
                        for h in range(2):
                            mm = nc.tensor.matmul(sum_bank[h], lo_hot[:, col, :],
                                                  spread[:, col % NR, h * NT // 2:(h + 1) * NT // 2, :],
                                                  start=False, stop=False)
                        mm.then_inc(g_used, 1)
                for h in range(2):
                    mm = nc.tensor.matmul(sum_bank[h], zero_f[:, 0:P], zero_f[:, 0:half], start=False, stop=True)
                mm.then_inc(g_sums, 1)

            for g in range(NT // 4):
                pe.wait_ge(res_ready, g + 1)
                if g >= 2:
                    pe.wait_ge(res_copied, g - 1)
                if g < 2:
                    pe.wait_ge(down_done, NE * NSUB)
                for q in range(4):
                    mm = nc.tensor.transpose(banks[4 + g % 2][:, q * P:(q + 1) * P], x_tok[:, 4 * g + q, :], ident[:, :])
                mm.then_inc(res_turned, 1)

        @block.scalar
        def _(ac):
            def root(v, n):
                ac.wait_ge(var_ready, n)
                nc.scalar.sqrt(v, v).then_inc(root_done, 1)

            for g in range(NT // 4):
                ac.wait_ge(x_turned, g + 1)
                nc.scalar.copy(x_tok[:, 4 * g:4 * g + 4, :], banks[g % 2][:, :]).then_inc(x_copied, 1)
                if g % 2 == 0 and g >= 2:
                    b = g // 2 - 1
                    root(rstd[:, b * TB:(b + 1) * TB], b + 1)
            root(rstd[:, (B - 1) * TB:B * TB], B)

            def sigmoid(b):
                ac.wait_ge(off_read, b + 1)
                nc.scalar.activation(mask[:, b * TB:(b + 1) * TB, :], off_sb[:, b * TB:(b + 1) * TB, 2 * K:3 * K],
                                     ACT.Sigmoid).then_inc(mask_done, 1)

            for b in range(B):
                for h in range(2):
                    g = 2 * b + h
                    ac.wait_ge(n_turned, g + 1)
                    nc.scalar.copy(ringed[:, b, 1 + 16 * h:17 + 16 * h, 1:W + 1],
                                   banks[2 + g % 2][:, :].rearrange("p (y x) -> p y x", x=W)).then_inc(n_copied, 1)
                for j in range(NCH):
                    m = b * NCH + j
                    ac.wait_ge(cols_done, m + 1)
                    if m >= 2:
                        ac.wait_ge(off_done, m - 1)
                    for kj in range(3):
                        rows = slice(32 * kj, 32 * kj + 32)
                        ins = nc.scalar.copy(col_sums[rows, m % 2, :].rearrange("p (y x) -> p y x", x=W),
                                             banks[m % 2][rows, 0:OROWS * PW].rearrange("p (y x) -> p y x", x=PW)
                                             [:, :, kj:kj + W])
                    ins.then_inc(cols_copied, 1)
                if b >= 1:
                    sigmoid(b - 1)
            sigmoid(B - 1)

            def scale(it, u, g):
                ac.wait_ge(cells_in[3 * u + g], 48 * (it + 1))
                if g == 0:
                    ac.wait_ge(w_ready, 2 * it + u + 1)
                for k in range(3 * g, 3 * g + 3):
                    for c in range(3):
                        ins = nc.scalar.activation(cell[:, u, k, c, :], cell[:, u, k, c, :], ACT.Copy,
                                                   scale=w_slot[:, u, c, k:k + 1])
                ins.then_inc(scaled_a, 1)

            def evict(n, u, g):
                ac.wait_ge(turned, n + SLOTS)
                nc.scalar.copy(samp[:, u, 3 * g:3 * g + 3, :], banks[g][:, 0:3 * P]).then_inc(samp_ready, 1)

            with ac.Fori(0, NT // 2) as it:
                for u in range(2):
                    n = 6 * it + 3 * u
                    scale(it, u, 0)
                    evict(n, 1 - u, 2)
                    scale(it, u, 1)
                    evict(n + 1, u, 0)
                    scale(it, u, 2)
                    evict(n + 2, u, 1)
            evict(3 * NT, 1, 2)

            root(rstd[:, :], B + 1)
            for g in range(NT // 4):
                ac.wait_ge(t_turned, g + 1)
                nc.scalar.copy(chan[:, g * 512:(g + 1) * 512], banks[g % 2][:, :]).then_inc(t_copied, 1)

            ac.wait_ge(off_read, B)
            nc.scalar.copy(act_gate[:, 0:1], ident[:, 0:1]).then_inc(hid_ready, HID_CREDIT)
            with ac.Fori(0, NSUB // 2) as it:
                for u in range(2):
                    sub = 2 * it + u
                    ac.wait_ge(pair_lg, sub + 1)
                    nc.scalar.activation(ex[:, :, :], lg[:, 3, :, :], ACT.Exp).then_inc(pair_ex, 1)
                    for e in range(NE):
                        for f in range(NF):
                            n = e * NF + f
                            ac.wait_ge(up_done, NE * NF * sub + n + 1)
                            nc.scalar.activation(hid[:, (e % 2) * NF + f, :], banks[4 + n % 2][:, :], ACT.Gelu,
                                                 bias=b1_sb[:, e, f:f + 1]).then_inc(hid_ready, 1)
            ac.wait_ge(general_known, 1)
            general = ac.value_load(general_i[0:1, 0:1], min_val=0, max_val=1)
            with ac.If(general == 1):
                with ac.Fori(0, EC // GC) as it:
                    ac.wait_ge(g_lg, it + 1)
                    nc.scalar.activation(ex[:, 0:GC, :], lg[:, 3, 0:GC, :], ACT.Exp).then_inc(g_ex, 1)
            ac.wait_ge(dn_ready, 1)
            nc.scalar.activation(dn[:, 0:2, :, :], dn[:, 0:2, :, :], ACT.Exp).then_inc(dn_exp, 1)
            root(cmp[:, 1, :], B + 2)
            ac.wait_ge(sc_ready, 1)
            nc.scalar.activation(gate[:, :, :], gate[:, :, :], ACT.Exp).then_inc(sc_exp, 1)
            for g in range(NT // 4):
                ac.wait_ge(res_turned, g + 1)
                nc.scalar.copy(chan[:, g * 512:(g + 1) * 512], banks[4 + g % 2][:, :]).then_inc(res_copied, 1)

        @block.vector
        def _(ve):
            st = Steps(dve)
            V = nc.vector

            def done(ins):
                st.add(ins)
                ve.wait_ge(dve, st.now())

            roots = [0]

            def moments(i0, n, eps):
                s = stats[:, i0:i0 + n, :]
                a, d, v = (st_a[:, j, i0:i0 + n] for j in range(3))
                V.tensor_tensor(a, s[:, :, 1], s[:, :, 4], ALU.add)
                V.tensor_tensor(d, s[:, :, 1], s[:, :, 4], ALU.subtract)
                done(V.tensor_tensor(v, s[:, :, 2], s[:, :, 5], ALU.add))
                V.tensor_scalar(mean[:, i0:i0 + n], a, 0.5, None, ALU.mult)
                done(V.tensor_tensor(d, d, d, ALU.mult))
                done(V.scalar_tensor_tensor(out=v, in0=d, scalar=C / 4.0, in1=v, op0=ALU.mult, op1=ALU.add))
                V.tensor_scalar(rstd[:, i0:i0 + n], v, 1.0 / C, eps, ALU.mult, ALU.add).then_inc(var_ready, 1)
                roots[0] += 1
                ve.wait_ge(root_done, roots[0])
                done(V.reciprocal(rstd[:, i0:i0 + n], rstd[:, i0:i0 + n]))

            V.memset(offw_sb[:, :, NOFF:], 0.0).then_inc(pad_ready, 1)
            V.memset(zero_bf[:, :], 0.0)
            V.memset(zero_f[:, :], 0.0).then_inc(zeros_ready, 1)
            V.memset(lost[:, :], 0.0)
            V.memset(x_all[:, 0, :], 0.0)
            V.memset(pk_src[:, :], 0.0)
            V.memset(pk_dst[:, :], 0.0)
            V.memset(idx_f[:, NT:NT + 2, :], 0.0)
            V.memset(corner_w[:, NT:NT + 2, :, :], 0.0)
            done(V.memset(dve_gate[:, :], 0.0))

            ve.wait_ge(ident_ready, 1)
            done(V.tensor_tensor(add_taps, ident[:, 0:NOFF], ident[:, 32:32 + NOFF], ALU.add))
            V.tensor_tensor(add_taps, add_taps, ident[:, 64:64 + NOFF], ALU.add).then_inc(add_ready, 1)

            for b in range(B):
                for h in range(2):
                    ve.wait_ge(x_copied, 2 * b + h + 1)
                    for q in range(4):
                        t = b * TB + 4 * h + q
                        ins = V.bn_stats(stats[:, t, :], x_tok[:, t, :])
                done(ins)
                moments(b * TB, TB, EPS_C)
                for t in range(b * TB, (b + 1) * TB):
                    ins = V.tensor_scalar(n_tok[:, t, :], x_tok[:, t, :], mean[:, t:t + 1], rstd[:, t:t + 1],
                                          ALU.subtract, ALU.mult)
                ins.then_inc(normed, 1)

            ve.wait_ge(pool_step, POOL_CONST)
            V.tensor_copy(iota_f[:, :], iota_i[:, :])
            V.tensor_scalar(part_i[:, 1:2], part_i[:, 0:1], 5, None, ALU.arith_shift_right)
            done(V.tensor_scalar(part_i[:, 2:3], part_i[:, 0:1], W - 1, None, ALU.bitwise_and))
            done(V.tensor_copy(part_f[:, 1:3], part_i[:, 1:3]))

            def sampling(b):
                i = slice(b * TB, (b + 1) * TB)
                ve.wait_ge(off_done, NCH * (b + 1))
                o = banks[4 + b][:, 0:TB * 32].rearrange("p (t c) -> p t c", c=32)[:, :, 0:NOFF]
                st.add(V.tensor_tensor(off_sb[:, i, :], o, offb_sb[:, :].unsqueeze(1).to_broadcast([P, TB, NOFF]), ALU.add))
                V.tensor_scalar(py[:, i, :], by_i[:, i, :], part_f[:, 1:2], None, ALU.add)
                done(V.tensor_scalar(px[:, i, :], bx_i[:, i, :], part_f[:, 2:3], None, ALU.add))
                dyx = off_sb[:, i, 0:2 * K].rearrange("p t (k s) -> p t k s", s=2)
                V.tensor_tensor(py[:, i, :], py[:, i, :], dyx[:, :, :, 0], ALU.add).then_inc(off_read, 1)
                done(V.tensor_tensor(px[:, i, :], px[:, i, :], dyx[:, :, :, 1], ALU.add))
                for q, c in ((py, cy), (px, cx)):
                    ins = V.tensor_scalar(c[:, i, :], q[:, i, :], -0.5, 0.0, ALU.add, ALU.max)
                done(ins)
                V.tensor_scalar(cy_i[:, i, :], cy[:, i, :], float(H - 2), None, ALU.min)
                done(V.tensor_scalar(cx_i[:, i, :], cx[:, i, :], float(W - 2), None, ALU.min))
                V.tensor_copy(cy[:, i, :], cy_i[:, i, :])
                done(V.tensor_copy(cx[:, i, :], cx_i[:, i, :]))
                V.tensor_tensor(py[:, i, :], py[:, i, :], cy[:, i, :], ALU.subtract)
                V.tensor_tensor(px[:, i, :], px[:, i, :], cx[:, i, :], ALU.subtract)
                done(V.scalar_tensor_tensor(out=cy[:, i, :], in0=cy[:, i, :], scalar=float(W), in1=cx[:, i, :],
                                            op0=ALU.mult, op1=ALU.add))
                V.tensor_tensor(idx_f[:, i, :], cy[:, i, :], bt_i[:, i, :], ALU.add)
                for r, h0, h1 in ((py, hy0, hy1), (px, hx0, hx1)):
                    V.tensor_scalar(h0[:, i, :], r[:, i, :], -1.0, 1.0, ALU.mult, ALU.add)
                    ins = V.tensor_scalar(h1[:, i, :], r[:, i, :], -1.0, 2.0, ALU.mult, ALU.add)
                done(ins)
                for r, h0, h1 in ((py, hy0, hy1), (px, hx0, hx1)):
                    V.scalar_tensor_tensor(out=h0[:, i, :], in0=r[:, i, :], scalar=1.0, in1=h0[:, i, :],
                                           op0=ALU.add, op1=ALU.min)
                    ins = V.scalar_tensor_tensor(out=h1[:, i, :], in0=r[:, i, :], scalar=1.0, in1=h1[:, i, :],
                                                 op0=ALU.mult, op1=ALU.min)
                done(ins)
                ve.wait_ge(mask_done, b + 1)
                for h in (hx0, hx1):
                    V.tensor_scalar(h[:, i, :], h[:, i, :], 0.0, None, ALU.max)
                for h in (hy0, hy1):
                    ins = V.scalar_tensor_tensor(out=h[:, i, :], in0=h[:, i, :], scalar=0.0, in1=mask[:, i, :],
                                                 op0=ALU.max, op1=ALU.mult)
                done(ins)
                for c, (hy, hx) in enumerate(((hy0, hx0), (hy0, hx1), (hy1, hx0), (hy1, hx1))):
                    ins = V.tensor_tensor(corner_w[:, i, c, :], hy[:, i, :], hx[:, i, :], ALU.mult)
                done(ins)

            ve.wait_ge(w_in, 16 * len(PARAMS))
            for b in range(B):
                sampling(b)
                if b == 0:
                    for u in range(2):
                        V.tensor_copy(w_slot[:, u, :, :], corner_w[:, u, :, :]).then_inc(w_ready, 1)
                        V.tensor_copy(idx_slot[:, u, :], idx_f[:, u, :]).then_inc(idx_ready, 3)

            idx_flat = idx_f[:, :, :].rearrange("p t k -> p (t k)")
            w_flat = corner_w[:, :, :, :].rearrange("p t c k -> p (t c k)")
            x_flat = x_all[:, :, :].rearrange("p t c -> p (t c)")
            ve.wait_ge(e_in, 32)
            loop_at = st.now()
            st.base, st.n = None, 0
            STEPS = LOOP_STEPS
            with ve.Fori(0, NT // 2) as it:
                st.base = it * STEPS + loop_at
                gates = [0]

                def step(ins):
                    st.add(ins)
                    ve.wait_ge(dve, st.now())

                def gated(ins_of):
                    V.tensor_scalar(dve_gate[0:1, gates[0]:gates[0] + 1], iota_f[0:1, 0:1], 0.0, None, ALU.add)
                    gates[0] += 1
                    step(ins_of())

                def corner(u, g):
                    ve.wait_ge(cells_in[3 * u + g], 48 * (it + 1))
                    for k in range(3 * g, 3 * g + 3):
                        ins = V.tensor_scalar(cell[:, u, k, 3, :], cell[:, u, k, 3, :], w_slot[:, u, 3, k:k + 1], None, ALU.mult)
                    ins.then_inc(scaled_v, 1)
                    V.tensor_scalar(idx_slot[:, u, 3 * g:3 * g + 3],
                                    idx_flat[:, bass.ds((2 * it + u + 2) * K + 3 * g, 3)],
                                    0.0, None, ALU.add).then_inc(idx_ready, 1)

                def weights(u):
                    ve.wait_ge(scaled_a, 6 * it + 3 * u + 3)
                    ve.wait_ge(scaled_v, 6 * it + 3 * u + 3)
                    V.tensor_scalar(w_slot[:, u, :, :].rearrange("p c k -> p (c k)"),
                                    w_flat[:, bass.ds((2 * it + u + 2) * 4 * K, 4 * K)], 0.0, None, ALU.add)\
                        .then_inc(w_ready, 1)

                def residual(u):
                    ve.wait_ge(conv_done, 2 * it + u + 1)
                    xs = x_flat[:, bass.ds((2 * it + u) * C, C)]
                    st.add(V.tensor_tensor(xs, banks[4 - u][:, 0:C], xs, ALU.add))

                def pick(r):
                    top = kept[:, 8 * r:8 * r + 8]
                    gated(lambda: V.max(top, ka))
                    if r < CAP // 8:
                        gated(lambda: V.match_replace(ka, top, ka, 0.0))

                corner(0, 0)
                e_src = edge_f[:, bass.ds(it * SEG, SEG)]
                e_dst = edge_f[:, bass.ds(it * SEG + EC, SEG)]
                ka, kb = key_a[:, 0, :], key_a[:, 1, :]
                V.tensor_scalar(kb, e_dst, float(M), None, ALU.is_lt)
                step(V.tensor_scalar(ka, e_src, float(M - 1), -float(M), ALU.min, ALU.mult))
                step(V.scalar_tensor_tensor(out=ka, in0=ka, scalar=float(M * (M - 1) + 1), in1=e_dst, op0=ALU.add, op1=ALU.add))
                step(V.tensor_tensor(ka, ka, kb, ALU.mult))
                for r in range(0, 3):
                    pick(r)
                corner(0, 1)
                for r in range(3, 6):
                    pick(r)
                corner(0, 2)
                for r in range(6, CAP // 8 + 1):
                    pick(r)
                V.tensor_tensor(lost[:, 0:1], lost[:, 0:1], kept[:, CAP:CAP + 1], ALU.max)
                V.scalar_tensor_tensor(out=lost[:, 1:2], in0=kept[:, PCAP:PCAP + 1], scalar=float(M) + 0.5,
                                       in1=lost[:, 1:2], op0=ALU.is_gt, op1=ALU.max)
                V.tensor_scalar(pairs1[:, bass.ds(it * PCAP, PCAP)], kept[:, 0:PCAP], 0.0, None, ALU.add)
                step(V.tensor_scalar(kept_i[:, 0, :], kept[:, 0:CAP], -1.0, None, ALU.add))
                weights(0)
                residual(0)
                corner(1, 0)
                V.tensor_scalar(kept_i[:, 1, :], kept_i[:, 0, :], LO - 1, None, ALU.bitwise_and)
                step(V.tensor_scalar(kept_i[:, 2, :], kept_i[:, 0, :], 6, None, ALU.arith_shift_right))
                step(V.tensor_copy(kept_lohi[:, :, :], kept_i[:, 1:3, :]))
                ve.wait_ge(hist_done, it + 1)
                for h in range(2):
                    ins = V.tensor_tensor(onehots[:, h, :, :], lanes[:, :, :],
                                          kept_lohi[:, h, :].unsqueeze(1).to_broadcast([P, LO, CAP]), ALU.is_equal)
                    if h == 1:
                        ins.then_inc(hot_ready, 1)
                    corner(1, 1 + h)
                weights(1)
                residual(1)
                assert st.n == STEPS, st.n
            st.base, st.n = loop_at + STEPS * (NT // 2), 0
            ve.wait_ge(conv_done, NT + 1)
            done(V.tensor_tensor(x_tok[:, NT - 1, :], banks[4][:, 0:C], x_tok[:, NT - 1, :], ALU.add))

            ve.wait_ge(hist_done, NT // 2 + 2)
            V.tensor_copy(hist_sb[:, :], banks[7][0:LO, 0:LO]).then_inc(hist_copied, 1)
            for t in range(NT):
                ins = V.bn_stats(stats[:, t, :], x_tok[:, t, :])
            done(ins)
            moments(0, NT, EPS_T)
            ve.wait_ge(cells_out[B - 1], 64)
            for t in range(NT):
                ins = V.tensor_scalar(n_tok[:, t, :], x_tok[:, t, :], mean[:, t:t + 1], rstd[:, t:t + 1],
                                      ALU.subtract, ALU.mult)
                if t % 4 == 3:
                    ins.then_inc(t_normed, 1)

            for r in range(PC // 8 + 1):
                top = pairs2[:, 8 * r:8 * r + 8]
                if r == 0:
                    V.tensor_scalar(lost[:, 0:1], lost[:, 0:1], lost[:, 1:2], None, ALU.max)
                    hits = key_a[:, 0, 0:NSEG * PCAP]
                    done(V.tensor_scalar(hits, pairs1[:, :], float(M) + 0.5, None, ALU.is_gt))
                    done(V.tensor_tensor(pairs1[:, :], pairs1[:, :], hits, ALU.mult))
                done(V.max(top, pairs1[:, :]))
                if r < PC // 8:
                    done(V.match_replace(pairs1[:, :], top, pairs1[:, :], 0.0))
            V.tensor_tensor(lost[:, 0:1], lost[:, 0:1], pairs2[:, PC:PC + 1], ALU.max)

            keys = pairs2[:, 0:PC]
            V.tensor_scalar(pk_void[:, :], keys, 0.5, 64.0, ALU.is_lt, ALU.mult)
            done(V.tensor_scalar(pk_i[:, 0, :], keys, -1.0, None, ALU.add))
            V.tensor_scalar(pk_i[:, 1, :], pk_i[:, 0, :], 12, None, ALU.arith_shift_right)
            V.tensor_scalar(pk_i[:, 2, :], pk_i[:, 0, :], M - 1, None, ALU.bitwise_and)
            done(V.tensor_scalar(pk_i[:, 3, :], pk_i[:, 0, :], P - 1, None, ALU.bitwise_and))
            V.tensor_scalar(pk_src[:, 0:PC], pk_i[:, 1, :], -1.0, float(M - 1), ALU.mult, ALU.add)
            V.tensor_copy(pk_dst[:, 0:PC], pk_i[:, 2, :])
            V.tensor_copy(pk_lo[:, :], pk_i[:, 3, :])
            done(V.tensor_scalar(pk_i[:, 0, :], pk_i[:, 2, :], 7, None, ALU.arith_shift_right))
            V.tensor_scalar(pk_src[:, 0:PC], pk_src[:, 0:PC], float(M - 1), None, ALU.min)
            done(V.tensor_tensor(pk_hi[:, :], pk_i[:, 0, :], pk_void[:, :], ALU.add))
            for u in range(2):
                V.tensor_copy(src_idx[:, u, :], pk_src[:, u * SUB:(u + 1) * SUB])
                V.tensor_copy(dst_idx[:, u, :], pk_dst[:, u * SUB:(u + 1) * SUB]).then_inc(pair_idx_ready, 1)

            done(V.memset(trow[:, :, :], 1.0))
            h_of = trow[:, :, HEADS:ROW].rearrange("p i (h f) -> p i h f", h=HEADS)[:, :, :, 1:]
            ve.wait_ge(proj_done, 1)
            pv = banks[2][:, :].rearrange("p (i f) -> p i f", f=HE)
            pv4 = banks[2][:, :].rearrange("p (i h e) -> p i h e", h=HEADS, e=NE)
            V.tensor_copy(h_of, pv4)
            for n, dst in ((0, trow[:, :, 0:HEADS]), (1, a_dst[:, :, :])):
                done(V.tensor_tensor(tmp16[:, :, :], pv, small[:, n, :].unsqueeze(1).to_broadcast([P, NT, HE]), ALU.mult))
                ins = V.tensor_reduce(dst, tmp16[:, :, :].rearrange("p i (h e) -> p i h e", e=NE), AX.X, ALU.add)
                done(ins)
            V.tensor_scalar(amax_p[:, HEADS:HEADS + 1], lost[:, 0:1], 1.0 if general_always else 0.0, None, ALU.add)
            V.tensor_reduce(amax_p[:, 0:HEADS], trow[:, :, 0:HEADS].rearrange("p i h -> p h i"), AX.X, ALU.max)\
                .then_inc(amax_ready, 1)
            V.tensor_copy(act_gate[:, 1:2], ident[:, 0:1]).then_inc(rows_ready, 1)

            ve.wait_ge(folded, 1)
            V.tensor_copy(count[:, :], banks[3][:, 0:NT])
            ve.wait_ge(last_done, 1)
            done(V.tensor_copy(last_tok[:, :], banks[6][:, 0:ROW]))

            a_src = trow[:, :, 0:HEADS]
            ve.wait_ge(amax_done, 1)
            V.tensor_scalar(general_i[:, :], amax[:, HEADS:HEADS + 1], 0.5, None, ALU.is_gt).then_inc(general_known, 1)
            V.tensor_tensor(dn[:, 0, :, :], a_src, a_dst[:, :, :], ALU.add)
            V.tensor_tensor(dn[:, 1, :, :], a_dst[:, :, :], last_tok[:, 0:HEADS].unsqueeze(1).to_broadcast([P, NT, HEADS]), ALU.add)
            done(V.tensor_tensor(dn[:, 2, :, :], a_dst[:, :, :], amax[:, 0:HEADS].unsqueeze(1).to_broadcast([P, NT, HEADS]), ALU.add))
            done(V.scalar_tensor_tensor(out=dn[:, 0:3, :, :], in0=dn[:, 0:3, :, :], scalar=0.2, in1=dn[:, 0:3, :, :],
                                        op0=ALU.mult, op1=ALU.max))
            V.tensor_tensor(dn[:, 0, :, :], dn[:, 0, :, :], dn[:, 2, :, :], ALU.subtract)
            V.tensor_tensor(dn[:, 1, :, :], dn[:, 1, :, :], dn[:, 2, :, :], ALU.subtract).then_inc(dn_ready, 1)

            def one_hots(lo, hi, n):
                V.tensor_tensor(lo_hot[:, 0:n, :], iota_f[:, :].unsqueeze(1).to_broadcast([P, n, P]),
                                lo.unsqueeze(2).to_broadcast([P, n, P]), ALU.is_equal)
                V.tensor_tensor(hi_hot[:, 0:n, :], iota_f[:, 0:NT].unsqueeze(1).to_broadcast([P, n, NT]),
                                hi.unsqueeze(2).to_broadcast([P, n, NT]), ALU.is_equal)

            def exponents(step, sg, dg, n):
                V.tensor_tensor(lg[:, 0, 0:n, :], sg[:, :, 0:HEADS], dg, ALU.add)
                step(V.tensor_tensor(lg[:, 1, 0:n, :], dg, amax[:, 0:HEADS].unsqueeze(1).to_broadcast([P, n, HEADS]), ALU.add))
                step(V.scalar_tensor_tensor(out=lg[:, 0:2, 0:n, :], in0=lg[:, 0:2, 0:n, :], scalar=0.2,
                                            in1=lg[:, 0:2, 0:n, :], op0=ALU.mult, op1=ALU.max))
                return V.tensor_tensor(lg[:, 3, 0:n, :], lg[:, 0, 0:n, :], lg[:, 1, 0:n, :], ALU.subtract)

            def messages(sg, n):
                return V.tensor_tensor(val[:, 0:n, :].rearrange("p c (h f) -> p c h f", h=HEADS),
                                       sg[:, :, HEADS:ROW].rearrange("p c (h f) -> p c h f", h=HEADS),
                                       ex[:, 0:n, :].unsqueeze(3).to_broadcast([P, n, HEADS, NE + 1]), ALU.mult)

            def spread_column(col):
                return V.tensor_tensor(spread[:, col % NR, :, :],
                                       hi_hot[:, col, :].unsqueeze(2).to_broadcast([P, NT, VAL]),
                                       val[:, col, :].unsqueeze(1).to_broadcast([P, NT, VAL]), ALU.mult)

            V.tensor_copy(act_gate[:, 2:3], ident[:, 0:1]).then_inc(y_ready, 1)
            V.tensor_copy(act_gate[:, 3:4], ident[:, 0:1]).then_inc(y_ready, 1)
            loop_at = st.now()
            PSTEPS = PAIR_STEPS
            with ve.Fori(0, NSUB // 2) as it:
                st.base, st.n = it * PSTEPS + loop_at, 0

                def step(ins):
                    st.add(ins)
                    ve.wait_ge(dve, st.now())

                for u in range(2):
                    sub = 2 * it + u
                    sg, dg = src_got[:, u, :, :], dst_got[:, u, :, :]
                    ve.wait_ge(spread_used, SUB * sub + NR)
                    one_hots(pk_lo[:, bass.ds(sub * SUB, SUB)], pk_hi[:, bass.ds(sub * SUB, SUB)], SUB)
                    ve.wait_ge(pair_in[u], 32 * SUB * (it + 1))
                    exponents(step, sg, dg, SUB).then_inc(pair_lg, 1)
                    ve.wait_ge(pair_ex, sub + 1)
                    step(messages(sg, SUB))
                    V.tensor_scalar(src_idx[:, u, :], pk_src[:, bass.ds((sub + 2) * SUB, SUB)], 0.0, None, ALU.add)
                    V.tensor_scalar(dst_idx[:, u, :], pk_dst[:, bass.ds((sub + 2) * SUB, SUB)], 0.0, None, ALU.add)\
                        .then_inc(pair_idx_ready, 1)
                    col = 0
                    for e in range(NE):
                        for _ in range(4 if e == 0 else 3):
                            if col >= NR:
                                ve.wait_ge(spread_used, SUB * sub + col + 1)
                            spread_column(col).then_inc(spread_ready, 1)
                            col += 1
                        ve.wait_ge(down_done, NE * sub + e + 1)
                        V.tensor_tensor(y_exp[:, bass.ds(sub * 4, 4), e, :],
                                        banks[6 + e % 2][:, :].rearrange("p (q c) -> p q c", q=4),
                                        b2_sb[:, e, :].unsqueeze(1).to_broadcast([P, 4, C]), ALU.add).then_inc(y_ready, 1)
                assert st.n == PSTEPS, st.n
            st.base, st.n = loop_at + PSTEPS * (NSUB // 2), 0

            ve.wait_ge(sums_done, 1)
            ve.wait_ge(general_known, 1)
            general = ve.value_load(general_i[0:1, 0:1], min_val=0, max_val=1)
            with ve.If(general == 1):
                V.tensor_scalar(count[:, :], count[:, :], 0.0, None, ALU.mult)
                V.tensor_copy(act_gate[:, 1:2], ident[:, 0:1]).then_inc(g_free, 1)
                V.tensor_copy(act_gate[:, 2:3], ident[:, 0:1]).then_inc(g_step, 1)
                G_STEPS = 5
                with ve.Fori(0, EC // GC // 2) as it:
                  for u in range(2):
                    gs = Steps(g_step)
                    gs.base = (2 * it + u) * G_STEPS + 1

                    def step(ins):
                        gs.add(ins)
                        ve.wait_ge(g_step, gs.now())

                    ve.wait_ge(g_step, gs.now())
                    ve.wait_ge(g_edges_in, 64 * it + 32 * u + 32)
                    V.tensor_scalar(src_idx[:, 0, 0:GC], g_edge[:, 0, :], float(M - 1), None, ALU.min)
                    V.tensor_scalar(dst_idx[:, 0, 0:GC], g_edge[:, 1, :], float(M - 1), None, ALU.min).then_inc(g_idx, 1)
                    V.tensor_scalar(g_int[:, 0, :], g_edge[:, 1, :], P - 1, None, ALU.bitwise_and)
                    step(V.tensor_scalar(g_int[:, 1, :], g_edge[:, 1, :], 7, None, ALU.arith_shift_right))
                    step(V.tensor_copy(g_lohi[:, :, :], g_int[:, :, :]))
                    V.tensor_scalar(dve_gate[0:1, 0:1], iota_f[0:1, 0:1], 0.0, None, ALU.add).then_inc(g_free, 1)
                    ve.wait_ge(g_used, GC * (2 * it + u) + NR)
                    one_hots(g_lohi[:, 0, :], g_lohi[:, 1, :], GC)
                    for n in range(2):
                        ve.wait_ge(g_rows_in[u][n], 16 * GC * (it + 1))
                    exponents(step, src_got[:, 0, 0:GC, :], dst_got[:, 0, 0:GC, :], GC).then_inc(g_lg, 1)
                    ve.wait_ge(g_ex, 2 * it + u + 1)
                    step(messages(src_got[:, 0, 0:GC, :], GC))
                    for col in range(GC):
                        if col >= NR:
                            ve.wait_ge(g_used, GC * (2 * it + u) + col + 1)
                        spread_column(col).then_inc(g_spread, 1)
                    assert gs.n == G_STEPS, gs.n
                ve.wait_ge(g_sums, 1)

            for h in range(2):
                ins = V.tensor_copy(sums[:, h * NT // 2:(h + 1) * NT // 2, :], banks[h][:, 0:NT // 2 * VAL])
            done(ins)
            ve.wait_ge(dn_exp, 1)
            own, lastw = dn[:, 0, :, :], dn[:, 1, :, :]
            done(V.tensor_tensor(lastw, lastw, count[:, :].unsqueeze(2).to_broadcast([P, NT, HEADS]), ALU.mult))
            sums4 = sums[:, :, :].rearrange("p i (h f) -> p i h f", h=HEADS)
            rows4 = trow[:, :, HEADS:ROW].rearrange("p i (h f) -> p i h f", h=HEADS)
            last4 = last_tok[:, HEADS:ROW].rearrange("p (h f) -> p h f", h=HEADS)
            F = NE + 1
            for h in range(HEADS):
                V.tensor_tensor(rows4[:, :, h, :], rows4[:, :, h, :], own[:, :, h].unsqueeze(2).to_broadcast([P, NT, F]), ALU.mult)
                ins = V.tensor_tensor(big[:, :, h, :], last4[:, h, :].unsqueeze(1).to_broadcast([P, NT, F]),
                                      lastw[:, :, h].unsqueeze(2).to_broadcast([P, NT, F]), ALU.mult)
            done(ins)
            done(V.tensor_tensor(sums[:, :, :], sums[:, :, :], trow[:, :, HEADS:ROW], ALU.add))
            done(V.tensor_tensor(sums4, sums4, big, ALU.add))
            den = dn[:, 2, :, :]
            done(V.tensor_scalar(den, sums4[:, :, :, 0], 1e-16, None, ALU.add))
            done(V.reciprocal(den, den))
            t4 = tmp16[:, :, :].rearrange("p i (h e) -> p i h e", e=NE)
            done(V.tensor_tensor(t4, sums4[:, :, :, 1:], den.unsqueeze(3).to_broadcast([P, NT, HEADS, NE]), ALU.mult))

            def vec(n):
                return small[:, n, :].unsqueeze(1).to_broadcast([P, NT, HE])
            done(V.tensor_tensor(tmp16[:, :, :], tmp16[:, :, :], vec(2), ALU.add))
            mu, var = cmp[:, 0, :], cmp[:, 1, :]
            done(V.tensor_reduce(mu, tmp16[:, :, :], AX.X, ALU.add))
            done(V.tensor_scalar(mu, mu, 1.0 / HE, None, ALU.mult))
            done(V.tensor_tensor(tmp16[:, :, :], tmp16[:, :, :], mu.unsqueeze(2).to_broadcast([P, NT, HE]), ALU.subtract))
            sq = bigf[:, 0:NT * HE].rearrange("p (i f) -> p i f", f=HE)
            done(V.tensor_tensor(sq, tmp16[:, :, :], tmp16[:, :, :], ALU.mult))
            done(V.tensor_reduce(var, sq, AX.X, ALU.add))
            V.tensor_scalar(var, var, 1.0 / HE, EPS_T, ALU.mult, ALU.add).then_inc(var_ready, 1)
            ve.wait_ge(root_done, B + 2)
            done(V.reciprocal(var, var))
            done(V.tensor_tensor(tmp16[:, :, :], tmp16[:, :, :], var.unsqueeze(2).to_broadcast([P, NT, HE]), ALU.mult))
            done(V.tensor_tensor(tmp16[:, :, :], tmp16[:, :, :], vec(3), ALU.mult))
            done(V.tensor_tensor(tmp16[:, :, :], tmp16[:, :, :], vec(4), ALU.add))
            done(V.tensor_reduce(score[:, :, :], tmp16[:, :, :].rearrange("p i (h e) -> p i e h", e=NE), AX.X, ALU.add))
            done(V.tensor_scalar(score[:, :, :], score[:, :, :], 1.0 / HEADS, None, ALU.mult))
            top = cmp[:, 2, :]
            done(V.tensor_reduce(top, score[:, :, :], AX.X, ALU.max))
            V.tensor_tensor(gate[:, :, :], score[:, :, :], top.unsqueeze(2).to_broadcast([P, NT, NE]), ALU.subtract)\
                .then_inc(sc_ready, 1)
            beat = bigf[:, 0:NE * NT].rearrange("p (e i) -> p e i", e=NE)
            done(V.memset(beat, 0.0))
            for a in range(NE):
                for b in range(a + 1, NE):
                    done(V.tensor_tensor(cmp[:, 3, :], score[:, :, a], score[:, :, b], ALU.is_ge))
                    V.tensor_tensor(beat[:, b, :], beat[:, b, :], cmp[:, 3, :], ALU.add)
                    done(V.tensor_tensor(cmp[:, 4, :], score[:, :, a], score[:, :, b], ALU.is_lt))
                    done(V.tensor_tensor(beat[:, a, :], beat[:, a, :], cmp[:, 4, :], ALU.add))
            ve.wait_ge(sc_exp, 1)
            done(V.scalar_tensor_tensor(out=gate[:, :, :], in0=beat.rearrange("p e i -> p i e"), scalar=1.5,
                                        in1=gate[:, :, :], op0=ALU.is_lt, op1=ALU.mult))
            done(V.tensor_reduce(cmp[:, 5, :], gate[:, :, :], AX.X, ALU.add))
            done(V.reciprocal(cmp[:, 5, :], cmp[:, 5, :]))
            done(V.tensor_tensor(gate[:, :, :], gate[:, :, :], cmp[:, 5, :].unsqueeze(2).to_broadcast([P, NT, NE]), ALU.mult))

            for g in range(NT // 4):
                for e in range(NE):
                    for t in range(4 * g, 4 * g + 4):
                        ins = V.scalar_tensor_tensor(out=x_tok[:, t, :], in0=y_exp[:, t, e, :], scalar=gate[:, t, e:e + 1],
                                                     in1=x_tok[:, t, :], op0=ALU.mult, op1=ALU.add)
                    if e < NE - 1:
                        done(ins)
                ins.then_inc(res_ready, 1)


_INS = ["x", "L0_conv_offset_w", "L0_conv_offset_b", "L0_conv_dcn_w", "L0_ffn_W_gat", "L0_ffn_att_src", "L0_ffn_att_dst",
        "L0_ffn_b_gat", "L0_ffn_ln_gamma", "L0_ffn_ln_beta", "L0_ffn_W1", "L0_ffn_b1", "L0_ffn_W2", "L0_ffn_b2",
        "L0_ffn_edge_index"]


def kernel(**inputs):
    import numpy as np
    import concourse.bacc as bacc
    from concourse import mybir as mb
    from concourse.bass_utils import run_bass_kernel_spmd as run

    nc = bacc.Bacc("TRN2", target_bir_lowering=False, num_devices=1)
    arrays, args = {}, []
    for name in _INS:
        a = np.asarray(inputs[name])
        if name == "L0_conv_offset_w" or name == "L0_conv_dcn_w":
            a = a.reshape(a.shape[0], a.shape[1], 9).transpose(1, 2, 0)
        if name == "L0_ffn_b1":
            a = a.reshape(a.shape[0], -1, 128).transpose(2, 0, 1)
        a = np.ascontiguousarray(a)
        arrays[f"in_{name}_dram"] = a
        args.append(nc.dram_tensor(f"in_{name}_dram", a.shape, mb.dt.from_np(a.dtype), kind="ExternalInput").ap())
    args.append(nc.dram_tensor("out_0_dram", inputs["x"].shape, mb.dt.float32, kind="ExternalOutput").ap())
    metaformer(nc, *args)
    r = run(nc, [arrays], core_ids=[0])
    return r.results[0]["out_0_dram"]
```

```python
from contextlib import ExitStack

import concourse.bass as bass
from concourse import mybir

P = 128
ALU = mybir.AluOpType
ACT = mybir.ActivationFunctionType
AX = mybir.AxisListType
F32 = mybir.dt.float32
BF16 = mybir.dt.bfloat16
I32 = mybir.dt.int32
RMAX = bass.bass_isa.ReduceOp.max


class Steps:

    def __init__(self, sem):
        self.sem, self.base, self.n = sem, 0, 0

    def now(self):
        return self.base + self.n

    def add(self, ins):
        ins.then_inc(self.sem, 1)
        self.n += 1


def metaformer(nc, x, offw, offb, dcnw, wgat, att_s, att_d, b_gat, ln_g, ln_b, w1, b1, w2, b2, edges, out,
               general_always=False):
    B, C, H, W = x.shape
    HW = H * W
    M = B * HW
    NT = M // P
    TB = HW // P
    K = 9
    NOFF = 3 * K
    HEADS, NE = att_s.shape
    HE = HEADS * NE
    HID = w1.shape[2]
    NF = HID // P
    EC = edges.shape[1] // P
    SHIFTS = [0, 1, W, W + 1]
    FRONT = W + 1
    EPS_C, EPS_T = 1e-6, 1e-5

    SEG = 256
    NSEG = EC // SEG
    CAP = 64
    PCAP = 16
    PICKED = 104
    OWN = 56
    REST = 96
    SUB = 10
    NSUB = NT // 4
    PC = SUB * NSUB
    ROW = HEADS + HEADS * (NE + 1)
    VAL = HEADS * (NE + 1)
    LO = 64
    assert PC == OWN + REST // 4 and CAP // 8 + 1 == K and EC % SEG == 0 and NSEG * 2 == NT and M == LO * LO and NE == 4

    with ExitStack() as ctx:
        def sb(name, shape, dt=F32):
            return ctx.enter_context(nc.sbuf_tensor(name, shape, dt))

        def sem(name):
            return ctx.enter_context(nc.semaphore(name))

        cells = nc.dram_tensor("cells", [FRONT + M, 4 * C], F32)
        src_rows = nc.dram_tensor("src_rows", [M, ROW], F32)
        dst_rows = nc.dram_tensor("dst_rows", [M, HEADS], F32)

        chan = sb("chan", [P, M])
        x_all = sb("x_all", [P, 1 + NT, C])
        x_tok = x_all[:, 1:, :]
        n_tok = sb("n_tok", [P, NT, C])
        PH, PW = H + 2, W + 2
        padded = sb("padded", [P, B * PH * PW])
        ringed = padded[:, :].rearrange("p (b y x) -> p b y x", b=B, y=PH)
        onehots = padded[:, 0:4096].bitcast(BF16).rearrange("p (h j c) -> p h j c", h=2, j=LO)
        late_at = [0]

        def late(shape):
            n = 1
            for d in shape[1:]:
                n *= d
            late_at[0] += n
            assert late_at[0] <= B * PH * PW
            flat = padded[:, late_at[0] - n:late_at[0]]
            if len(shape) == 3:
                return flat.rearrange("p (a b) -> p a b", b=shape[2])
            return flat.rearrange("p (a b c) -> p a b c", b=shape[2], c=shape[3])

        arena = sb("arena", [P, 2 * EC + 2 * K * 4 * C])
        edge_i = arena[:, 0:2 * EC].bitcast(I32).rearrange("p (s e) -> p s e", s=2)
        edge_f = arena[:, 0:2 * EC].bitcast(I32)
        cell = arena[:, 2 * EC:].rearrange("p (u k c f) -> p u k c f", u=2, k=K, c=4)
        y_exp = arena[:, 0:NT * NE * C].rearrange("p (i e c) -> p i e c", i=NT, e=NE)
        NSC, NST = 6912, 2 * K * C
        scratch = sb("scratch", [P, NSC])
        samp = scratch[:, NSC - NST:].rearrange("p (u k c) -> p u k c", u=2, k=K)

        ident = sb("ident", [P, P])
        last_row = sb("last_row", [P, P])
        fold = sb("fold", [LO, 2, P])
        offw_sb = sb("offw_sb", [P, K, 32])
        dcnw_sb = sb("dcnw_sb", [P, K, C])
        PROJ = HE + 2 * HEADS
        wgat_sb = sb("wgat_sb", [P, PROJ])
        w1_sb = sb("w1_sb", [P, NE, HID])
        w2_sb = sb("w2_sb", [P, NE, NF, C])
        b1_sb = sb("b1_sb", [P, NE, NF])
        b2_sb = sb("b2_sb", [P, NE, C])
        offb_sb = sb("offb_sb", [P, NOFF])
        small = sb("small", [P, 5, HE])

        iota_i = arena[:, 2 * EC:2 * EC + P].bitcast(I32)
        att_products = arena[:, 2 * EC + P:2 * EC + P + HE]
        iota_f = sb("iota_f", [P, P])
        lanes = sb("lanes", [P, LO, 64], BF16)
        part_i = sb("part_i", [P, 4], I32)
        part_f = sb("part_f", [P, 4])
        zero_bf = sb("zero_bf", [P, LO], BF16)
        zero_f = sb("zero_f", [P, 320])
        pool_gate = sb("pool_gate", [P, 5])
        dve_gate = sb("dve_gate", [P, 64])

        stats = sb("stats", [P, NT, 6])
        st_a = sb("st_a", [P, 3, NT])
        mean = sb("mean", [P, NT])
        rstd = sb("rstd", [P, NT])
        shift = sb("shift", [P, NT])

        idx_f = sb("idx_f", [P, NT + 2, K])
        corner_w = sb("corner_w", [P, NT + 2, 4, K])
        idx_slot = sb("idx_slot", [P, 2, K], I32)
        w_slot = sb("w_slot", [P, 2, 4, K])

        keys = sb("keys", [P, SEG])
        kept = sb("kept", [P, CAP + 8])
        kept_i = sb("kept_i", [P, 3, CAP], I32)
        kept_lohi = sb("kept_lohi", [P, 2, CAP], BF16)
        pairs1 = sb("pairs1", [P, NSEG * PCAP])
        pairs2 = sb("pairs2", [P, PICKED + 8])
        lost = sb("lost", [P, 2])
        pk_i = sb("pk_i", [P, 4, PC], I32)
        pk_src = sb("pk_src", [P, PC + 2 * SUB])
        pk_dst = sb("pk_dst", [P, PC + 2 * SUB])
        pk_lo = sb("pk_lo", [P, PC])
        pk_hi = sb("pk_hi", [P, PC])
        pk_void = sb("pk_void", [P, PC])
        hist_sb = sb("hist_sb", [LO, LO])
        count = sb("count", [P, NT])

        trow = late([P, NT, ROW])
        a_dst = late([P, NT, HEADS])
        tmp16 = late([P, NT, HE])
        amax_p = sb("amax_p", [P, HEADS])
        amax = sb("amax", [P, HEADS])
        lost_all = sb("lost_all", [P, 1])
        last_tok = sb("last_tok", [P, ROW])
        src_idx = sb("src_idx", [P, 2, SUB], I32)
        dst_idx = sb("dst_idx", [P, 2, SUB], I32)
        src_got = late([P, 2, SUB, ROW])
        dst_got = late([P, 2, SUB, HEADS])
        lg = late([P, 4, SUB, HEADS])
        ex = late([P, SUB, HEADS])
        val = scratch[:, 0:2 * SUB * VAL].rearrange("p (u c v) -> p u c v", u=2, v=VAL)
        hi_hot = scratch[:, 2 * SUB * VAL:2 * SUB * (VAL + NT)].rearrange("p (u c i) -> p u c i", u=2, i=NT)
        assert VAL + NT <= P // 2
        lo_hot = n_tok[:, 0:2 * SUB, :].rearrange("p (u c) l -> p u c l", u=2)
        NR = 4
        assert 2 * SUB % NR == 0
        spread = scratch[:, SUB * P:SUB * P + NR * NT * VAL].rearrange("p (r i v) -> p r i v", r=NR, i=NT)
        hid = scratch[:, 4608:4608 + 2048].rearrange("p (f t) -> p f t", f=4)
        wins_flat = scratch[:, 0:NT * NE * NE]
        lost_to = scratch[:, NT * NE * NE:NT * NE * (NE + 2)].rearrange("p (n i e) -> p n i e", n=2, i=NT)
        sums = late([P, NT, VAL])
        dn = late([P, 6, NT, HEADS])
        score = late([P, NT, NE])
        gate = late([P, NT, NE])
        cmp = scratch[:, 6656:6912].rearrange("p (n i) -> p n i", n=8)
        general_i = sb("general_i", [P, 1], I32)
        GC = 8
        g_edge = sb("g_edge", [P, 2, GC], I32)
        g_int = sb("g_int", [P, 2, GC], I32)
        g_lohi = sb("g_lohi", [P, 2, GC])

        beta_mean = sb("beta_mean", [P, NE])
        act_gate = sb("act_gate", [P, 4])
        off_sb = scratch[:, 0:NT * NOFF].rearrange("p (t c) -> p t c", c=NOFF)
        TK = NT * K
        OROWS = 8
        NCH = H // OROWS
        col_sums = scratch[:, NSC - 2 * OROWS * W - NOFF:NSC - NOFF].rearrange("p (u f) -> p u f", u=2)
        add_taps = scratch[:, NSC - NOFF:NSC]
        (py, px, cy, cx, hy0, hy1, hx0, hx1, mask) = (
            scratch[:, NT * NOFF + n * TK:NT * NOFF + (n + 1) * TK].rearrange("p (t k) -> p t k", k=K) for n in range(9))
        (cy_i, cx_i, by_i, bx_i, bt_i) = (
            scratch[:, NT * NOFF + (9 + n) * TK:NT * NOFF + (10 + n) * TK].bitcast(I32).rearrange("p (t k) -> p t k", k=K)
            for n in range(5))
        bigf = arena[:, NT * NE * C:NT * NE * C + NT * VAL]
        big = bigf[:, :].rearrange("p (i h f) -> p i h f", h=HEADS, f=NE + 1)
        at = NT * NE * C + NT * VAL
        rest = arena[0:32, at:at + 4 * (PICKED - OWN)]
        rest_top = arena[0:32, at + 4 * (PICKED - OWN):at + 4 * (PICKED - OWN) + REST + 8]
        N_ENDS = sum((FRONT > shift) + (shift > 0) for shift in SHIFTS)
        POOL_CONST = 12
        HID_CREDIT = 2
        QUARTER = [range(SUB * e // NE, SUB * (e + 1) // NE) for e in range(NE)]
        SLOTS = 6
        LOOP_STEPS = 25
        PAIR_STEPS = 3

        banks = [ctx.enter_context(nc.psum_tensor(f"bank{n}", [P, 512], F32)) for n in range(8)]

        x_in = [sem(f"x_in{b}") for b in range(B)]
        w_in, offw_in = sem("w_in"), sem("offw_in")
        ident_ready, ring_ready, pad_ready, add_ready = (sem(n) for n in ("ident_ready", "ring_ready", "pad_ready",
                                                                          "add_ready"))
        cols_done, cols_copied = sem("cols_done"), sem("cols_copied")
        e_in = sem("e_in")
        pool_step = sem("pool_step")
        x_turned, x_copied = sem("x_turned"), sem("x_copied")
        var_ready, root_done = sem("var_ready"), sem("root_done")
        zeros_ready, ends_out = sem("zeros_ready"), sem("ends_out")
        gate_done = sem("gate_done")
        general_known = sem("general_known")
        g_rows_in = [[sem(f"general_{n}_in{u}") for n in ("src", "dst")] for u in range(2)]
        (g_step, g_free, g_edges_in, g_idx, g_lg, g_ex, g_spread, g_used, g_sums, g_gate) = (
            sem("general_" + n) for n in ("step", "free", "edges_in", "idx", "lg", "ex", "spread", "used", "sums",
                                          "gate"))
        normed, n_turned, n_copied = sem("normed"), sem("n_turned"), sem("n_copied")
        cells_out = [sem(f"cells_out{b}") for b in range(B)]
        off_done, off_read, mask_done = sem("off_done"), sem("off_read"), sem("mask_done")
        dve = sem("dve")
        idx_ready = sem("idx_ready")
        cells_in = [sem(f"cells_in{s}") for s in range(6)]
        scaled_a, scaled_v, w_ready, turned, samp_ready, conv_done = (
            sem(n) for n in ("scaled_a", "scaled_v", "w_ready", "turned", "samp_ready", "conv_done"))
        hot_ready, hist_done = sem("hot_ready"), sem("hist_done")
        hist_copied = sem("hist_copied")
        t_normed, t_turned, t_copied = sem("t_normed"), sem("t_turned"), sem("t_copied")
        table_in = sem("table_in")
        shift_ready, t_normed_a, w_att_ready = sem("shift_ready"), sem("t_normed_a"), sem("w_att_ready")
        proj_done, rows_ready, rows_out = sem("proj_done"), sem("rows_ready"), sem("rows_out")
        amax_ready, amax_done, last_done = sem("amax_ready"), sem("amax_done"), sem("last_done")
        pair_idx_ready = sem("pair_idx_ready")
        picked, rest_in, rest_picked, rest_out = (sem(n) for n in ("picked", "rest_in", "rest_picked", "rest_out"))
        lost_ready, lost_done = sem("lost_ready"), sem("lost_done")
        pair_in = [sem(f"pair_in{u}") for u in range(2)]
        pair_lg, pair_ex = sem("pair_lg"), sem("pair_ex")
        spread_ready, spread_used = sem("spread_ready"), sem("spread_used")
        up_done, hid_ready, down_done, y_ready = sem("up_done"), sem("hid_ready"), sem("down_done"), sem("y_ready")
        sums_done = sem("sums_done")
        gates_ready, outputs_weighed, second_weighed = sem("gates_ready"), sem("outputs_weighed"), sem("second_weighed")
        dn_ready, dn_exp = sem("dn_ready"), sem("dn_exp")
        sc_ready, sc_exp = sem("sc_ready"), sem("sc_exp")
        res_ready, res_turned, res_copied, res_out = (sem(n) for n in ("res_ready", "res_turned", "res_copied", "res_out"))

        block = ctx.enter_context(nc.Block())

        PARAMS = [(offb_sb[:, :], offb.partition_broadcast(P)), (dcnw_sb[:, :, :], dcnw), (wgat_sb[:, 0:HE], wgat),
                  (w1_sb[:, :, :], w1.rearrange("e d f -> d e f")),
                  (w2_sb[:, :, :, :], w2.rearrange("e (f p) d -> p e f d", p=P)),
                  (b1_sb[:, :, :], b1),
                  (b2_sb[:, :, :], b2.partition_broadcast(P))]
        PARAMS += [(small[:, n, :], v.partition_broadcast(P)) for n, v in enumerate(
            (att_s.rearrange("h e -> (h e)"), att_d.rearrange("h e -> (h e)"), b_gat, ln_g, ln_b))]

        @block.sync
        def _(sp):
            for b in range(B):
                sp.dma_start(chan[:, b * HW:(b + 1) * HW], x[b].rearrange("c h w -> c (h w)")).then_inc(x_in[b], 16)
            sp.wait_ge(pad_ready, 1)
            sp.dma_start(offw_sb[:, :, 0:NOFF], offw).then_inc(offw_in, 16)
            for dst, src in PARAMS:
                sp.dma_start(dst, src).then_inc(w_in, 16)
            sp.wait_ge(zeros_ready, 1)
            for c, shift in enumerate(SHIFTS):
                for r0, r1 in ((0, FRONT - shift), (FRONT + M - shift, FRONT + M)):
                    if r1 > r0:
                        sp.dma_start(cells[r0:r1, c * C:(c + 1) * C], zero_f[0:r1 - r0, 0:C]).then_inc(ends_out, 16)
            for b in range(B):
                sp.wait_ge(normed, b + 1)
                for c, shift in enumerate(SHIFTS):
                    r0 = FRONT + b * HW - shift
                    sp.dma_start(cells[r0:r0 + HW, c * C:(c + 1) * C].rearrange("(i p) c -> p i c", p=P),
                                 n_tok[:, b * TB:(b + 1) * TB, :]).then_inc(cells_out[b], 16)
            for s in range(2):
                sp.dma_start(edge_i[:, s, :], edges[s].rearrange("(p e) -> p e", p=P)).then_inc(e_in, 16)
            for h in range(2):
                sp.wait_ge(rows_ready, h + 1)
                i = slice(h * NT // 2, (h + 1) * NT // 2)
                r = slice(h * M // 2, (h + 1) * M // 2)
                sp.dma_start(src_rows[r, :].rearrange("(i p) c -> p i c", p=P), trow[:, i, :]).then_inc(rows_out, 16)
                sp.dma_start(dst_rows[r, :].rearrange("(i p) c -> p i c", p=P), a_dst[:, i, :]).then_inc(rows_out, 16)
            sp.wait_ge(picked, 1)
            for q in range(4):
                n = PICKED - OWN
                sp.dma_start(rest[:, q * n:(q + 1) * n], pairs2[32 * q:32 * q + 32, OWN:PICKED]).then_inc(rest_in, 16)
            sp.wait_ge(rest_picked, 1)
            for q in range(4):
                n = REST // 4
                sp.dma_start(pairs2[32 * q:32 * q + 32, OWN:PC], rest_top[:, q * n:(q + 1) * n]).then_inc(rest_out, 16)
            sp.wait_ge(general_known, 1)
            general = sp.value_load(general_i[0:1, 0:1], min_val=0, max_val=1)
            with sp.If(general == 1):
                with sp.Fori(0, EC // GC) as it:
                    sp.wait_ge(g_free, it + 1)
                    for s in range(2):
                        sp.dma_start(g_edge[:, s, :], edges[s].rearrange("(p e) -> p e", p=P)[:, bass.ds(it * GC, GC)])\
                            .then_inc(g_edges_in, 16)
            for g in range(NT // 4):
                sp.wait_ge(res_copied, g + 1)
                b, h = divmod(g, TB // 4)
                sp.dma_start(out[b].rearrange("c h w -> c (h w)")[:, h * 512:(h + 1) * 512],
                             chan[:, g * 512:(g + 1) * 512]).then_inc(res_out, 16)
            sp.wait_ge(res_out, 16 * (NT // 4))

        @block.gpsimd
        def _(pool):
            st = Steps(pool_step)
            st.add(nc.gpsimd.memset(ident[:, :], 0.0))
            pool.wait_ge(pool_step, st.now())
            nc.gpsimd.affine_select(out=ident[:, :], in_=ident[:, :], compare_op=ALU.not_equal, fill=1.0,
                                    base=0, pattern=[[-1, P]], channel_multiplier=1).then_inc(ident_ready, 1)
            nc.gpsimd.memset(ringed[:, :, ::PH - 1, :], 0.0)
            nc.gpsimd.memset(ringed[:, :, 1:PH - 1, ::PW - 1], 0.0).then_inc(ring_ready, 1)
            st.add(nc.gpsimd.memset(last_row[:, :], 1.0))
            st.add(nc.gpsimd.memset(fold[:, :, :], 0.0))
            nc.gpsimd.memset(pool_gate[:, 0:4], 0.0).then_inc(gate_done, 1)
            nc.gpsimd.memset(pool_gate[:, 4:5], 0.0).then_inc(turned, SLOTS)
            pool.wait_ge(pool_step, st.now())
            st.add(nc.gpsimd.affine_select(out=last_row[:, :], in_=last_row[:, :], compare_op=ALU.is_ge, fill=0.0,
                                           base=-(P - 1), pattern=[[0, P]], channel_multiplier=1))
            for h in range(2):
                st.add(nc.gpsimd.affine_select(out=fold[:, h, :], in_=fold[:, h, :], compare_op=ALU.not_equal,
                                               fill=1.0, base=h * LO, pattern=[[-1, P]], channel_multiplier=1))
            st.add(nc.gpsimd.iota(iota_i[:, :], [[1, P]], base=0, channel_multiplier=0))
            st.add(nc.gpsimd.iota(part_i[:, 0:1], [[0, 1]], base=0, channel_multiplier=1))
            st.add(nc.gpsimd.iota(by_i, [[0, B], [P // W, TB], [1, 3], [0, 3]], base=-1, channel_multiplier=0))
            st.add(nc.gpsimd.iota(bx_i, [[0, NT], [0, 3], [1, 3]], base=-1, channel_multiplier=0))
            st.add(nc.gpsimd.iota(bt_i, [[HW, B], [0, TB], [0, K]], base=FRONT, channel_multiplier=0))
            st.add(nc.gpsimd.iota(lanes[:, :, :], [[1, LO], [0, 64]], base=0, channel_multiplier=0,
                                  allow_small_or_imprecise_dtypes=True))
            assert st.n == POOL_CONST, st.n

            for b in range(B):
                pool.wait_ge(cells_out[b], 64)
            pool.wait_ge(ends_out, 16 * N_ENDS)
            with pool.Fori(0, NT // 2) as it:
                for u in range(2):
                    for g in range(3):
                        n = 6 * it + 3 * u + g
                        if (3 * u + g) % 2 == 0:
                            pool.wait_ge(idx_ready, n + 2)
                            pool.wait_ge(turned, n + 2)
                            pool.wait_ge(gate_done, 3 * it + (3 * u + g) // 2 + 1)
                            nc.gpsimd.tensor_tensor(pool_gate[:, 0:1], ident[:, 0:1], ident[:, 1:2], ALU.add)\
                                .then_inc(gate_done, 1)
                        for k in range(3 * g, 3 * g + 3):
                            nc.gpsimd.indirect_dma_start(
                                cell[:, u, k, :, :].rearrange("p c f -> p (c f)"), None, cells[:, :],
                                bass.IndirectOffsetOnAxis(ap=idx_slot[:, u, k:k + 1], axis=0))\
                                .then_inc(cells_in[3 * u + g], 16)

            pool.wait_ge(amax_ready, 1)
            nc.gpsimd.partition_all_reduce(amax[:, :], amax_p[:, :], P, RMAX).then_inc(amax_done, 1)
            pool.wait_ge(rows_out, 64)
            with pool.Fori(0, NSUB // 2) as it:
                for u in range(2):
                    pool.wait_ge(pair_idx_ready, 2 * it + u + 1)
                    pool.wait_ge(gate_done, 2 * it + u + 1 + 3 * NT // 2)
                    nc.gpsimd.tensor_tensor(pool_gate[:, 2 + u:3 + u], ident[:, 0:1], ident[:, 1:2], ALU.add).then_inc(gate_done, 1)
                    for c in range(SUB):
                        nc.gpsimd.indirect_dma_start(
                            src_got[:, u, c, :], None, src_rows[:, :],
                            bass.IndirectOffsetOnAxis(ap=src_idx[:, u, c:c + 1], axis=0)).then_inc(pair_in[u], 16)
                        nc.gpsimd.indirect_dma_start(
                            dst_got[:, u, c, :], None, dst_rows[:, :],
                            bass.IndirectOffsetOnAxis(ap=dst_idx[:, u, c:c + 1], axis=0)).then_inc(pair_in[u], 16)

            pool.wait_ge(lost_ready, 1)
            nc.gpsimd.partition_all_reduce(lost_all[:, :], lost[:, 0:1], P, RMAX).then_inc(lost_done, 1)
            pool.wait_ge(general_known, 1)
            general = pool.value_load(general_i[0:1, 0:1], min_val=0, max_val=1)
            with pool.If(general == 1):
                nc.gpsimd.memset(pool_gate[:, 0:2], 0.0).then_inc(g_gate, 1)
                with pool.Fori(0, EC // GC // 2) as it:
                    for u in range(2):
                        pool.wait_ge(g_idx, 2 * it + u + 1)
                        pool.wait_ge(g_gate, 2 * it + u + 1)
                        nc.gpsimd.tensor_tensor(pool_gate[:, 0:1], ident[:, 0:1], ident[:, 1:2], ALU.add).then_inc(g_gate, 1)
                        for c in range(GC):
                            nc.gpsimd.indirect_dma_start(
                                src_got[:, 0, c, :], None, src_rows[:, :],
                                bass.IndirectOffsetOnAxis(ap=src_idx[:, 0, c:c + 1], axis=0)).then_inc(g_rows_in[u][0], 16)
                            nc.gpsimd.indirect_dma_start(
                                dst_got[:, 0, c, :], None, dst_rows[:, :],
                                bass.IndirectOffsetOnAxis(ap=dst_idx[:, 0, c:c + 1], axis=0)).then_inc(g_rows_in[u][1], 16)

            pool.wait_ge(gates_ready, 1)
            for g in range(NT // 4):
                if g == NT // 4 - 1:
                    pool.wait_ge(y_ready, NE * NSUB + 2)
                for t in range(4 * g, 4 * g + 2):
                    ins = nc.gpsimd.tensor_scalar(y_exp[:, t, 1, :], y_exp[:, t, 1, :], gate[:, t, 1:2], None, ALU.mult)
                ins.then_inc(second_weighed, 1)

        @block.tensor
        def _(pe):
            pe.wait_ge(ident_ready, 1)
            for b in range(B):
                pe.wait_ge(x_in[b], 16)
                for h in range(2):
                    g = 2 * b + h
                    if g >= 2:
                        pe.wait_ge(x_copied, g - 1)
                    for q in range(4):
                        t = 4 * g + q
                        mm = nc.tensor.transpose(banks[6 + g % 2][:, q * P:(q + 1) * P], chan[:, t * P:(t + 1) * P], ident[:, :])
                    mm.then_inc(x_turned, 1)

            def add_columns(m):
                pe.wait_ge(cols_copied, m + 1)
                b, j = divmod(m, NCH)
                for q in range(2):
                    o = (2 * j + q) * 32
                    mm = nc.tensor.matmul(banks[4 + b][:, o:o + NOFF], col_sums[0:96, m % 2, q * P:(q + 1) * P],
                                          add_taps[0:96, :], start=True, stop=True)
                mm.then_inc(off_done, 1)

            pe.wait_ge(offw_in, 16)
            pe.wait_ge(ring_ready, 1)
            pe.wait_ge(add_ready, 1)
            for b in range(B):
                pe.wait_ge(normed, b + 1)
                for h in range(2):
                    g = 2 * b + h
                    if g >= 2:
                        pe.wait_ge(n_copied, g - 1)
                    for q in range(4):
                        mm = nc.tensor.transpose(banks[2 + g % 2][:, q * P:(q + 1) * P], n_tok[:, 4 * g + q, :], ident[:, :])
                    mm.then_inc(n_turned, 1)
                pe.wait_ge(n_copied, 2 * b + 2)
                for j in range(NCH):
                    m = b * NCH + j
                    if m >= 2:
                        pe.wait_ge(cols_copied, m - 1)
                    for ki in range(3):
                        at = (b * PH + j * OROWS + ki) * PW
                        mm = nc.tensor.matmul(banks[m % 2][0:96, 0:OROWS * PW],
                                              offw_sb[:, 3 * ki:3 * ki + 3, :].rearrange("p k c -> p (k c)"),
                                              padded[:, at:at + OROWS * PW], start=(ki == 0), stop=(ki == 2))
                    mm.then_inc(cols_done, 1)
                    if m >= 1:
                        add_columns(m - 1)
            add_columns(B * NCH - 1)

            pe.wait_ge(w_in, 16 * len(PARAMS))
            pe.wait_ge(off_read, B)
            hist = banks[7][0:LO, 0:LO]
            nc.tensor.matmul(hist, zero_bf[:, :], zero_bf[:, :], start=True, stop=False).then_inc(hist_done, 1)
            nc.tensor.matmul(banks[4][:, 0:C], zero_f[:, 0:P], zero_f[:, 0:C], start=True, stop=False)

            def turn(n, u, g):
                pe.wait_ge(scaled_a, n + 1)
                pe.wait_ge(scaled_v, n + 1)
                for j in range(3):
                    for c in range(4):
                        mm = nc.tensor.matmul(banks[g][:, j * P:(j + 1) * P], cell[:, u, 3 * g + j, c, :], ident[:, :],
                                              is_transpose=True, start=(c == 0), stop=(c == 3))
                mm.then_inc(turned, 1)

            def weigh(n, u, g):
                pe.wait_ge(samp_ready, n + 1)
                for k in range(3 * g, 3 * g + 3):
                    mm = nc.tensor.matmul(banks[3 + u][:, 0:C], samp[:, u, k, :], dcnw_sb[:, k, :],
                                          start=(k == 0), stop=(k == K - 1))
                if g == 2:
                    mm.then_inc(conv_done, 1)

            with pe.Fori(0, NT // 2) as it:
                for u in range(2):
                    n = 6 * it + 3 * u
                    turn(n, u, 0)
                    weigh(n, 1 - u, 2)
                    turn(n + 1, u, 1)
                    weigh(n + 1, u, 0)
                    turn(n + 2, u, 2)
                    weigh(n + 2, u, 1)
                pe.wait_ge(hot_ready, it + 1)
                for c in range(CAP):
                    mm = nc.tensor.matmul(hist, onehots[:, 0, :, c], onehots[:, 1, :, c], start=False, stop=False)
                mm.then_inc(hist_done, 1)
            weigh(3 * NT, 1, 2)
            nc.tensor.matmul(hist, zero_bf[:, :], zero_bf[:, :], start=False, stop=True).then_inc(hist_done, 1)

            pe.wait_ge(w_att_ready, 1)
            for g in range(NT // 4 + 1):
                if g < NT // 4:
                    pe.wait_ge(t_normed if g % 2 == 0 else t_normed_a, g // 2 + 1)
                    if g >= 2:
                        pe.wait_ge(t_copied, g - 1)
                    for q in range(4):
                        mm = nc.tensor.transpose(banks[g % 2][:, q * P:(q + 1) * P], n_tok[:, 4 * g + q, :], ident[:, :])
                    mm.then_inc(t_turned, 1)
                if g >= 1:
                    pe.wait_ge(t_copied, g)
                    for t in range(4 * g - 4, 4 * g):
                        i = t % (NT // 2)
                        mm = nc.tensor.matmul(banks[2 + t // (NT // 2)][:, i * PROJ:(i + 1) * PROJ],
                                              chan[:, t * P:(t + 1) * P], wgat_sb[:, :], start=True, stop=True)
                    if g % (NT // 8) == 0:
                        mm.then_inc(proj_done, 1)
            pe.wait_ge(hist_copied, 1)
            hv = hist_sb[:, :].rearrange("l (i h) -> l h i", h=2)
            for h in range(2):
                nc.tensor.matmul(banks[6][:, ROW:ROW + NT], fold[:, h, :], hv[:, h, :], start=(h == 0), stop=(h == 1))
            pe.wait_ge(rows_ready, 2)
            nc.tensor.matmul(banks[6][:, 0:ROW], last_row[:, :], trow[:, NT - 1, :], start=True, stop=True)\
                .then_inc(last_done, 1)

            half = NT // 2 * VAL
            sum_bank = [banks[0][:, 0:half], banks[1][:, 0:half]]
            for h in range(2):
                pe.wait_ge(t_copied, NT // 4)
                mm = nc.tensor.matmul(sum_bank[h], zero_f[:, 0:P], zero_f[:, 0:half], start=True, stop=False)
            mm.then_inc(spread_used, NR)

            def up(s, e):
                chunk = chan[:, bass.ds(s * 512, 512)]
                for f in range(NF):
                    n = e * NF + f
                    pe.wait_ge(hid_ready, NE * NF * s + n + 1)
                    nc.tensor.matmul(banks[4 + n % 2][:, :], w1_sb[:, e, f * P:(f + 1) * P], chunk,
                                     start=True, stop=True).then_inc(up_done, 1)

            def down(s, e):
                pe.wait_ge(hid_ready, NE * NF * s + (e + 1) * NF + HID_CREDIT)
                pe.wait_ge(y_ready, NE * s + e + 1)
                for q in range(4):
                    for f in range(NF):
                        mm = nc.tensor.matmul(banks[6 + e % 2][:, q * C:(q + 1) * C],
                                              hid[:, (e % 2) * NF + f, q * P:(q + 1) * P], w2_sb[:, e, f, :],
                                              start=(f == 0), stop=(f == NF - 1))
                mm.then_inc(down_done, 1)

            def add_pairs(s, u, e, last=False):
                for col in QUARTER[e]:
                    pe.wait_ge(spread_ready, SUB * s + col + 1)
                    for h in range(2):
                        mm = nc.tensor.matmul(sum_bank[h], lo_hot[:, u, col, :],
                                              spread[:, (u * SUB + col) % NR, h * NT // 2:(h + 1) * NT // 2, :],
                                              start=False, stop=(last and col == SUB - 1))
                    mm.then_inc(sums_done if last and col == SUB - 1 else spread_used, 1)

            for n in range(2 * NE + 1):
                if n < 2 * NE:
                    up(n // NE, n % NE)
                if n > 0:
                    down((n - 1) // NE, (n - 1) % NE)

            def pair_step(p, u):
                for e in range(NE):
                    up(p + 2, e)
                    add_pairs(p, u, e)
                    down(p + 2, e)

            with pe.Fori(0, NSUB // 2 - 2) as it:
                pair_step(2 * it, 0)
                pair_step(2 * it + 1, 1)
            pair_step(NSUB - 4, 0)
            for p in range(NSUB - 3, NSUB):
                for e in range(NE):
                    add_pairs(p, p % 2, e, last=(p == NSUB - 1))

            pe.wait_ge(general_known, 1)
            general = pe.value_load(general_i[0:1, 0:1], min_val=0, max_val=1)
            with pe.If(general == 1):
                for h in range(2):
                    mm = nc.tensor.matmul(sum_bank[h], zero_f[:, 0:P], zero_f[:, 0:half], start=True, stop=False)
                mm.then_inc(g_used, NR)
                with pe.Fori(0, EC // GC) as it:
                    for col in range(GC):
                        pe.wait_ge(g_spread, GC * it + col + 1)
                        for h in range(2):
                            mm = nc.tensor.matmul(sum_bank[h], lo_hot[:, 0, col, :],
                                                  spread[:, col % NR, h * NT // 2:(h + 1) * NT // 2, :],
                                                  start=False, stop=False)
                        mm.then_inc(g_used, 1)
                for h in range(2):
                    mm = nc.tensor.matmul(sum_bank[h], zero_f[:, 0:P], zero_f[:, 0:half], start=False, stop=True)
                mm.then_inc(g_sums, 1)

            for e in range(NE + 1):
                if e < NE:
                    up(NSUB - 1, e)
                if e > 0:
                    down(NSUB - 1, e - 1)

            for g in range(NT // 4):
                pe.wait_ge(res_ready, g + 1)
                if g >= 2:
                    pe.wait_ge(res_copied, g - 1)
                if g < 2:
                    pe.wait_ge(down_done, NE * NSUB)
                pe.wait_ge(outputs_weighed, g + 1)
                pe.wait_ge(second_weighed, g + 1)
                for q in range(4):
                    t = 4 * g + q
                    parts = [x_tok[:, t, :], y_exp[:, t, 0, :], y_exp[:, t, 1, :]]
                    for n, part in enumerate(parts):
                        mm = nc.tensor.matmul(banks[4 + g % 2][:, q * P:(q + 1) * P], part, ident[:, :],
                                              is_transpose=True, start=(n == 0), stop=(n == len(parts) - 1))
                mm.then_inc(res_turned, 1)

        @block.scalar
        def _(ac):
            def root(v, n):
                ac.wait_ge(var_ready, n)
                nc.scalar.sqrt(v, v).then_inc(root_done, 1)

            def x_tokens(b):
                for g in range(2 * b, 2 * b + 2):
                    ac.wait_ge(x_turned, g + 1)
                    nc.scalar.copy(x_tok[:, 4 * g:4 * g + 4, :], banks[6 + g % 2][:, :]).then_inc(x_copied, 1)

            def std(b):
                root(rstd[:, b * TB:(b + 1) * TB], b + 1)

            def ring_fill(b):
                for h in range(2):
                    g = 2 * b + h
                    ac.wait_ge(n_turned, g + 1)
                    nc.scalar.copy(ringed[:, b, 1 + 16 * h:17 + 16 * h, 1:W + 1],
                                   banks[2 + g % 2][:, :].rearrange("p (y x) -> p y x", x=W)).then_inc(n_copied, 1)

            def columns(b, chunks):
                for j in chunks:
                    m = b * NCH + j
                    ac.wait_ge(cols_done, m + 1)
                    if m >= 2:
                        ac.wait_ge(off_done, m - 1)
                    for kj in range(3):
                        rows = slice(32 * kj, 32 * kj + 32)
                        ins = nc.scalar.copy(col_sums[rows, m % 2, :].rearrange("p (y x) -> p y x", x=W),
                                             banks[m % 2][rows, 0:OROWS * PW].rearrange("p (y x) -> p y x", x=PW)
                                             [:, :, kj:kj + W])
                    ins.then_inc(cols_copied, 1)

            def sigmoid(b):
                ac.wait_ge(off_read, b + 1)
                nc.scalar.activation(mask[:, b * TB:(b + 1) * TB, :], off_sb[:, b * TB:(b + 1) * TB, 2 * K:3 * K],
                                     ACT.Sigmoid).then_inc(mask_done, 1)

            x_tokens(0)
            x_tokens(1)
            std(0)
            x_tokens(2)
            x_tokens(3)
            ring_fill(0)
            std(1)
            columns(0, (0, 1))
            std(2)
            columns(0, (2, 3))
            ring_fill(1)
            columns(1, (0,))
            std(3)
            columns(1, (1, 2, 3))
            for b in range(2, B):
                sigmoid(b - 2)
                ring_fill(b)
                columns(b, range(NCH))
            sigmoid(B - 2)
            sigmoid(B - 1)

            def scale(it, u, g):
                ac.wait_ge(cells_in[3 * u + g], 48 * (it + 1))
                if g == 0:
                    ac.wait_ge(w_ready, 2 * it + u + 1)
                for k in range(3 * g, 3 * g + 3):
                    for c in range(4 if k == K - 1 else 3):
                        ins = nc.scalar.activation(cell[:, u, k, c, :], cell[:, u, k, c, :], ACT.Copy,
                                                   scale=w_slot[:, u, c, k:k + 1])
                ins.then_inc(scaled_a, 1)

            def evict(n, u, g):
                ac.wait_ge(turned, n + SLOTS)
                nc.scalar.copy(samp[:, u, 3 * g:3 * g + 3, :], banks[g][:, 0:3 * P]).then_inc(samp_ready, 1)

            with ac.Fori(0, NT // 2) as it:
                for u in range(2):
                    n = 6 * it + 3 * u
                    scale(it, u, 0)
                    evict(n, 1 - u, 2)
                    scale(it, u, 1)
                    evict(n + 1, u, 0)
                    scale(it, u, 2)
                    evict(n + 2, u, 1)
            evict(3 * NT, 1, 2)

            ac.wait_ge(cells_out[B - 1], 64)

            def token_std(b):
                root(rstd[:, b * TB:(b + 1) * TB], B + b + 1)

            def token_norm(b):
                ac.wait_ge(shift_ready, b + 1)
                for t in range(b * TB + 4, b * TB + 8):
                    ins = nc.scalar.activation(n_tok[:, t, :], x_tok[:, t, :], ACT.Identity,
                                               scale=rstd[:, t:t + 1], bias=shift[:, t:t + 1])
                ins.then_inc(t_normed_a, 1)

            def token_channels(g):
                ac.wait_ge(t_turned, g + 1)
                nc.scalar.copy(chan[:, g * 512:(g + 1) * 512], banks[g % 2][:, :]).then_inc(t_copied, 1)

            nc.scalar.sqrt(act_gate[:, 0:1], ident[:, 0:1]).then_inc(table_in, 1)
            token_std(0)
            token_norm(0)
            for b in range(B):
                token_channels(2 * b)
                if b < B - 1:
                    token_std(b + 1)
                    token_channels(2 * b + 1)
                    token_norm(b + 1)
                else:
                    token_channels(2 * b + 1)

            ac.wait_ge(off_read, B)
            ac.wait_ge(table_in, 1)
            nc.scalar.copy(act_gate[:, 0:1], ident[:, 0:1]).then_inc(hid_ready, HID_CREDIT)

            def hidden(s, e):
                for f in range(NF):
                    n = e * NF + f
                    ac.wait_ge(up_done, NE * NF * s + n + 1)
                    nc.scalar.activation(hid[:, (e % 2) * NF + f, :], banks[4 + n % 2][:, :], ACT.Gelu,
                                         bias=b1_sb[:, e, f:f + 1]).then_inc(hid_ready, 1)

            def pair_exp(s):
                ac.wait_ge(pair_lg, s + 1)
                nc.scalar.activation(ex[:, :, :], lg[:, 3, :, :], ACT.Exp).then_inc(pair_ex, 1)

            for e in range(NE):
                hidden(0, e)
            ac.wait_ge(dn_ready, 1)
            nc.scalar.activation(dn[:, 0:2, :, :], dn[:, 0:2, :, :], ACT.Exp).then_inc(dn_exp, 1)

            def pair_step(p, exp_after):
                for e in range(NE):
                    hidden(p + 2, e)
                    if e == exp_after:
                        pair_exp(p + 1)

            pair_step(-1, 2)
            with ac.Fori(0, NSUB // 2 - 2) as it:
                pair_step(2 * it, 1)
                pair_step(2 * it + 1, 1)
            pair_step(NSUB - 4, 1)
            pair_exp(NSUB - 2)
            pair_exp(NSUB - 1)
            ac.wait_ge(general_known, 1)
            general = ac.value_load(general_i[0:1, 0:1], min_val=0, max_val=1)
            with ac.If(general == 1):
                with ac.Fori(0, EC // GC) as it:
                    ac.wait_ge(g_lg, it + 1)
                    nc.scalar.activation(ex[:, 0:GC, :], lg[:, 3, 0:GC, :], ACT.Exp).then_inc(g_ex, 1)
            hidden(NSUB - 1, 0)
            root(cmp[:, 1, :], 2 * B + 1)
            hidden(NSUB - 1, 1)
            ac.wait_ge(sc_ready, 1)
            nc.scalar.activation(gate[:, :, :], gate[:, :, :], ACT.Exp).then_inc(sc_exp, 1)
            hidden(NSUB - 1, 2)
            hidden(NSUB - 1, 3)

            def weigh_outputs(g):
                if g == NT // 4 - 1:
                    ac.wait_ge(y_ready, NE * NSUB + 2)
                for t in range(4 * g, 4 * g + 4):
                    for e in ((0,) if t % 4 < 2 else (0, 1)):
                        ins = nc.scalar.activation(y_exp[:, t, e, :], y_exp[:, t, e, :], ACT.Copy, scale=gate[:, t, e:e + 1])
                ins.then_inc(outputs_weighed, 1)

            def evict_results(g):
                ac.wait_ge(res_turned, g + 1)
                nc.scalar.copy(chan[:, g * 512:(g + 1) * 512], banks[4 + g % 2][:, :]).then_inc(res_copied, 1)

            ac.wait_ge(gates_ready, 1)
            weigh_outputs(0)
            for g in range(NT // 4):
                if g + 1 < NT // 4:
                    weigh_outputs(g + 1)
                evict_results(g)

        @block.vector
        def _(ve):
            st = Steps(dve)
            V = nc.vector

            def done(ins):
                st.add(ins)
                ve.wait_ge(dve, st.now())

            roots = [0]

            def variance(i0, n, eps):
                s = stats[:, i0:i0 + n, :]
                a, d, v = (st_a[:, j, i0:i0 + n] for j in range(3))
                V.tensor_tensor(a, s[:, :, 1], s[:, :, 4], ALU.add)
                V.tensor_tensor(d, s[:, :, 1], s[:, :, 4], ALU.subtract)
                done(V.tensor_tensor(v, s[:, :, 2], s[:, :, 5], ALU.add))
                V.tensor_scalar(mean[:, i0:i0 + n], a, 0.5, None, ALU.mult)
                done(V.tensor_tensor(d, d, d, ALU.mult))
                done(V.scalar_tensor_tensor(out=v, in0=d, scalar=C / 4.0, in1=v, op0=ALU.mult, op1=ALU.add))
                V.tensor_scalar(rstd[:, i0:i0 + n], v, 1.0 / C, eps, ALU.mult, ALU.add).then_inc(var_ready, 1)
                roots[0] += 1

            def inverse(i0, n):
                ve.wait_ge(root_done, roots[0])
                done(V.reciprocal(rstd[:, i0:i0 + n], rstd[:, i0:i0 + n]))

            V.memset(offw_sb[:, :, NOFF:], 0.0).then_inc(pad_ready, 1)
            V.memset(zero_bf[:, :], 0.0)
            V.memset(zero_f[:, :], 0.0).then_inc(zeros_ready, 1)
            V.memset(lost[:, :], 0.0)
            V.memset(x_all[:, 0, :], 0.0)
            V.memset(pk_src[:, :], 0.0)
            V.memset(pk_dst[:, :], 0.0)
            V.memset(idx_f[:, NT:NT + 2, :], 0.0)
            V.memset(corner_w[:, NT:NT + 2, :, :], 0.0)
            done(V.memset(dve_gate[:, :], 0.0))

            ve.wait_ge(ident_ready, 1)
            done(V.tensor_tensor(add_taps, ident[:, 0:NOFF], ident[:, 32:32 + NOFF], ALU.add))
            V.tensor_tensor(add_taps, add_taps, ident[:, 64:64 + NOFF], ALU.add).then_inc(add_ready, 1)

            for b in range(B):
                for h in range(2):
                    ve.wait_ge(x_copied, 2 * b + h + 1)
                    for q in range(4):
                        t = b * TB + 4 * h + q
                        ins = V.bn_stats(stats[:, t, :], x_tok[:, t, :])
                done(ins)
                variance(b * TB, TB, EPS_C)
                inverse(b * TB, TB)
                for t in range(b * TB, (b + 1) * TB):
                    ins = V.tensor_scalar(n_tok[:, t, :], x_tok[:, t, :], mean[:, t:t + 1], rstd[:, t:t + 1],
                                          ALU.subtract, ALU.mult)
                ins.then_inc(normed, 1)

            ve.wait_ge(pool_step, POOL_CONST)
            V.tensor_copy(iota_f[:, :], iota_i[:, :])
            V.tensor_scalar(part_i[:, 1:2], part_i[:, 0:1], 5, None, ALU.arith_shift_right)
            done(V.tensor_scalar(part_i[:, 2:3], part_i[:, 0:1], W - 1, None, ALU.bitwise_and))
            done(V.tensor_copy(part_f[:, 1:3], part_i[:, 1:3]))

            def sampling(b):
                i = slice(b * TB, (b + 1) * TB)
                ve.wait_ge(off_done, NCH * (b + 1))
                o = banks[4 + b][:, 0:TB * 32].rearrange("p (t c) -> p t c", c=32)[:, :, 0:NOFF]
                st.add(V.tensor_tensor(off_sb[:, i, :], o, offb_sb[:, :].unsqueeze(1).to_broadcast([P, TB, NOFF]), ALU.add))
                V.tensor_scalar(py[:, i, :], by_i[:, i, :], part_f[:, 1:2], None, ALU.add)
                done(V.tensor_scalar(px[:, i, :], bx_i[:, i, :], part_f[:, 2:3], None, ALU.add))
                dyx = off_sb[:, i, 0:2 * K].rearrange("p t (k s) -> p t k s", s=2)
                V.tensor_tensor(py[:, i, :], py[:, i, :], dyx[:, :, :, 0], ALU.add).then_inc(off_read, 1)
                done(V.tensor_tensor(px[:, i, :], px[:, i, :], dyx[:, :, :, 1], ALU.add))
                for q, c in ((py, cy), (px, cx)):
                    ins = V.tensor_scalar(c[:, i, :], q[:, i, :], -0.5, 0.0, ALU.add, ALU.max)
                done(ins)
                V.tensor_scalar(cy_i[:, i, :], cy[:, i, :], float(H - 2), None, ALU.min)
                done(V.tensor_scalar(cx_i[:, i, :], cx[:, i, :], float(W - 2), None, ALU.min))
                V.tensor_copy(cy[:, i, :], cy_i[:, i, :])
                done(V.tensor_copy(cx[:, i, :], cx_i[:, i, :]))
                V.tensor_tensor(py[:, i, :], py[:, i, :], cy[:, i, :], ALU.subtract)
                V.tensor_tensor(px[:, i, :], px[:, i, :], cx[:, i, :], ALU.subtract)
                done(V.scalar_tensor_tensor(out=cy[:, i, :], in0=cy[:, i, :], scalar=float(W), in1=cx[:, i, :],
                                            op0=ALU.mult, op1=ALU.add))
                V.tensor_tensor(idx_f[:, i, :], cy[:, i, :], bt_i[:, i, :], ALU.add)
                for r, h0, h1 in ((py, hy0, hy1), (px, hx0, hx1)):
                    V.tensor_scalar(h0[:, i, :], r[:, i, :], -1.0, 1.0, ALU.mult, ALU.add)
                    ins = V.tensor_scalar(h1[:, i, :], r[:, i, :], -1.0, 2.0, ALU.mult, ALU.add)
                done(ins)
                for r, h0, h1 in ((py, hy0, hy1), (px, hx0, hx1)):
                    V.scalar_tensor_tensor(out=h0[:, i, :], in0=r[:, i, :], scalar=1.0, in1=h0[:, i, :],
                                           op0=ALU.add, op1=ALU.min)
                    ins = V.scalar_tensor_tensor(out=h1[:, i, :], in0=r[:, i, :], scalar=1.0, in1=h1[:, i, :],
                                                 op0=ALU.mult, op1=ALU.min)
                done(ins)
                ve.wait_ge(mask_done, b + 1)
                for h in (hx0, hx1):
                    V.tensor_scalar(h[:, i, :], h[:, i, :], 0.0, None, ALU.max)
                for h in (hy0, hy1):
                    ins = V.scalar_tensor_tensor(out=h[:, i, :], in0=h[:, i, :], scalar=0.0, in1=mask[:, i, :],
                                                 op0=ALU.max, op1=ALU.mult)
                done(ins)
                for c, (hy, hx) in enumerate(((hy0, hx0), (hy0, hx1), (hy1, hx0), (hy1, hx1))):
                    ins = V.tensor_tensor(corner_w[:, i, c, :], hy[:, i, :], hx[:, i, :], ALU.mult)
                done(ins)

            ve.wait_ge(w_in, 16 * len(PARAMS))
            done(V.tensor_scalar(small[:, 3:5, :], small[:, 3:5, :], 1.0 / HEADS, None, ALU.mult))
            done(V.tensor_reduce(beta_mean[:, :], small[:, 4, :].rearrange("p (h e) -> p e h", e=NE), AX.X, ALU.add))
            for n in range(2):
                done(V.tensor_tensor(att_products, wgat_sb[:, 0:HE], small[:, n, :], ALU.mult))
                done(V.tensor_reduce(wgat_sb[:, HE + n * HEADS:HE + (n + 1) * HEADS],
                                     att_products.rearrange("p (h e) -> p h e", e=NE), AX.X, ALU.add))
            V.tensor_copy(act_gate[:, 3:4], ident[:, 0:1]).then_inc(w_att_ready, 1)
            for b in range(B):
                sampling(b)
                if b == 0:
                    for u in range(2):
                        V.tensor_copy(w_slot[:, u, :, :], corner_w[:, u, :, :]).then_inc(w_ready, 1)
                        V.tensor_copy(idx_slot[:, u, :], idx_f[:, u, :]).then_inc(idx_ready, 3)

            idx_flat = idx_f[:, :, :].rearrange("p t k -> p (t k)")
            w_flat = corner_w[:, :, :, :].rearrange("p t c k -> p (t c k)")
            x_flat = x_all[:, :, :].rearrange("p t c -> p (t c)")
            ve.wait_ge(e_in, 32)
            loop_at = st.now()
            st.base, st.n = None, 0
            STEPS = LOOP_STEPS
            with ve.Fori(0, NT // 2) as it:
                st.base = it * STEPS + loop_at
                gates = [0]

                def step(ins):
                    st.add(ins)
                    ve.wait_ge(dve, st.now())

                def take_wait():
                    V.tensor_scalar(dve_gate[0:1, gates[0]:gates[0] + 1], iota_f[0:1, 0:1], 0.0, None, ALU.add)
                    gates[0] += 1

                def next_indices(u, k):
                    V.tensor_scalar(idx_slot[:, u, k:k + 3], idx_flat[:, bass.ds((2 * it + u + 2) * K + k, 3)],
                                    0.0, None, ALU.add).then_inc(idx_ready, 1)

                def corner_tap(u, k):
                    if k % 3 == 0:
                        ve.wait_ge(cells_in[3 * u + k // 3], 48 * (it + 1))
                    if k == K - 1:
                        return
                    ins = V.tensor_scalar(cell[:, u, k, 3, :], cell[:, u, k, 3, :], w_slot[:, u, 3, k:k + 1], None, ALU.mult)
                    if k % 3 == 2 or k == K - 2:
                        ins.then_inc(scaled_v, 1)

                def weights(u):
                    ve.wait_ge(scaled_a, 6 * it + 3 * u + 3)
                    ve.wait_ge(scaled_v, 6 * it + 3 * u + 3)
                    V.tensor_scalar(w_slot[:, u, :, :].rearrange("p c k -> p (c k)"),
                                    w_flat[:, bass.ds((2 * it + u + 2) * 4 * K, 4 * K)], 0.0, None, ALU.add)\
                        .then_inc(w_ready, 1)

                def residual(u):
                    ve.wait_ge(conv_done, 2 * it + u + 1)
                    xs = x_flat[:, bass.ds((2 * it + u) * C, C)]
                    st.add(V.tensor_tensor(xs, banks[4 - u][:, 0:C], xs, ALU.add))

                e_src = edge_f[:, bass.ds(it * SEG, SEG)]
                e_dst = edge_f[:, bass.ds(it * SEG + EC, SEG)]
                ka = keys[:, :]
                step(V.tensor_scalar(ka, e_src, float(M - 1), -float(M), ALU.min, ALU.mult))
                step(V.scalar_tensor_tensor(out=ka, in0=ka, scalar=float(M * (M - 1) + 1), in1=e_dst, op0=ALU.add, op1=ALU.add))
                step(V.scalar_tensor_tensor(out=ka, in0=e_dst, scalar=float(M), in1=ka, op0=ALU.is_lt, op1=ALU.mult))
                for rnd in range(CAP // 8 + 1):
                    top = kept[:, 8 * rnd:8 * rnd + 8]
                    take_wait()
                    st.add(V.max(top, ka))
                    corner_tap(0, rnd)
                    ve.wait_ge(dve, st.now())
                    if rnd < CAP // 8:
                        take_wait()
                        st.add(V.match_replace(ka, top, ka, 0.0))
                        if rnd % 3 == 0:
                            next_indices(0, rnd)
                        ve.wait_ge(dve, st.now())
                st.add(V.tensor_scalar(kept_i[:, 0, :], kept[:, 0:CAP], -1.0, None, ALU.add))
                V.tensor_tensor(lost[:, 0:1], lost[:, 0:1], kept[:, CAP:CAP + 1], ALU.max)
                V.scalar_tensor_tensor(out=lost[:, 1:2], in0=kept[:, PCAP:PCAP + 1], scalar=float(M) + 0.5,
                                       in1=lost[:, 1:2], op0=ALU.is_gt, op1=ALU.max)
                V.tensor_scalar(pairs1[:, bass.ds(it * PCAP, PCAP)], kept[:, 0:PCAP], 0.0, None, ALU.add)
                ve.wait_ge(dve, st.now())
                V.tensor_scalar(kept_i[:, 1, :], kept_i[:, 0, :], LO - 1, None, ALU.bitwise_and)
                st.add(V.tensor_scalar(kept_i[:, 2, :], kept_i[:, 0, :], 6, None, ALU.arith_shift_right))
                residual(0)
                ve.wait_ge(dve, st.now())
                st.add(V.tensor_copy(kept_lohi[:, :, :], kept_i[:, 1:3, :]))
                for k in range(3):
                    corner_tap(1, k)
                next_indices(1, 0)
                ve.wait_ge(dve, st.now())
                ve.wait_ge(hist_done, it + 1)
                for h in range(2):
                    ins = V.tensor_tensor(onehots[:, h, :, :], lanes[:, :, :],
                                          kept_lohi[:, h, :].unsqueeze(1).to_broadcast([P, LO, CAP]), ALU.is_equal)
                    if h == 0:
                        weights(0)
                    else:
                        ins.then_inc(hot_ready, 1)
                    for k in range(3 * h + 3, 3 * h + 6):
                        corner_tap(1, k)
                    next_indices(1, 3 * h + 3)
                residual(1)
                weights(1)
                assert st.n == STEPS, st.n
            st.base, st.n = loop_at + STEPS * (NT // 2), 0
            ve.wait_ge(conv_done, NT + 1)
            done(V.tensor_tensor(x_tok[:, NT - 1, :], banks[4][:, 0:C], x_tok[:, NT - 1, :], ALU.add))

            ve.wait_ge(hist_done, NT // 2 + 2)
            V.tensor_copy(hist_sb[:, :], banks[7][0:LO, 0:LO]).then_inc(hist_copied, 1)

            def token_variance(b):
                for t in range(b * TB, (b + 1) * TB):
                    ins = V.bn_stats(stats[:, t, :], x_tok[:, t, :])
                done(ins)
                variance(b * TB, TB, EPS_T)

            ve.wait_ge(cells_out[B - 1], 64)
            token_variance(0)
            for b in range(B):
                i = slice(b * TB, (b + 1) * TB)
                inverse(b * TB, TB)
                V.scalar_tensor_tensor(out=shift[:, i], in0=mean[:, i], scalar=-1.0, in1=rstd[:, i],
                                       op0=ALU.mult, op1=ALU.mult).then_inc(shift_ready, 1)
                for t in range(b * TB, b * TB + 4):
                    ins = V.tensor_scalar(n_tok[:, t, :], x_tok[:, t, :], mean[:, t:t + 1], rstd[:, t:t + 1],
                                          ALU.subtract, ALU.mult)
                ins.then_inc(t_normed, 1)
                if b < B - 1:
                    token_variance(b + 1)
                if b == 0:
                    V.memset(trow[:, :, :], 1.0)

            def token_rows(h):
                i = slice(h * NT // 2, (h + 1) * NT // 2)
                ve.wait_ge(proj_done, h + 1)
                pv = banks[2 + h][:, 0:NT // 2 * PROJ].rearrange("p (i f) -> p i f", f=PROJ)
                h_of = trow[:, i, HEADS:ROW].rearrange("p i (h f) -> p i h f", h=HEADS)[:, :, :, 1:]
                V.tensor_copy(h_of, pv[:, :, 0:HE].rearrange("p i (h e) -> p i h e", e=NE))
                V.tensor_copy(trow[:, i, 0:HEADS], pv[:, :, HE:HE + HEADS])
                st.add(V.tensor_copy(a_dst[:, i, :], pv[:, :, HE + HEADS:PROJ]))
                ve.wait_ge(dve, st.now())
                V.tensor_copy(act_gate[:, 1:2], ident[:, 0:1]).then_inc(rows_ready, 1)

            token_rows(0)

            def pick_pairs(tops, left, r0, n, last):
                for r in range(r0 // 8, (r0 + n) // 8):
                    top = tops[:, 8 * r:8 * r + 8]
                    done(V.max(top, left))
                    done(V.match_replace(left, top, left, 0.0))
                if last:
                    done(V.max(tops[:, r0 + n:r0 + n + 8], left))

            V.tensor_scalar(lost[:, 0:1], lost[:, 0:1], lost[:, 1:2], None, ALU.max)
            hits = keys[:, 0:NSEG * PCAP]
            done(V.tensor_scalar(hits, pairs1[:, :], float(M) + 0.5, None, ALU.is_gt))
            done(V.tensor_tensor(pairs1[:, :], pairs1[:, :], hits, ALU.mult))
            pick_pairs(pairs2, pairs1[:, :], 0, OWN, False)
            token_rows(1)
            V.tensor_reduce(amax_p[:, :], trow[:, :, 0:HEADS].rearrange("p i h -> p h i"), AX.X, ALU.max)\
                .then_inc(amax_ready, 1)

            def unpack(c0, c1):
                c = slice(c0, c1)
                V.tensor_scalar(pk_void[:, c], pairs2[:, c], 0.5, 64.0, ALU.is_lt, ALU.mult)
                done(V.tensor_scalar(pk_i[:, 0, c], pairs2[:, c], -1.0, None, ALU.add))
                V.tensor_scalar(pk_i[:, 1, c], pk_i[:, 0, c], 12, None, ALU.arith_shift_right)
                V.tensor_scalar(pk_i[:, 2, c], pk_i[:, 0, c], M - 1, None, ALU.bitwise_and)
                done(V.tensor_scalar(pk_i[:, 3, c], pk_i[:, 0, c], P - 1, None, ALU.bitwise_and))
                V.tensor_scalar(pk_src[:, c], pk_i[:, 1, c], -1.0, float(M - 1), ALU.mult, ALU.add)
                V.tensor_copy(pk_dst[:, c], pk_i[:, 2, c])
                V.tensor_copy(pk_lo[:, c], pk_i[:, 3, c])
                done(V.tensor_scalar(pk_i[:, 0, c], pk_i[:, 2, c], 7, None, ALU.arith_shift_right))
                V.tensor_scalar(pk_src[:, c], pk_src[:, c], float(M - 1), None, ALU.min)
                done(V.tensor_tensor(pk_hi[:, c], pk_i[:, 0, c], pk_void[:, c], ALU.add))

            unpack(0, OWN)
            for u in range(2):
                V.tensor_copy(src_idx[:, u, :], pk_src[:, u * SUB:(u + 1) * SUB])
                V.tensor_copy(dst_idx[:, u, :], pk_dst[:, u * SUB:(u + 1) * SUB]).then_inc(pair_idx_ready, 1)

            ve.wait_ge(last_done, 1)
            V.tensor_copy(count[:, :], banks[6][:, ROW:ROW + NT])
            done(V.tensor_copy(last_tok[:, :], banks[6][:, 0:ROW]))

            a_src = trow[:, :, 0:HEADS]
            ve.wait_ge(amax_done, 1)
            V.tensor_tensor(dn[:, 0, :, :], a_src, a_dst[:, :, :], ALU.add)
            V.tensor_tensor(dn[:, 1, :, :], a_dst[:, :, :], last_tok[:, 0:HEADS].unsqueeze(1).to_broadcast([P, NT, HEADS]), ALU.add)
            done(V.tensor_tensor(dn[:, 2, :, :], a_dst[:, :, :], amax[:, 0:HEADS].unsqueeze(1).to_broadcast([P, NT, HEADS]), ALU.add))
            done(V.scalar_tensor_tensor(out=dn[:, 0:3, :, :], in0=dn[:, 0:3, :, :], scalar=0.2, in1=dn[:, 0:3, :, :],
                                        op0=ALU.mult, op1=ALU.max))
            V.tensor_tensor(dn[:, 0, :, :], dn[:, 0, :, :], dn[:, 2, :, :], ALU.subtract)
            V.tensor_tensor(dn[:, 1, :, :], dn[:, 1, :, :], dn[:, 2, :, :], ALU.subtract).then_inc(dn_ready, 1)

            def one_hots(u, lo, hi, n):
                V.tensor_tensor(lo_hot[:, u, 0:n, :], iota_f[:, :].unsqueeze(1).to_broadcast([P, n, P]),
                                lo.unsqueeze(2).to_broadcast([P, n, P]), ALU.is_equal)
                V.tensor_tensor(hi_hot[:, u, 0:n, :], iota_f[:, 0:NT].unsqueeze(1).to_broadcast([P, n, NT]),
                                hi.unsqueeze(2).to_broadcast([P, n, NT]), ALU.is_equal)

            def exponents(step, sg, dg, n):
                V.tensor_tensor(lg[:, 0, 0:n, :], sg[:, :, 0:HEADS], dg, ALU.add)
                step(V.tensor_tensor(lg[:, 1, 0:n, :], dg, amax[:, 0:HEADS].unsqueeze(1).to_broadcast([P, n, HEADS]), ALU.add))
                step(V.scalar_tensor_tensor(out=lg[:, 0:2, 0:n, :], in0=lg[:, 0:2, 0:n, :], scalar=0.2,
                                            in1=lg[:, 0:2, 0:n, :], op0=ALU.mult, op1=ALU.max))
                return V.tensor_tensor(lg[:, 3, 0:n, :], lg[:, 0, 0:n, :], lg[:, 1, 0:n, :], ALU.subtract)

            def messages(u, sg, n):
                return V.tensor_tensor(val[:, u, 0:n, :].rearrange("p c (h f) -> p c h f", h=HEADS),
                                       sg[:, :, HEADS:ROW].rearrange("p c (h f) -> p c h f", h=HEADS),
                                       ex[:, 0:n, :].unsqueeze(3).to_broadcast([P, n, HEADS, NE + 1]), ALU.mult)

            def spread_column(u, col):
                return V.tensor_tensor(spread[:, (u * SUB + col) % NR, :, :],
                                       hi_hot[:, u, col, :].unsqueeze(2).to_broadcast([P, NT, VAL]),
                                       val[:, u, col, :].unsqueeze(1).to_broadcast([P, NT, VAL]), ALU.mult)

            V.tensor_copy(act_gate[:, 2:3], ident[:, 0:1]).then_inc(y_ready, 1)
            V.tensor_copy(act_gate[:, 3:4], ident[:, 0:1]).then_inc(y_ready, 1)

            def hots(s, u):
                one_hots(u, pk_lo[:, bass.ds(s * SUB, SUB)], pk_hi[:, bass.ds(s * SUB, SUB)], SUB)

            def logits(s, k, u):
                ve.wait_ge(pair_in[u], 32 * SUB * (k + 1))
                exponents(done, src_got[:, u, :, :], dst_got[:, u, :, :], SUB).then_inc(pair_lg, 1)

            def weighted(s, u):
                ve.wait_ge(pair_ex, s + 1)
                done(messages(u, src_got[:, u, :, :], SUB))
                for idx, pk in ((src_idx, pk_src), (dst_idx, pk_dst)):
                    ins = V.tensor_scalar(idx[:, u, :], pk[:, bass.ds((s + 2) * SUB, SUB)], 0.0, None, ALU.add)
                ins.then_inc(pair_idx_ready, 1)

            def spreads(s, u, e):
                for col in QUARTER[e]:
                    ve.wait_ge(spread_used, SUB * s + col + 1)
                    spread_column(u, col).then_inc(spread_ready, 1)

            def outputs(s, e):
                ve.wait_ge(down_done, NE * s + e + 1)
                V.tensor_tensor(y_exp[:, bass.ds(s * 4, 4), e, :],
                                banks[6 + e % 2][:, :].rearrange("p (q c) -> p q c", q=4),
                                b2_sb[:, e, :].unsqueeze(1).to_broadcast([P, 4, C]), ALU.add).then_inc(y_ready, 1)

            ve.wait_ge(t_turned, NT // 4)
            hots(0, 0)
            pick_pairs(pairs2, pairs1[:, :], OWN, PICKED - OWN, True)
            V.tensor_tensor(lost[:, 0:1], lost[:, 0:1], pairs2[:, PICKED:PICKED + 1], ALU.max).then_inc(picked, 1)
            outputs(0, 0)
            outputs(0, 1)
            ve.wait_ge(rest_in, 64)
            pick_pairs(rest_top, rest, 0, 24, False)
            outputs(0, 2)
            pick_pairs(rest_top, rest, 24, 24, False)
            outputs(0, 3)
            pick_pairs(rest_top, rest, 48, 24, False)
            outputs(1, 0)
            pick_pairs(rest_top, rest, 72, 24, True)
            done(V.tensor_tensor(lost[0:32, 0:1], lost[0:32, 0:1], rest_top[:, REST:REST + 1], ALU.max))
            V.tensor_copy(act_gate[:, 1:2], ident[:, 0:1]).then_inc(rest_picked, 1)
            V.tensor_scalar(lost[:, 0:1], lost[:, 0:1], 1.0 if general_always else 0.0, None, ALU.add)\
                .then_inc(lost_ready, 1)
            outputs(1, 1)
            logits(0, 0, 0)
            outputs(1, 2)
            weighted(0, 0)
            outputs(1, 3)

            def pair_step(p, k, u):
                for e in range(NE):
                    if e < NE - 1:
                        spreads(p, u, e + 1)
                    else:
                        spreads(p + 1, 1 - u, 0)
                    if e == 0:
                        ve.wait_ge(spread_used, SUB * p + NR)
                        hots(p + 1, 1 - u)
                    if e == 2:
                        weighted(p + 1, 1 - u)
                    outputs(p + 2, e)
                    if e == 0:
                        logits(p + 1, k, 1 - u)

            spreads(0, 0, 0)
            ve.wait_ge(rest_out, 64)
            unpack(OWN, PC)
            loop_at = st.now()
            with ve.Fori(0, NSUB // 2 - 2) as it:
                st.base, st.n = it * 2 * PAIR_STEPS + loop_at, 0
                pair_step(2 * it, it, 0)
                pair_step(2 * it + 1, it + 1, 1)
                assert st.n == 2 * PAIR_STEPS, st.n
            st.base, st.n = loop_at + 2 * PAIR_STEPS * (NSUB // 2 - 2), 0
            pair_step(NSUB - 4, NSUB // 2 - 2, 0)
            for p in (NSUB - 3, NSUB - 2):
                spreads(p, p % 2, 1)
                ve.wait_ge(spread_used, SUB * p + NR)
                hots(p + 1, (p + 1) % 2)
                logits(p + 1, (p + 1) // 2, (p + 1) % 2)
                for e in range(2, NE):
                    spreads(p, p % 2, e)
                weighted(p + 1, (p + 1) % 2)
                spreads(p + 1, (p + 1) % 2, 0)
            for e in range(1, NE):
                spreads(NSUB - 1, 1, e)
            ve.wait_ge(rows_out, 64)
            ve.wait_ge(dn_exp, 1)
            own, lastw = dn[:, 0, :, :], dn[:, 1, :, :]
            done(V.tensor_tensor(lastw, lastw, count[:, :].unsqueeze(2).to_broadcast([P, NT, HEADS]), ALU.mult))
            rows4 = trow[:, :, HEADS:ROW].rearrange("p i (h f) -> p i h f", h=HEADS)
            last4 = last_tok[:, HEADS:ROW].rearrange("p (h f) -> p h f", h=HEADS)
            F = NE + 1
            for h in range(HEADS):
                V.tensor_tensor(rows4[:, :, h, :], rows4[:, :, h, :], own[:, :, h].unsqueeze(2).to_broadcast([P, NT, F]), ALU.mult)
                ins = V.tensor_tensor(big[:, :, h, :], last4[:, h, :].unsqueeze(1).to_broadcast([P, NT, F]),
                                      lastw[:, :, h].unsqueeze(2).to_broadcast([P, NT, F]), ALU.mult)
            done(ins)
            done(V.tensor_tensor(big, big, rows4, ALU.add))

            ve.wait_ge(lost_done, 1)
            V.tensor_scalar(general_i[:, :], lost_all[:, :], 0.5, None, ALU.is_gt).then_inc(general_known, 1)
            ve.wait_ge(sums_done, 1)
            ve.wait_ge(general_known, 1)
            general = ve.value_load(general_i[0:1, 0:1], min_val=0, max_val=1)
            with ve.If(general == 1):
                V.tensor_copy(big, rows4)
                V.tensor_copy(act_gate[:, 1:2], ident[:, 0:1]).then_inc(g_free, 1)
                V.tensor_copy(act_gate[:, 2:3], ident[:, 0:1]).then_inc(g_step, 1)
                G_STEPS = 5
                with ve.Fori(0, EC // GC // 2) as it:
                    for u in range(2):
                        gs = Steps(g_step)
                        gs.base = (2 * it + u) * G_STEPS + 1

                        def step(ins):
                            gs.add(ins)
                            ve.wait_ge(g_step, gs.now())

                        ve.wait_ge(g_step, gs.now())
                        ve.wait_ge(g_edges_in, 64 * it + 32 * u + 32)
                        V.tensor_scalar(src_idx[:, 0, 0:GC], g_edge[:, 0, :], float(M - 1), None, ALU.min)
                        V.tensor_scalar(dst_idx[:, 0, 0:GC], g_edge[:, 1, :], float(M - 1), None, ALU.min).then_inc(g_idx, 1)
                        V.tensor_scalar(g_int[:, 0, :], g_edge[:, 1, :], P - 1, None, ALU.bitwise_and)
                        step(V.tensor_scalar(g_int[:, 1, :], g_edge[:, 1, :], 7, None, ALU.arith_shift_right))
                        step(V.tensor_copy(g_lohi[:, :, :], g_int[:, :, :]))
                        V.tensor_scalar(dve_gate[0:1, 0:1], iota_f[0:1, 0:1], 0.0, None, ALU.add).then_inc(g_free, 1)
                        ve.wait_ge(g_used, GC * (2 * it + u) + NR)
                        one_hots(0, g_lohi[:, 0, :], g_lohi[:, 1, :], GC)
                        for n in range(2):
                            ve.wait_ge(g_rows_in[u][n], 16 * GC * (it + 1))
                        exponents(step, src_got[:, 0, 0:GC, :], dst_got[:, 0, 0:GC, :], GC).then_inc(g_lg, 1)
                        ve.wait_ge(g_ex, 2 * it + u + 1)
                        step(messages(0, src_got[:, 0, 0:GC, :], GC))
                        for col in range(GC):
                            if col >= NR:
                                ve.wait_ge(g_used, GC * (2 * it + u) + col + 1)
                            spread_column(0, col).then_inc(g_spread, 1)
                        assert gs.n == G_STEPS, gs.n
                ve.wait_ge(g_sums, 1)

            half = NT // 2
            for h in range(2):
                i = slice(h * NT // 2, (h + 1) * NT // 2)
                ins = V.tensor_tensor(sums[:, i, :], banks[h][:, 0:half * VAL].rearrange("p (i v) -> p i v", v=VAL),
                                      bigf[:, h * half * VAL:(h + 1) * half * VAL].rearrange("p (i v) -> p i v", v=VAL), ALU.add)
            done(ins)
            sums4 = sums[:, :, :].rearrange("p i (h f) -> p i h f", h=HEADS)
            den = dn[:, 2, :, :]
            done(V.tensor_scalar(den, sums4[:, :, :, 0], 1e-16, None, ALU.add))
            done(V.reciprocal(den, den))
            t4 = tmp16[:, :, :].rearrange("p i (h e) -> p i h e", e=NE)
            done(V.tensor_tensor(t4, sums4[:, :, :, 1:], den.unsqueeze(3).to_broadcast([P, NT, HEADS, NE]), ALU.mult))

            def vec(n):
                return small[:, n, :].unsqueeze(1).to_broadcast([P, NT, HE])
            done(V.tensor_tensor(tmp16[:, :, :], tmp16[:, :, :], vec(2), ALU.add))
            mu, var = cmp[:, 0, :], cmp[:, 1, :]
            done(V.tensor_reduce(mu, tmp16[:, :, :], AX.X, ALU.add))
            done(V.scalar_tensor_tensor(out=tmp16[:, :, :], in0=mu.unsqueeze(2).to_broadcast([P, NT, HE]), scalar=-1.0 / HE,
                                        in1=tmp16[:, :, :], op0=ALU.mult, op1=ALU.add))
            sq = bigf[:, 0:NT * HE].rearrange("p (i f) -> p i f", f=HE)
            done(V.tensor_tensor(sq, tmp16[:, :, :], tmp16[:, :, :], ALU.mult))
            done(V.tensor_reduce(var, sq, AX.X, ALU.add))
            V.tensor_scalar(var, var, 1.0 / HE, EPS_T, ALU.mult, ALU.add).then_inc(var_ready, 1)
            outputs(NSUB - 1, 0)
            ve.wait_ge(root_done, 2 * B + 1)
            done(V.reciprocal(var, var))
            done(V.tensor_tensor(tmp16[:, :, :], tmp16[:, :, :], var.unsqueeze(2).to_broadcast([P, NT, HE]), ALU.mult))
            done(V.tensor_tensor(tmp16[:, :, :], tmp16[:, :, :], vec(3), ALU.mult))
            done(V.tensor_reduce(score[:, :, :], tmp16[:, :, :].rearrange("p i (h e) -> p i e h", e=NE), AX.X, ALU.add))
            done(V.tensor_tensor(score[:, :, :], score[:, :, :], beta_mean[:, :].unsqueeze(1).to_broadcast([P, NT, NE]),
                                 ALU.add))
            top = cmp[:, 2, :]
            V.memset(wins_flat, 0.0)
            done(V.tensor_reduce(top, score[:, :, :], AX.X, ALU.max))
            V.tensor_tensor(gate[:, :, :], score[:, :, :], top.unsqueeze(2).to_broadcast([P, NT, NE]), ALU.subtract)\
                .then_inc(sc_ready, 1)
            wins = wins_flat.rearrange("p (i a b) -> p i a b", a=NE, b=NE)
            for a in range(NE - 1):
                n = NE - 1 - a
                ins = V.tensor_tensor(wins[:, :, a, a + 1:], score[:, :, a].unsqueeze(2).to_broadcast([P, NT, n]),
                                      score[:, :, a + 1:], ALU.is_ge)
            done(ins)
            V.tensor_reduce(lost_to[:, 0, :, :], wins.rearrange("p i a b -> p i b a"), AX.X, ALU.add)
            done(V.tensor_reduce(lost_to[:, 1, :, :], wins, AX.X, ALU.add))
            beat = lost_to[:, 0, :, :]
            done(V.tensor_tensor(beat, beat, lost_to[:, 1, :, :], ALU.subtract))
            outputs(NSUB - 1, 1)
            ve.wait_ge(sc_exp, 1)
            for e in range(NE):
                ins = V.scalar_tensor_tensor(out=gate[:, :, e], in0=beat[:, :, e], scalar=1.5 - (NE - 1 - e),
                                             in1=gate[:, :, e], op0=ALU.is_lt, op1=ALU.mult)
            done(ins)
            done(V.tensor_reduce(cmp[:, 5, :], gate[:, :, :], AX.X, ALU.add))
            done(V.reciprocal(cmp[:, 5, :], cmp[:, 5, :]))
            done(V.tensor_tensor(gate[:, :, :], gate[:, :, :], cmp[:, 5, :].unsqueeze(2).to_broadcast([P, NT, NE]), ALU.mult))

            V.tensor_copy(act_gate[:, 2:3], ident[:, 0:1]).then_inc(gates_ready, 1)
            for g in range(NT // 4):
                if g == 2:
                    outputs(NSUB - 1, 2)
                    outputs(NSUB - 1, 3)
                for e in (3, 2):
                    for t in range(4 * g, 4 * g + 4):
                        ins = V.scalar_tensor_tensor(out=x_tok[:, t, :], in0=y_exp[:, t, e, :], scalar=gate[:, t, e:e + 1],
                                                     in1=x_tok[:, t, :], op0=ALU.mult, op1=ALU.add)
                    if e == 3:
                        done(ins)
                ins.then_inc(res_ready, 1)


_INS = ["x", "L0_conv_offset_w", "L0_conv_offset_b", "L0_conv_dcn_w", "L0_ffn_W_gat", "L0_ffn_att_src", "L0_ffn_att_dst",
        "L0_ffn_b_gat", "L0_ffn_ln_gamma", "L0_ffn_ln_beta", "L0_ffn_W1", "L0_ffn_b1", "L0_ffn_W2", "L0_ffn_b2",
        "L0_ffn_edge_index"]


def kernel(**inputs):
    import numpy as np
    import concourse.bacc as bacc
    from concourse import mybir as mb
    from concourse.bass_utils import run_bass_kernel_spmd as run

    nc = bacc.Bacc("TRN2", target_bir_lowering=False, num_devices=1)
    arrays, args = {}, []
    for name in _INS:
        a = np.asarray(inputs[name])
        if name == "L0_conv_offset_w" or name == "L0_conv_dcn_w":
            a = a.reshape(a.shape[0], a.shape[1], 9).transpose(1, 2, 0)
        if name == "L0_ffn_b1":
            a = a.reshape(a.shape[0], -1, 128).transpose(2, 0, 1)
        a = np.ascontiguousarray(a)
        arrays[f"in_{name}_dram"] = a
        args.append(nc.dram_tensor(f"in_{name}_dram", a.shape, mb.dt.from_np(a.dtype), kind="ExternalInput").ap())
    args.append(nc.dram_tensor("out_0_dram", inputs["x"].shape, mb.dt.float32, kind="ExternalOutput").ap())
    metaformer(nc, *args)
    r = run(nc, [arrays], core_ids=[0])
    return r.results[0]["out_0_dram"]
```
